# Optimizing a Trainium2 kernel written in Bass

```python
import numpy as np
import jax
import jax.numpy as jnp

def _softmax(x, axis=-1):
    return jax.nn.softmax(x, axis=axis)

def _gelu(x):
    return jax.nn.gelu(x, approximate=True)

def _silu(x):
    return jax.nn.silu(x)

def _sigmoid(x):
    return jax.nn.sigmoid(x)

def _layernorm(x, axis=-1, eps=1e-05):
    m = jnp.mean(x, axis=axis, keepdims=True)
    v = jnp.var(x, axis=axis, keepdims=True)
    return (x - m) / jnp.sqrt(v + eps)

def _scatter_add(tgt, idx, src, axis=0):
    return tgt.at[idx].add(src)

def _segment_sum(src, seg, n):
    return jax.ops.segment_sum(src, seg, n)
kernel_name = 'mk_perceiver_d2_seqx_r4_e82283'

def setup_inputs(seed: int=0):
    np.random.seed(seed)
    _w = jnp.asarray

    def _rec_inputs():
        import jax
        import jax.numpy as jnp
        _rk = jax.random.key(seed)
        x = -0.0005207 + 1.001 * jax.random.normal(jax.random.fold_in(_rk, 1), (8, 64, 256), jnp.float32)
        _lenS = 64 - jax.random.randint(jax.random.fold_in(_rk, 7), (8,), 0, max(1, 64 // 4) + 1, jnp.int32)
        _lenS2 = 1024 - jax.random.randint(jax.random.fold_in(_rk, 8), (8,), 0, max(1, 1024 // 4) + 1, jnp.int32)
        _ctx_1024P = jax.random.normal(jax.random.fold_in(_rk, 11), (8, 16, 256), jnp.float32)
        _ctx_1024c = jax.random.dirichlet(jax.random.fold_in(_rk, 511), 0.3 * jnp.ones((16,), jnp.float32), (8, 1024))
        _ctx_1024t = jnp.einsum('bsk,bkd->bsd', _ctx_1024c, _ctx_1024P)
        _ctx_1024t = _ctx_1024t * jax.lax.rsqrt(jnp.mean(jnp.square(_ctx_1024t)) + 1e-12) * 0.953939
        ctx_1024 = -1.52775e-05 + 0.999936 * (_ctx_1024t + 0.3 * jax.random.normal(jax.random.fold_in(_rk, 611), (8, 1024, 256), jnp.float32))
        return (x, ctx_1024)
    x, ctx_1024 = _rec_inputs()

    def _L0_xattn_setup():
        import jax, jax.numpy as jnp
        import numpy as np
        DIM = 256
        HEADS = 16
        DHEAD = 64
        INNER = HEADS * DHEAD
        EPS = 1e-05

        def layer_norm(x, g, b):
            mu = jnp.mean(x, axis=-1, keepdims=True)
            var = jnp.mean(jnp.square(x - mu), axis=-1, keepdims=True)
            return (x - mu) * jax.lax.rsqrt(var + EPS) * g + b

        def apply_rope(x, cos, sin):
            d2 = x.shape[-1] // 2
            x1, x2 = (x[..., :d2], x[..., d2:])
            return jnp.concatenate([x1 * cos - x2 * sin, x2 * cos + x1 * sin], axis=-1)
        key = jax.random.key(seed)
        ks = jax.random.split(key, 10)
        B, N, S = (8, 64, 1024)
        latents = jax.random.normal(ks[0], (B, N, DIM), dtype=jnp.float32)
        context = jax.random.normal(ks[1], (B, S, DIM), dtype=jnp.float32)
        cos = jax.random.uniform(ks[2], (S, DHEAD // 2), dtype=jnp.float32)
        sin = jax.random.uniform(ks[3], (S, DHEAD // 2), dtype=jnp.float32)
        init = lambda k, shp, fan_in: jax.random.normal(k, shp, dtype=jnp.float32) / np.sqrt(fan_in)
        return {'latents': latents, 'context': context, 'cos': cos, 'sin': sin, 'ln_lat_g': jnp.ones((DIM,), jnp.float32), 'ln_lat_b': jnp.zeros((DIM,), jnp.float32), 'ln_ctx_g': jnp.ones((DIM,), jnp.float32), 'ln_ctx_b': jnp.zeros((DIM,), jnp.float32), 'Wq': init(ks[4], (DIM, INNER), DIM), 'Wkv': init(ks[5], (DIM, 2 * INNER), DIM), 'Wo': init(ks[6], (INNER, DIM), INNER), 'bo': jnp.zeros((DIM,), jnp.float32)}
    _L0_xattn_all = _L0_xattn_setup()
    _L0_xattn_in = {k: v for k, v in _L0_xattn_all.items() if k in ('cos', 'sin', 'ln_lat_g', 'ln_lat_b', 'ln_ctx_g', 'ln_ctx_b', 'Wq', 'Wkv', 'Wo', 'bo')}
    del _L0_xattn_all

    def _L0_attn_setup():
        import jax, jax.numpy as jnp
        import numpy as np
        import math
        N_EMBD = 256
        N_HEAD = 16
        BLOCK_SIZE = 256
        B, T = (4, 256)
        key = jax.random.key(seed)
        ks = jax.random.split(key, 7)
        C = N_EMBD
        return {'x': jax.random.normal(ks[0], (B, T, C), dtype=jnp.float32), 'Wqk': jax.random.normal(ks[1], (C, 2 * C), dtype=jnp.float32) * 0.02, 'bqk': jnp.zeros((2 * C,), dtype=jnp.float32), 'Wgate': jax.random.normal(ks[2], (C, N_HEAD), dtype=jnp.float32) * 0.02, 'bgate': jnp.zeros((N_HEAD,), dtype=jnp.float32), 'Wproj': jax.random.normal(ks[3], (C, C), dtype=jnp.float32) * 0.02, 'bproj': jnp.zeros((C,), dtype=jnp.float32)}
    _L0_attn_all = _L0_attn_setup()
    _L0_attn_in = {k: v for k, v in _L0_attn_all.items() if k in ('Wqk', 'bqk', 'Wgate', 'bgate', 'Wproj', 'bproj')}
    del _L0_attn_all

    def _L0_ffn_setup():
        import jax, jax.numpy as jnp
        import numpy as np
        DIM = 256
        E = 8
        K = 2
        EPS = 1e-05

        def _ln(x, g, b):
            mu = jnp.mean(x, axis=-1, keepdims=True)
            var = jnp.mean(jnp.square(x - mu), axis=-1, keepdims=True)
            return (x - mu) * jax.lax.rsqrt(var + EPS) * g + b
        key = jax.random.key(seed)
        ks = jax.random.split(key, 8)
        H = 2 * DIM
        s_in = 1.0 / np.sqrt(DIM)
        s_h = 1.0 / np.sqrt(H)
        return {'x': jax.random.normal(ks[0], (2, 512, DIM), dtype=jnp.float32), 'gate_w': jax.random.uniform(ks[1], (DIM, E), minval=-s_in, maxval=s_in, dtype=jnp.float32), 'w1': jax.random.uniform(ks[2], (E, DIM, H), minval=-s_in, maxval=s_in, dtype=jnp.float32), 'b1': jax.random.uniform(ks[3], (E, H), minval=-s_in, maxval=s_in, dtype=jnp.float32), 'ln1_g': jnp.ones((E, H), dtype=jnp.float32), 'ln1_b': jnp.zeros((E, H), dtype=jnp.float32), 'w2': jax.random.uniform(ks[4], (E, H, DIM), minval=-s_h, maxval=s_h, dtype=jnp.float32), 'b2': jax.random.uniform(ks[5], (E, DIM), minval=-s_h, maxval=s_h, dtype=jnp.float32), 'ln_g': jnp.ones((DIM,), dtype=jnp.float32), 'ln_b': jnp.zeros((DIM,), dtype=jnp.float32)}
    _L0_ffn_all = _L0_ffn_setup()
    _L0_ffn_in = {k: v for k, v in _L0_ffn_all.items() if k in ('gate_w', 'w1', 'b1', 'ln1_g', 'ln1_b', 'w2', 'b2', 'ln_g', 'ln_b')}
    del _L0_ffn_all

    def _L1_xattn_setup():
        import jax, jax.numpy as jnp
        import numpy as np
        D_MODEL = 256
        H = 16
        D_K = D_MODEL // H
        key = jax.random.key(seed)
        ks = jax.random.split(key, 11)
        B, S = (2, 512)
        scale = 1.0 / np.sqrt(D_MODEL)
        inp = {'query': jax.random.normal(ks[0], (B, S, D_MODEL), jnp.float32), 'key': jax.random.normal(ks[1], (B, S, D_MODEL), jnp.float32), 'value': jax.random.normal(ks[2], (B, S, D_MODEL), jnp.float32), 'Wq': jax.random.normal(ks[3], (D_MODEL, D_MODEL), jnp.float32) * scale, 'bq': jnp.zeros((D_MODEL,), jnp.float32), 'Wk': jax.random.normal(ks[4], (D_MODEL, D_MODEL), jnp.float32) * scale, 'bk': jnp.zeros((D_MODEL,), jnp.float32), 'Wv': jax.random.normal(ks[5], (D_MODEL, D_MODEL), jnp.float32) * scale, 'bv': jnp.zeros((D_MODEL,), jnp.float32), 'Wo': jax.random.normal(ks[6], (D_MODEL, D_MODEL), jnp.float32) * scale, 'bo': jnp.zeros((D_MODEL,), jnp.float32)}
        return inp
    _L1_xattn_all = _L1_xattn_setup()
    _L1_xattn_in = {k: v for k, v in _L1_xattn_all.items() if k in ('Wq', 'bq', 'Wk', 'bk', 'Wv', 'bv', 'Wo', 'bo')}
    del _L1_xattn_all

    def _L1_attn_setup():
        import jax, jax.numpy as jnp
        import numpy as np
        L, B, D, FF = (1024, 4, 256, 1024)
        EPS = 1e-05

        def layer_norm(x, w, b):
            mu = jnp.mean(x, axis=-1, keepdims=True)
            var = jnp.var(x, axis=-1, keepdims=True)
            return (x - mu) * jax.lax.rsqrt(var + EPS) * w + b

        def spiral_conv(h, lmlg, theta, last_conv_init):
            seq_len = h.shape[0]
            gamma = jnp.exp(-jnp.exp(lmlg))
            c = gamma * jnp.exp(1j * theta.astype(jnp.complex64))
            n = jnp.arange(seq_len)[:, None]
            filt = jnp.power(c[None, :], n)
            filt_fft = jnp.fft.fft(filt, n=2 * seq_len, axis=0)
            x_fft = jnp.fft.fft(h.astype(jnp.complex64), n=2 * seq_len, axis=0)
            conv = jnp.fft.ifft(filt_fft[:, None, :] * x_fft, axis=0)[:seq_len]
            last_conv = jax.lax.stop_gradient(jnp.broadcast_to(last_conv_init[None, :], (h.shape[1], h.shape[2]))).astype(jnp.complex64)
            conv_with_past = conv + last_conv[None, :, :] * filt[:, None, :] * c[None, None, :]
            return conv_with_past.real * h
        key = jax.random.key(seed)
        ks = jax.random.split(key, 10)
        return {'x': jax.random.normal(ks[0], (L, B, D), dtype=jnp.float32), 'lmlg': jax.random.normal(ks[1], (D,), dtype=jnp.float32), 'theta': jax.random.normal(ks[2], (D,), dtype=jnp.float32), 'last_conv_init': jax.random.normal(ks[3], (D,), dtype=jnp.float32), 'ln_w': jax.random.normal(ks[4], (D,), dtype=jnp.float32) * 0.1 + 1.0, 'ln_b': jax.random.normal(ks[5], (D,), dtype=jnp.float32) * 0.1, 'w1': jax.random.normal(ks[6], (D, FF), dtype=jnp.float32) / np.sqrt(D), 'b1': jax.random.normal(ks[7], (FF,), dtype=jnp.float32) * 0.02, 'w2': jax.random.normal(ks[8], (FF, D), dtype=jnp.float32) / np.sqrt(FF), 'b2': jax.random.normal(ks[9], (D,), dtype=jnp.float32) * 0.02}
    _L1_attn_all = _L1_attn_setup()
    _L1_attn_in = {k: v for k, v in _L1_attn_all.items() if k in ('lmlg', 'theta', 'last_conv_init', 'ln_w', 'ln_b', 'w1', 'b1', 'w2', 'b2')}
    del _L1_attn_all

    def _L1_ffn_setup():
        import jax, jax.numpy as jnp
        import numpy as np
        B, S, D, E, H, DO = (4, 512, 256, 8, 1024, 256)
        TOP_K = 2
        LN_EPS = 1e-05
        key = jax.random.key(seed)
        ks = jax.random.split(key, 9)
        s = 0.02
        return {'x': jax.random.normal(ks[0], (B, S, D), dtype=jnp.float32), 'W1': jax.random.normal(ks[1], (E, D, H), dtype=jnp.float32) * s, 'b1': jnp.zeros((E, H), dtype=jnp.float32), 'W2': jax.random.normal(ks[2], (E, H, DO), dtype=jnp.float32) * s, 'b2': jnp.zeros((E, DO), dtype=jnp.float32), 'gate_W': jax.random.normal(ks[3], (D, E), dtype=jnp.float32) * s, 'shared_W': jax.random.normal(ks[4], (D, DO), dtype=jnp.float32) * s, 'shared_b': jnp.zeros((DO,), dtype=jnp.float32), 'gamma': jnp.ones((DO,), dtype=jnp.float32), 'beta': jnp.zeros((DO,), dtype=jnp.float32)}
    _L1_ffn_all = _L1_ffn_setup()
    _L1_ffn_in = {k: v for k, v in _L1_ffn_all.items() if k in ('W1', 'b1', 'W2', 'b2', 'gate_W', 'shared_W', 'shared_b', 'gamma', 'beta')}
    del _L1_ffn_all
    return {'x': x, 'ctx_1024': ctx_1024, 'L0_xattn_cos': _L0_xattn_in['cos'], 'L0_xattn_sin': _L0_xattn_in['sin'], 'L0_xattn_ln_lat_g': _L0_xattn_in['ln_lat_g'], 'L0_xattn_ln_lat_b': _L0_xattn_in['ln_lat_b'], 'L0_xattn_ln_ctx_g': _L0_xattn_in['ln_ctx_g'], 'L0_xattn_ln_ctx_b': _L0_xattn_in['ln_ctx_b'], 'L0_xattn_Wq': _L0_xattn_in['Wq'], 'L0_xattn_Wkv': _L0_xattn_in['Wkv'], 'L0_xattn_Wo': _L0_xattn_in['Wo'], 'L0_xattn_bo': _L0_xattn_in['bo'], 'L0_attn_Wqk': _L0_attn_in['Wqk'], 'L0_attn_bqk': _L0_attn_in['bqk'], 'L0_attn_Wgate': _L0_attn_in['Wgate'], 'L0_attn_bgate': _L0_attn_in['bgate'], 'L0_attn_Wproj': _L0_attn_in['Wproj'], 'L0_attn_bproj': _L0_attn_in['bproj'], 'L0_ffn_gate_w': _L0_ffn_in['gate_w'], 'L0_ffn_w1': _L0_ffn_in['w1'], 'L0_ffn_b1': _L0_ffn_in['b1'], 'L0_ffn_ln1_g': _L0_ffn_in['ln1_g'], 'L0_ffn_ln1_b': _L0_ffn_in['ln1_b'], 'L0_ffn_w2': _L0_ffn_in['w2'], 'L0_ffn_b2': _L0_ffn_in['b2'], 'L0_ffn_ln_g': _L0_ffn_in['ln_g'], 'L0_ffn_ln_b': _L0_ffn_in['ln_b'], 'L1_xattn_Wq': _L1_xattn_in['Wq'], 'L1_xattn_bq': _L1_xattn_in['bq'], 'L1_xattn_Wk': _L1_xattn_in['Wk'], 'L1_xattn_bk': _L1_xattn_in['bk'], 'L1_xattn_Wv': _L1_xattn_in['Wv'], 'L1_xattn_bv': _L1_xattn_in['bv'], 'L1_xattn_Wo': _L1_xattn_in['Wo'], 'L1_xattn_bo': _L1_xattn_in['bo'], 'L1_attn_lmlg': _L1_attn_in['lmlg'], 'L1_attn_theta': _L1_attn_in['theta'], 'L1_attn_last_conv_init': _L1_attn_in['last_conv_init'], 'L1_attn_ln_w': _L1_attn_in['ln_w'], 'L1_attn_ln_b': _L1_attn_in['ln_b'], 'L1_attn_w1': _L1_attn_in['w1'], 'L1_attn_b1': _L1_attn_in['b1'], 'L1_attn_w2': _L1_attn_in['w2'], 'L1_attn_b2': _L1_attn_in['b2'], 'L1_ffn_W1': _L1_ffn_in['W1'], 'L1_ffn_b1': _L1_ffn_in['b1'], 'L1_ffn_W2': _L1_ffn_in['W2'], 'L1_ffn_b2': _L1_ffn_in['b2'], 'L1_ffn_gate_W': _L1_ffn_in['gate_W'], 'L1_ffn_shared_W': _L1_ffn_in['shared_W'], 'L1_ffn_shared_b': _L1_ffn_in['shared_b'], 'L1_ffn_gamma': _L1_ffn_in['gamma'], 'L1_ffn_beta': _L1_ffn_in['beta']}

def reference(x, ctx_1024, L0_xattn_cos, L0_xattn_sin, L0_xattn_ln_lat_g, L0_xattn_ln_lat_b, L0_xattn_ln_ctx_g, L0_xattn_ln_ctx_b, L0_xattn_Wq, L0_xattn_Wkv, L0_xattn_Wo, L0_xattn_bo, L0_attn_Wqk, L0_attn_bqk, L0_attn_Wgate, L0_attn_bgate, L0_attn_Wproj, L0_attn_bproj, L0_ffn_gate_w, L0_ffn_w1, L0_ffn_b1, L0_ffn_ln1_g, L0_ffn_ln1_b, L0_ffn_w2, L0_ffn_b2, L0_ffn_ln_g, L0_ffn_ln_b, L1_xattn_Wq, L1_xattn_bq, L1_xattn_Wk, L1_xattn_bk, L1_xattn_Wv, L1_xattn_bv, L1_xattn_Wo, L1_xattn_bo, L1_attn_lmlg, L1_attn_theta, L1_attn_last_conv_init, L1_attn_ln_w, L1_attn_ln_b, L1_attn_w1, L1_attn_b1, L1_attn_w2, L1_attn_b2, L1_ffn_W1, L1_ffn_b1, L1_ffn_W2, L1_ffn_b2, L1_ffn_gate_W, L1_ffn_shared_W, L1_ffn_shared_b, L1_ffn_gamma, L1_ffn_beta):
    import jax
    import jax.numpy as jnp

    def _L0_xattn_ref(latents, context, cos, sin, ln_lat_g, ln_lat_b, ln_ctx_g, ln_ctx_b, Wq, Wkv, Wo, bo):
        import jax, jax.numpy as jnp
        import numpy as np
        DIM = 256
        HEADS = 16
        DHEAD = 64
        INNER = HEADS * DHEAD
        EPS = 1e-05

        def layer_norm(x, g, b):
            mu = jnp.mean(x, axis=-1, keepdims=True)
            var = jnp.mean(jnp.square(x - mu), axis=-1, keepdims=True)
            return (x - mu) * jax.lax.rsqrt(var + EPS) * g + b

        def apply_rope(x, cos, sin):
            d2 = x.shape[-1] // 2
            x1, x2 = (x[..., :d2], x[..., d2:])
            return jnp.concatenate([x1 * cos - x2 * sin, x2 * cos + x1 * sin], axis=-1)
        b, n, _ = latents.shape
        s = context.shape[1]
        lat = layer_norm(latents, ln_lat_g, ln_lat_b)
        ctx = layer_norm(context, ln_ctx_g, ln_ctx_b)
        q = (lat @ Wq).reshape(b, n, HEADS, DHEAD).transpose(0, 2, 1, 3)
        kv = ctx @ Wkv
        k, v = jnp.split(kv, 2, axis=-1)
        k = k.reshape(b, s, HEADS, DHEAD).transpose(0, 2, 1, 3)
        v = v.reshape(b, s, HEADS, DHEAD).transpose(0, 2, 1, 3)
        k = apply_rope(k, cos[None, None], sin[None, None])
        scale = DHEAD ** (-0.5)
        attn = jnp.einsum('bhnd,bhsd->bhns', q, k) * scale
        attn = jnp.clip(attn, -11.0, 11.0)
        attn = jax.nn.softmax(attn, axis=-1)
        out = jnp.einsum('bhns,bhsd->bhnd', attn, v)
        out = out.transpose(0, 2, 1, 3).reshape(b, n, INNER)
        return out @ Wo + bo

    def _L0_attn_ref(x, Wqk, bqk, Wgate, bgate, Wproj, bproj):
        import jax, jax.numpy as jnp
        import numpy as np
        import math
        N_EMBD = 256
        N_HEAD = 16
        BLOCK_SIZE = 256
        B, T = (4, 256)
        Bx, Tx, C = x.shape
        H = N_HEAD
        D = C // H
        windows = jnp.array([max(4, BLOCK_SIZE // 2 ** h) for h in range(H)], dtype=jnp.int32)
        qk = x @ Wqk + bqk
        q, k = jnp.split(qk, 2, axis=-1)
        v = k
        q = q.reshape(Bx, Tx, H, D).transpose(0, 2, 1, 3)
        k = k.reshape(Bx, Tx, H, D).transpose(0, 2, 1, 3)
        v = v.reshape(Bx, Tx, H, D).transpose(0, 2, 1, 3)
        i = jnp.arange(Tx)[:, None]
        j = jnp.arange(Tx)[None, :]
        mask = (j <= i)[None] & (j > i - windows[:, None, None])
        att = jnp.einsum('bhtd,bhsd->bhts', q, k) * (1.0 / math.sqrt(D))
        att = jnp.where(mask[None], att, -jnp.inf)
        att = jax.nn.softmax(att, axis=-1)
        out = jnp.einsum('bhts,bhsd->bhtd', att, v)
        combined = out.transpose(0, 2, 1, 3)
        gates = jax.nn.softmax(x @ Wgate + bgate, axis=-1)
        gated = (combined * gates[..., None]).reshape(Bx, Tx, C)
        return gated @ Wproj + bproj

    def _L0_ffn_ref(x, gate_w, w1, b1, ln1_g, ln1_b, w2, b2, ln_g, ln_b):
        import jax, jax.numpy as jnp
        import numpy as np
        DIM = 256
        E = 8
        K = 2
        EPS = 1e-05

        def _ln(x, g, b):
            mu = jnp.mean(x, axis=-1, keepdims=True)
            var = jnp.mean(jnp.square(x - mu), axis=-1, keepdims=True)
            return (x - mu) * jax.lax.rsqrt(var + EPS) * g + b
        shape = x.shape
        xf = x.reshape(-1, shape[-1])
        gates = jax.nn.softmax(xf @ gate_w, axis=-1)
        topw, topi = jax.lax.top_k(gates, K)
        topw = topw / jnp.sum(topw, axis=-1, keepdims=True)
        combine = jnp.sum(topw[:, :, None] * jax.nn.one_hot(topi, E, dtype=xf.dtype), axis=1)
        h = jnp.einsum('td,edh->teh', xf, w1) + b1
        h = _ln(h, ln1_g, ln1_b)
        h = jax.nn.gelu(h, approximate=False)
        y = jnp.einsum('teh,ehd->ted', h, w2) + b2
        out = jnp.einsum('ted,te->td', y, combine)
        out = _ln(out + xf, ln_g, ln_b)
        return out.reshape(shape)

    def _L1_xattn_ref(query, key, value, Wq, bq, Wk, bk, Wv, bv, Wo, bo):
        import jax, jax.numpy as jnp
        import numpy as np
        D_MODEL = 256
        H = 16
        D_K = D_MODEL // H
        B, Sq, _ = query.shape

        def proj(x, W, b):
            y = x @ W.T + b
            return y.reshape(B, -1, H, D_K).transpose(0, 2, 1, 3)
        q = proj(query, Wq, bq)
        k = proj(key, Wk, bk)
        v = proj(value, Wv, bv)
        scores = jnp.einsum('bhqd,bhkd->bhqk', q, k) / jnp.sqrt(jnp.float32(D_K))
        attn = jax.nn.softmax(scores, axis=-1)
        ctx = jnp.einsum('bhqk,bhkd->bhqd', attn, v)
        ctx = ctx.transpose(0, 2, 1, 3).reshape(B, Sq, D_MODEL)
        return ctx @ Wo.T + bo

    def _L1_attn_ref(x, lmlg, theta, last_conv_init, ln_w, ln_b, w1, b1, w2, b2):
        import jax, jax.numpy as jnp
        import numpy as np
        L, B, D, FF = (1024, 4, 256, 1024)
        EPS = 1e-05

        def layer_norm(x, w, b):
            mu = jnp.mean(x, axis=-1, keepdims=True)
            var = jnp.var(x, axis=-1, keepdims=True)
            return (x - mu) * jax.lax.rsqrt(var + EPS) * w + b

        def spiral_conv(h, lmlg, theta, last_conv_init):
            seq_len = h.shape[0]
            gamma = jnp.exp(-jnp.exp(lmlg))
            c = gamma * jnp.exp(1j * theta.astype(jnp.complex64))
            n = jnp.arange(seq_len)[:, None]
            filt = jnp.power(c[None, :], n)
            filt_fft = jnp.fft.fft(filt, n=2 * seq_len, axis=0)
            x_fft = jnp.fft.fft(h.astype(jnp.complex64), n=2 * seq_len, axis=0)
            conv = jnp.fft.ifft(filt_fft[:, None, :] * x_fft, axis=0)[:seq_len]
            last_conv = jax.lax.stop_gradient(jnp.broadcast_to(last_conv_init[None, :], (h.shape[1], h.shape[2]))).astype(jnp.complex64)
            conv_with_past = conv + last_conv[None, :, :] * filt[:, None, :] * c[None, None, :]
            return conv_with_past.real * h
        h = layer_norm(x, ln_w, ln_b)
        x = spiral_conv(h, lmlg, theta, last_conv_init) + x
        h = layer_norm(x, ln_w, ln_b)
        h = jax.nn.silu(h @ w1 + b1) @ w2 + b2
        return x + h

    def _L1_ffn_ref(x, W1, b1, W2, b2, gate_W, shared_W, shared_b, gamma, beta):
        import jax, jax.numpy as jnp
        import numpy as np
        B, S, D, E, H, DO = (4, 512, 256, 8, 1024, 256)
        TOP_K = 2
        LN_EPS = 1e-05
        d = x.shape[-1]
        flat = x.reshape(-1, d)
        n_exp = gate_W.shape[-1]
        probs = jax.nn.softmax(flat @ gate_W, axis=-1)
        topk_w, topk_idx = jax.lax.top_k(probs, TOP_K)
        topk_w = topk_w / topk_w.sum(axis=-1, keepdims=True)
        combine = (jax.nn.one_hot(topk_idx, n_exp, dtype=flat.dtype) * topk_w[..., None]).sum(axis=1)
        out = 0.5 * jax.nn.gelu(flat @ shared_W + shared_b, approximate=False)
        for e in range(n_exp):
            h = jax.nn.gelu(flat @ W1[e] + b1[e], approximate=False)
            out = out + combine[:, e:e + 1] * (h @ W2[e] + b2[e])
        mean = out.mean(axis=-1, keepdims=True)
        var = ((out - mean) ** 2).mean(axis=-1, keepdims=True)
        out = (out - mean) * jax.lax.rsqrt(var + LN_EPS) * gamma + beta
        return out.reshape(*x.shape[:-1], out.shape[-1])
    x = x + _L0_xattn_ref(_layernorm(x, axis=-1), ctx_1024, L0_xattn_cos, L0_xattn_sin, L0_xattn_ln_lat_g, L0_xattn_ln_lat_b, L0_xattn_ln_ctx_g, L0_xattn_ln_ctx_b, L0_xattn_Wq, L0_xattn_Wkv, L0_xattn_Wo, L0_xattn_bo)
    x = x + _L0_attn_ref(_layernorm(x, axis=-1), L0_attn_Wqk, L0_attn_bqk, L0_attn_Wgate, L0_attn_bgate, L0_attn_Wproj, L0_attn_bproj)
    x = x + _L0_ffn_ref(_layernorm(x, axis=-1), L0_ffn_gate_w, L0_ffn_w1, L0_ffn_b1, L0_ffn_ln1_g, L0_ffn_ln1_b, L0_ffn_w2, L0_ffn_b2, L0_ffn_ln_g, L0_ffn_ln_b)
    x = x + _L1_xattn_ref(_layernorm(x, axis=-1), ctx_1024, ctx_1024, L1_xattn_Wq, L1_xattn_bq, L1_xattn_Wk, L1_xattn_bk, L1_xattn_Wv, L1_xattn_bv, L1_xattn_Wo, L1_xattn_bo)
    x = x + _L1_attn_ref(_layernorm(x, axis=-1), L1_attn_lmlg, L1_attn_theta, L1_attn_last_conv_init, L1_attn_ln_w, L1_attn_ln_b, L1_attn_w1, L1_attn_b1, L1_attn_w2, L1_attn_b2)
    x = x + _L1_ffn_ref(_layernorm(x, axis=-1), L1_ffn_W1, L1_ffn_b1, L1_ffn_W2, L1_ffn_b2, L1_ffn_gate_W, L1_ffn_shared_W, L1_ffn_shared_b, L1_ffn_gamma, L1_ffn_beta)
    return x

_drawn_inputs = setup_inputs


def setup_inputs(seed=0):
    import zlib

    import numpy as np

    out = dict(_drawn_inputs(seed))
    spreads = {'L0_xattn_ln_lat_g': (1.0, 0.2),
     'L0_xattn_ln_lat_b': (0.0, 0.1),
     'L0_xattn_ln_ctx_g': (1.0, 0.2),
     'L0_xattn_ln_ctx_b': (0.0, 0.1),
     'L0_xattn_bo': (0.0, 0.1),
     'L0_attn_bqk': (0.0, 0.8),
     'L0_attn_bgate': (0.0, 0.8),
     'L0_attn_bproj': (0.0, 0.1),
     'L0_ffn_ln1_g': (1.0, 0.2),
     'L0_ffn_ln1_b': (0.0, 0.355),
     'L0_ffn_ln_g': (1.0, 0.2),
     'L0_ffn_ln_b': (0.0, 0.1),
     'L1_xattn_bq': (0.0, 0.322),
     'L1_xattn_bk': (0.0, 2.0),
     'L1_xattn_bv': (0.0, 0.1),
     'L1_xattn_bo': (0.0, 0.1),
     'L1_ffn_b1': (0.0, 0.1),
     'L1_ffn_b2': (0.0, 0.1),
     'L1_ffn_shared_b': (0.0, 0.1),
     'L1_ffn_gamma': (1.0, 0.2),
     'L1_ffn_beta': (0.0, 0.336)}
    factors = {'L0_attn_Wqk': 4.332,
     'L0_attn_Wgate': 5.729,
     'L0_attn_Wproj': 6.088,
     'L0_ffn_b1': 3.33,
     'L0_ffn_b2': 2.913,
     'L1_attn_b1': 12.406,
     'L1_attn_b2': 3.842}
    for name, (base, spread) in spreads.items():
        noise = np.random.default_rng([zlib.crc32(name.encode()), seed]).standard_normal(out[name].shape)
        drawn = base * np.exp(spread * noise) if base else spread * noise
        out[name] = jnp.asarray(drawn.astype(out[name].dtype))
    for name, factor in factors.items():
        out[name] = (out[name] * factor).astype(out[name].dtype)
    return out
```

```python
from contextlib import ExitStack

import numpy as np

import concourse.bass as bass
from concourse import mybir

P = 128
B, N, D, S, H = 8, 64, 256, 1024, 16
T = B * N
TT = T // P
KT = D // P
ST = S // P
EPS = 1e-5
DH = 64
NPAIR = H // 2
E = 8
H0 = 512
H1 = 1024
NEG = -1e30

F32 = mybir.dt.float32
F16 = mybir.dt.float16
F32R = mybir.dt.float32r
I32 = mybir.dt.int32
ALU = mybir.AluOpType
ACT = mybir.ActivationFunctionType
AX = mybir.AxisListType

COLS = {"L0_xattn_ln_lat_g": 2, "L0_xattn_ln_lat_b": 2, "L0_xattn_ln_ctx_g": 2, "L0_xattn_ln_ctx_b": 2,
        "L0_attn_bqk": 4, "L0_ffn_ln1_g": 32, "L0_ffn_ln1_b": 32, "L1_xattn_bq": 2, "L1_xattn_bk": 2,
        "L1_xattn_bv": 2, "L1_attn_lmlg": 2, "L1_attn_theta": 2, "L1_attn_last_conv_init": 2,
        "L1_attn_ln_w": 2, "L1_attn_ln_b": 2, "L1_attn_b1": 8, "L1_ffn_b1": 64}
ROWS = {"L0_xattn_bo": 256, "L0_attn_bqk": 512, "L0_attn_bgate": 16, "L0_attn_bproj": 256,
        "L0_ffn_ln_g": 256, "L0_ffn_ln_b": 256, "L1_xattn_bo": 256, "L1_attn_b2": 256,
        "L1_ffn_shared_b": 256, "L1_ffn_gamma": 256, "L1_ffn_beta": 256}


def offsets(widths):
    at, out = 0, {}
    for name, n in widths.items():
        out[name] = at
        at += n
    return out, at


COL_AT, NCOL = offsets(COLS)
ROW_AT, NROW = offsets(ROWS)


class Chain:

    def __init__(self, eng, sem):
        self.eng, self.sem, self.n, self.base = eng, sem, 0, 0

    def link(self, ins):
        self.n += 1
        ins.then_inc(self.sem, 1)
        self.eng.wait_ge(self.sem, self.base + self.n)

    def link_alone(self, ins, passed):
        self.n += 1
        ins.then_inc(self.sem, 1)
        wait_alone(self.eng, passed, self.sem, self.base + self.n)


def wait_alone(eng, passed, sem, value):
    eng.wait_ge(sem, value)
    eng.sem_inc(passed, 1)


def program(nc, A, phases=6):
    ctx = ExitStack()
    with ctx:
        def sb(name, shape, stack=ctx, dt=F32):
            return stack.enter_context(nc.sbuf_tensor(name, shape, dt))

        in_stage, finished = [], []

        def sem(name):
            in_stage.append(nc.alloc_semaphore(name))
            return in_stage[-1]

        x = sb("x", [P, TT, D])
        cols = sb("cols", [P, NCOL])
        rows = sb("rows", [P, NROW])
        ident = sb("ident", [P, P])
        head_mask = sb("head_mask", [P, 8])
        band = sb("band", [P, NPAIR, N])
        ps = ctx.enter_context(nc.psum_tensor("ps", [P, 8, 512], F32))

        def col(name, k=0):
            at = COL_AT[name] + k
            return cols[:, at:at + 1]

        def row(name, lo=0, n=None):
            at = ROW_AT[name] + lo
            return rows[:, at:at + (n or ROWS[name])]

        K = dict(nc=nc, A=A, sb=sb, sem=sem, x=x, cols=cols, rows=rows, ident=ident,
                 head_mask=head_mask, band=band, ps=ps, col=col, row=row, finished=finished)
        stages = (cross_attention_0, self_attention_0, experts_0, cross_attention_1, spiral_1, experts_1)
        for stage in stages[:phases]:
            with ExitStack() as own:
                stage(own, **K)
            for s in finished:
                nc.release_semaphore(s)
            finished[:], in_stage[:] = in_stage, []
        stored = sem("stored")
        with nc.Block() as block:
            @block.sync
            def _(sp):
                sp.dma_start(A["out"].rearrange("(t two) n d -> (two n) t d", two=2), x[:]).then_inc(stored, 16)
                sp.wait_ge(stored, 16)


def norm_stats(nc, step, src, stats, mv, var, tiles, ready):
    for t in range(tiles):
        last = nc.vector.bn_stats(stats[:, t, :], src[:, t, :])
    step.link(last)
    for t in range(tiles):
        last = nc.vector.bn_aggr(mv[:, t, :], stats[:, t, :])
    step.link(last)
    nc.vector.tensor_scalar(var[:, 0:tiles], mv[:, 0:tiles, 1], EPS, None, ALU.add).then_inc(ready, 1)


def split_matmul(nc, out, w, m, start, stop):
    nc.tensor.matmul(out, w[0], m[0], start=start, stop=False)
    nc.tensor.matmul(out, w[0], m[1], start=False, stop=False)
    return nc.tensor.matmul(out, w[1], m[0], start=False, stop=stop)


def norm_apply(nc, dst, src, mv, rstd, tiles):
    for t in range(tiles):
        last = nc.vector.tensor_scalar(dst[:, t, :], src[:, t, :], mv[:, t, 0:1], rstd[:, t:t + 1],
                                       ALU.subtract, ALU.mult)
    return last


def softmax_rows(nc, step, p, n, top):
    step.link(nc.vector.tensor_reduce(out=top, in_=p, axis=AX.X, op=ALU.max))
    return nc.vector.tensor_tensor(out=p, in0=p, in1=top.unsqueeze(2).to_broadcast(list(p.shape)), op=ALU.subtract)


def normalise_rows(nc, step, p, total):
    step.link(nc.vector.tensor_reduce(out=total, in_=p, axis=AX.X, op=ALU.add))
    step.link(nc.vector.reciprocal(total, total))
    return nc.vector.tensor_tensor(out=p, in0=p, in1=total.unsqueeze(2).to_broadcast(list(p.shape)), op=ALU.mult)


def top_two(nc, step, g, rank, picked, work, best):
    shape = list(g.shape)

    def wide(v):
        return v.unsqueeze(2).to_broadcast(shape)

    ranks = rank.unsqueeze(1).to_broadcast(shape)
    place = work[:, 0]
    taken = work[:, 1]
    rest = work[:, 2]
    top = best[:, 2]
    for n in range(2):
        src = g if n == 0 else rest
        step.link(nc.vector.tensor_reduce(out=best[:, n], in_=src, axis=AX.X, op=ALU.max))
        step.link(nc.vector.tensor_tensor(out=place, in0=src, in1=wide(best[:, n]), op=ALU.is_equal))
        step.link(nc.vector.tensor_tensor(out=place, in0=place, in1=ranks, op=ALU.mult))
        step.link(nc.vector.tensor_reduce(out=top, in_=place, axis=AX.X, op=ALU.max))
        mark = picked if n == 0 else taken
        step.link(nc.vector.tensor_tensor(out=mark, in0=place, in1=wide(top), op=ALU.is_equal))
        if n == 0:
            step.link(nc.vector.scalar_tensor_tensor(out=rest, in0=picked, scalar=-2.0, in1=g, op0=ALU.mult, op1=ALU.add))
    step.link(nc.vector.tensor_tensor(out=picked, in0=picked, in1=taken, op=ALU.add))
    step.link(nc.vector.tensor_tensor(out=picked, in0=picked, in1=g, op=ALU.mult))
    step.link(nc.vector.tensor_tensor(out=top, in0=best[:, 0], in1=best[:, 1], op=ALU.add))
    step.link(nc.vector.reciprocal(top, top))
    return nc.vector.tensor_tensor(out=picked, in0=picked, in1=wide(top), op=ALU.mult)


def cross_attention_0(own, nc, A, sb, sem, x, cols, rows, ident, head_mask, band, ps, col, row, finished):
    UNITS = 4
    GP = NPAIR // 2
    M = 8 * N
    wq = sb("wq", [P, KT, H * DH], own)
    wk = sb("wk", [P, KT, H * DH], own)
    wv = sb("wv", [P, KT, H * DH], own)
    wo = sb("wo", [P, NPAIR, D], own)
    cosT = sb("cosT", [P, S], own)
    sinT = sb("sinT", [P, S], own)
    z = [sb(f"z{i}", [P, ST, D], own) for i in range(2)]
    zT = [sb(f"zT{i}", [P, KT, S], own) for i in range(2)]
    q = sb("q", [P, NPAIR, B, 2, N], own)
    keys = [sb(f"keys{i}", [P, GP, S], own) for i in range(2)]
    kcos = [sb(f"kcos{i}", [P, 512], own) for i in range(2)]
    ksin = [sb(f"ksin{i}", [P, 512], own) for i in range(2)]
    NE = 4
    prob = [sb(f"prob{i}", [P, M], own) for i in range(NE)]
    psum_s = [sb(f"prob_sum{i}", [P, M], own) for i in range(2)]
    mix = sb("mix", [P, KT, H, 2, N], own)
    rden = sb("rden", [P, M], own)
    outT = sb("outT", [P, NPAIR, P], own)
    ones = sb("ones", [P, P], own)
    stats = sb("stats", [P, ST, 6], own)
    mv = sb("mv", [P, ST, 2], own)
    var = sb("var", [P, ST], own)
    rstd = sb("rstd", [P, ST], own)
    half = sb("half", [P, ST], own)
    lat = mix[:, 0].rearrange("p h a n -> p (h a n)")[:, 0:TT * D].rearrange("p (t d) -> p t d", t=TT)
    latT = mix[:, 1].rearrange("p h a n -> p (h a n)")[:, 0:KT * T].rearrange("p (k t) -> p k t", k=KT)

    keys_ps = [ps[:, 0, :], ps[:, 1, :]]
    score_ps = [ps[:, 2, :], ps[:, 3, :]]
    mix_ps = [ps[:, 4, :], ps[:, 5, :]]
    turn_ps = ps[:, 6, :]
    den_ps = ps[:, 7, :]

    x_loaded = sem("x_loaded"); cols_loaded = sem("cols_loaded"); rows_loaded = sem("rows_loaded")
    wq_loaded = sem("wq_loaded"); wk_loaded = sem("wk_loaded"); wvo_loaded = sem("wvo_loaded")
    rope_loaded = sem("rope_loaded"); ctx_loaded = sem("ctx_loaded")
    consts_made = sem("consts_made"); pool_step = sem("pool_step0"); dve_step = sem("dve_step0")
    pool_passed = sem("pool_passed0"); dve_passed = sem("dve_passed0")
    x_var = sem("x_var0"); x_rstd = sem("x_rstd0"); lat_ready = sem("lat_ready")
    lat_turned = sem("lat_turned"); latT_ready = sem("latT_ready"); q_done = sem("q_done")
    q_act = sem("q_act"); q_dve = sem("q_dve")
    ctx_var = sem("ctx_var"); ctx_rstd = sem("ctx_rstd"); z_ready = sem("z_ready")
    z_turned = sem("z_turned"); zT_ready = sem("zT_ready")
    key_mm = sem("key_mm"); key_read = sem("key_read"); key_ready = sem("key_ready")
    score_mm = sem("score_mm"); exp_done = sem("exp_done"); prob_ready = sem("prob_ready")
    mix_mm = sem("mix_mm"); sum_done = sem("sum_done"); mix_copied = sem("mix_copied")
    den_mm = sem("den_mm"); mix_ready = sem("mix_ready"); value_mm = sem("value_mm")
    outT_ready = sem("outT_ready"); out_mm = sem("out_mm"); x_added = sem("x_added0")

    RING = 2
    TILES = 2 * GP
    ctx_d = A["ctx_1024"].rearrange("b (t p) d -> b p t d", p=P)

    with nc.Block() as block:
        @block.sync
        def _(sp):
            sp.dma_start(x[:], A["x"].rearrange("(t two) n d -> (two n) t d", two=2)).then_inc(x_loaded, 16)
            sp.dma_start(cols[:], A["cols"]).then_inc(cols_loaded, 16)
            sp.dma_start(wq[:], A["wq_pairs"].rearrange("(k p) n -> p k n", p=P)).then_inc(wq_loaded, 16)
            sp.dma_start(z[0][:], ctx_d[0]).then_inc(ctx_loaded, 16)
            sp.dma_start(wk[:], A["wk_pairs"].rearrange("(k p) n -> p k n", p=P)).then_inc(wk_loaded, 16)
            sp.dma_start(cosT[:], A["cosT"]).then_inc(rope_loaded, 16)
            sp.dma_start(sinT[:], A["sinT"]).then_inc(rope_loaded, 16)
            sp.wait_ge(ctx_loaded, 16)
            sp.dma_start(z[1][:], ctx_d[1]).then_inc(ctx_loaded, 16)
            sp.dma_start(rows[:], A["rows"].to_broadcast([P, NROW])).then_inc(rows_loaded, 16)
            sp.dma_start(wv[:], A["wv"].rearrange("(k p) n -> p k n", p=P)).then_inc(wvo_loaded, 16)
            sp.dma_start(wo[:], A["L0_xattn_Wo"].rearrange("(k p) n -> p k n", p=P)).then_inc(wvo_loaded, 16)
            with sp.Fori(0, TT - 1) as i:
                for a in range(2):
                    sp.wait_ge(mix_mm, (2 * i + a + 1) * 2 * ST + NE)
                    sp.wait_ge(ctx_loaded, 16 * (2 * i + a + 2))
                    sp.dma_start(z[a][:], ctx_d[bass.ds(2 * i + a + 2, 1)].rearrange("b p t d -> (b p) t d")).then_inc(ctx_loaded, 16)

        @block.gpsimd
        def _(pool):
            step = Chain(pool, pool_step)
            step.link(nc.gpsimd.memset(ident[:], 0.0))
            step.link(nc.gpsimd.affine_select(out=ident[:], in_=ident[:], compare_op=ALU.not_equal, fill=1.0,
                                              base=0, pattern=[[-1, P]], channel_multiplier=1))
            step.link(nc.gpsimd.memset(half[:], -0.5))
            step.link(nc.gpsimd.memset(ones[:], 1.0))
            step.link(nc.gpsimd.memset(q[:], 0.0))
            pool.sem_inc(consts_made, 1)
            pool.sem_inc(key_ready, 2)
            pool.sem_inc(sum_done, NE)
            for n in range(2):
                pool.wait_ge(x_var, n + 1)
                nc.gpsimd.tensor_tensor(out=rstd[:, 0:TT], in0=var[:, 0:TT], in1=half[:, 0:TT], op=ALU.pow).then_inc(x_rstd, 1)

            def context_rstd(b):
                pool.wait_ge(ctx_var, b + 1)
                step.link(nc.gpsimd.tensor_tensor(out=rstd[:], in0=var[:], in1=half[:], op=ALU.pow))
                pool.sem_inc(ctx_rstd, 1)

            def turn_key(unit, t, parity):
                pool.wait_ge(key_read, unit * TILES + t + 1 + RING)
                nc.gpsimd.tensor_tensor(out=keys[parity][:, t % GP, (t // GP) * 512:(t // GP) * 512 + 512],
                                        in0=kcos[t % 2][:], in1=ksin[t % 2][:], op=ALU.add).then_inc(key_ready, 1)

            pool.wait_ge(x_rstd, 2)
            context_rstd(0)
            for t in range(TILES):
                turn_key(0, t, 0)
            step.link(nc.gpsimd.memset(head_mask[:], 1.0))
            for sign, base in ((1, 0), (-1, 15)):
                step.link(nc.gpsimd.affine_select(out=head_mask[:], in_=head_mask[:], compare_op=ALU.is_ge, fill=0.0,
                                                  base=base, pattern=[[-16 * sign, 8]], channel_multiplier=sign))
            step.link(nc.gpsimd.memset(band[:], 0.0))
            for hh in range(2):
                part = band[64 * hh:64 * hh + 64]
                step.link(nc.gpsimd.affine_select(out=part, in_=part, compare_op=ALU.is_ge, fill=NEG, base=0,
                                                  pattern=[[0, NPAIR], [-1, N]], channel_multiplier=1))
                for pair in range(NPAIR):
                    window = max(4, 256 >> (2 * pair + hh))
                    if window < N:
                        part = band[64 * hh:64 * hh + 64, pair]
                        step.link(nc.gpsimd.affine_select(out=part, in_=part, compare_op=ALU.is_ge, fill=NEG,
                                                          base=window - 1, pattern=[[1, N]], channel_multiplier=-1))

            first = step.n

            def turn(i, last):
                step.base, step.n = i * LINKS if last else i * LINKS, first
                for u in range(UNITS):
                    unit = i * UNITS + u
                    if not (last and u == UNITS - 1):
                        pool.wait_ge(score_mm, unit * ST)
                    for t in range(ST):
                        if t == 0:
                            wait_alone(pool, pool_passed, prob_ready, unit * ST + t + 1)
                        else:
                            pool.wait_ge(prob_ready, unit * ST + t + 1)
                        total, e = psum_s[u % 2], prob[t % NE]
                        if t == 0:
                            nc.gpsimd.tensor_copy(total[:], e[:]).then_inc(sum_done, 1)
                        else:
                            pool.wait_ge(sum_done, unit * ST + t + NE)
                            nc.gpsimd.tensor_tensor(out=total[:], in0=total[:], in1=e[:], op=ALU.add).then_inc(sum_done, 1)
                        if u % 2 == 0 and t == 3 and not (last and u == 2):
                            context_rstd(2 * i + u // 2 + 1)
                        if not (last and u == UNITS - 1):
                            turn_key(unit + 1, t, (u + 1) % 2)

            LINKS = 2
            with pool.Fori(0, TT - 1) as i:
                turn(i, False)
            turn(TT - 1, True)

        @block.scalar
        def _(act):
            act.sem_inc(exp_done, 2)
            act.wait_ge(cols_loaded, 16)
            for k in range(KT):
                act.wait_ge(lat_turned, k + 1)
                nc.scalar.activation(latT[:, k, :], keys_ps[k], ACT.Identity, bias=col("L0_xattn_ln_lat_b", k),
                                     scale=col("L0_xattn_ln_lat_g", k)).then_inc(latT_ready, 1)
            act.wait_ge(consts_made, 1)
            for pair in range(NPAIR):
                act.wait_ge(q_done, pair + 1)
                src = ps[:, 2 + pair % 4, :]
                for hh in range(2):
                    r = 32 * hh
                    last = nc.scalar.copy(q[r:r + 32, pair, :, hh, :], src[r:r + 32].rearrange("p (b n) -> p b n", b=B))
                last.then_inc(q_act, 1)

            def normed_context(b, a, g):
                act.wait_ge(z_turned, 4 * b + g + 1)
                k, h = g % 2, g // 2
                nc.scalar.activation(zT[a][:, k, h * 512:h * 512 + 512], turn_ps, ACT.Identity,
                                     bias=col("L0_xattn_ln_ctx_b", k), scale=col("L0_xattn_ln_ctx_g", k)).then_inc(zT_ready, 1)

            for g in range(4):
                normed_context(0, 0, g)

            def turn(i, last):
                for u in range(UNITS):
                    unit = i * UNITS + u
                    for t in range(ST):
                        tile = unit * ST + t
                        act.wait_ge(score_mm, tile + 1)
                        act.wait_ge(mix_mm, tile + 1)
                        act.wait_ge(sum_done, tile + 1)
                        nc.scalar.activation(prob[t % NE][:], score_ps[t % 2], ACT.Exp, scale=DH ** -0.5).then_inc(exp_done, 1)
                        if u % 2 == 0 and t >= 5 and not (last and u == 2):
                            if t == 5:
                                act.wait_ge(key_mm, (2 * i + u // 2) * 2 * TILES)
                            normed_context(2 * i + u // 2 + 1, (u // 2 + 1) % 2, t - 5)
                    if u % 2 == 0 and not (last and u == 2):
                        normed_context(2 * i + u // 2 + 1, (u // 2 + 1) % 2, 3)
                    act.wait_ge(mix_mm, (unit + 1) * ST + NE)
                    if u == 0:
                        act.wait_ge(value_mm, i)
                    for k in range(KT):
                        nc.scalar.copy(mix[:, k, 8 * (u % 2):8 * (u % 2) + 8, u // 2, :],
                                       mix_ps[k].rearrange("p (h n) -> p h n", h=8)).then_inc(mix_copied, 1)
                act.wait_ge(value_mm, i + 1)
                for n in range(2):
                    nc.scalar.copy(outT[:, 4 * n:4 * n + 4, :], score_ps[n].rearrange("p (a t) -> p a t", a=4)).then_inc(outT_ready, 1)

            with act.Fori(0, TT - 1) as i:
                turn(i, False)
            turn(TT - 1, True)

        @block.vector
        def _(dve):
            step = Chain(dve, dve_step)
            dve.sem_inc(key_read, RING)

            def norm_latents(n, src):
                for t in range(TT):
                    last = nc.vector.bn_stats(stats[:, t, :], src[:, t, :])
                step.link(last)
                for t in range(TT):
                    last = nc.vector.bn_aggr(mv[:, t, :], stats[:, t, :])
                step.link(last)
                nc.vector.tensor_scalar(var[:, 0:TT], mv[:, 0:TT, 1], EPS, None, ALU.add).then_inc(x_var, 1)
                dve.wait_ge(x_rstd, n + 1)
                for t in range(TT):
                    last = nc.vector.tensor_scalar(lat[:, t, :], src[:, t, :], mv[:, t, 0:1], rstd[:, t:t + 1],
                                                   ALU.subtract, ALU.mult)
                return last

            dve.wait_ge(x_loaded, 16)
            step.link(norm_latents(0, x))
            norm_latents(1, lat).then_inc(lat_ready, 1)

            def context_stats(b, a, lo, hi):
                if lo == 0:
                    dve.wait_ge(ctx_loaded, 16 * (b + 1))
                for t in range(lo, hi):
                    last = nc.vector.bn_stats(stats[:, t, :], z[a][:, t, :])
                if hi == ST:
                    step.link_alone(last, dve_passed)
                    for t in range(ST):
                        last = nc.vector.bn_aggr(mv[:, t, :], stats[:, t, :])
                    step.link(last)
                    nc.vector.tensor_scalar(var[:], mv[:, :, 1], EPS, None, ALU.add).then_inc(ctx_var, 1)

            def context_norm(b, a, lo, hi):
                dve.wait_ge(ctx_rstd, b + 1)
                for t in range(lo, hi):
                    last = nc.vector.tensor_scalar(z[a][:, t, :], z[a][:, t, :], mv[:, t, 0:1], rstd[:, t:t + 1],
                                                   ALU.subtract, ALU.mult)
                last.then_inc(z_ready, 1)

            dve.wait_ge(lat_ready, 1)
            context_stats(0, 0, 0, ST)
            context_norm(0, 0, 0, ST // 2)
            context_norm(0, 0, ST // 2, ST)
            dve.wait_ge(consts_made, 1)
            for pair in range(NPAIR):
                dve.wait_ge(q_done, pair + 1)
                src = ps[:, 2 + pair % 4, :]
                for hh in range(2):
                    r = 64 + 32 * hh
                    last = nc.vector.tensor_copy(q[r:r + 32, pair, :, hh, :], src[r:r + 32].rearrange("p (b n) -> p b n", b=B))
                last.then_inc(q_dve, 1)
            dve.wait_ge(rope_loaded, 32)
            dve.wait_ge(cols_loaded, 16)

            def key_products(unit, t):
                tile = unit * TILES + t
                dve.wait_ge(key_mm, tile + 1)
                dve.wait_ge(key_ready, tile + 1)
                src, at = keys_ps[t % 2], slice((t // GP) * 512, (t // GP) * 512 + 512)
                nc.vector.tensor_tensor(out=kcos[t % 2][:], in0=src, in1=cosT[:, at], op=ALU.mult)
                nc.vector.scalar_tensor_tensor(out=ksin[t % 2][0:64], in0=src[64:128], scalar=-1.0, in1=sinT[0:64, at],
                                               op0=ALU.mult, op1=ALU.mult)
                nc.vector.tensor_tensor(out=ksin[t % 2][64:128], in0=src[0:64], in1=sinT[64:128, at],
                                        op=ALU.mult).then_inc(key_read, 1)

            for t in range(TILES):
                key_products(0, t)
            first = step.n

            def turn(i, last):
                step.base, step.n = i * LINKS, first
                for u in range(UNITS):
                    unit = i * UNITS + u
                    for t in range(ST):
                        dve.wait_ge(exp_done, unit * ST + t + 1 + RING)
                        nc.vector.tensor_scalar(prob[t % NE][:], prob[t % NE][:], float(np.exp(np.float32(11))),
                                                float(np.exp(np.float32(-11))), ALU.min, ALU.max).then_inc(prob_ready, 1)
                        if not (last and u == UNITS - 1):
                            key_products(unit + 1, t)
                        if u % 2 == 0 and not (last and u == 2):
                            b, a = 2 * i + u // 2 + 1, (u // 2 + 1) % 2
                            if t == 2:
                                context_stats(b, a, 0, ST // 2)
                            if t == 3:
                                context_stats(b, a, ST // 2, ST)
                            if t == 4:
                                context_norm(b, a, 0, ST // 2)
                            if t == 5:
                                context_norm(b, a, ST // 2, ST)
                        if t == 3 and u > 0:
                            finish_mix(i, u - 1)
                finish_mix(i, UNITS - 1)
                dve.wait_ge(out_mm, i + 1)
                xt = x[:].rearrange("p t d -> p (t d)")[:, bass.ds(i * D, D)]
                step.link(nc.vector.tensor_tensor(out=xt, in0=den_ps[:, 0:D], in1=xt, op=ALU.add))
                nc.vector.tensor_tensor(out=xt, in0=xt, in1=row("L0_xattn_bo"), op=ALU.add).then_inc(x_added, 1)

            def finish_mix(i, u):
                dve.wait_ge(den_mm, i * UNITS + u + 1)
                step.link(nc.vector.reciprocal(rden[:], den_ps))
                dve.wait_ge(mix_copied, KT * (i * UNITS + u + 1))
                for k in range(KT):
                    part = mix[:, k, 8 * (u % 2):8 * (u % 2) + 8, u // 2, :]
                    step.link(nc.vector.scalar_tensor_tensor(out=part, in0=part, scalar=col("L0_xattn_ln_ctx_g", k),
                                                             in1=rden[:].rearrange("p (h n) -> p h n", h=8),
                                                             op0=ALU.mult, op1=ALU.mult))
                    last = nc.vector.tensor_scalar(part, part, col("L0_xattn_ln_ctx_b", k), None, ALU.add)
                last.then_inc(mix_ready, 1)

            LINKS = UNITS * 3 + 2 * 2 + 1
            dve.wait_ge(rows_loaded, 16)
            with dve.Fori(0, TT - 1) as i:
                turn(i, False)
            assert step.n == first + LINKS
            turn(TT - 1, True)

        @block.tensor
        def _(pe):
            pe.sem_inc(mix_mm, NE)
            pe.wait_ge(consts_made, 1)
            pe.wait_ge(lat_ready, 1)
            for k in range(KT):
                for t in range(TT):
                    last = nc.tensor.transpose(keys_ps[k][:, t * P:(t + 1) * P], lat[:, t, k * P:(k + 1) * P], ident[:])
                last.then_inc(lat_turned, 1)
            pe.wait_ge(latT_ready, KT)
            pe.wait_ge(wq_loaded, 16)
            for pair in range(NPAIR):
                if pair >= 4:
                    pe.wait_ge(q_act, pair - 3)
                    pe.wait_ge(q_dve, pair - 3)
                for k in range(KT):
                    last = nc.tensor.matmul(ps[:, 2 + pair % 4, :], wq[:, k, pair * P:(pair + 1) * P], latT[:, k, :],
                                            start=k == 0, stop=k == KT - 1)
                last.then_inc(q_done, 1)

            def turn_context(b, a, g):
                pe.wait_ge(z_ready, 2 * b + 1 + g // 2)
                pe.wait_ge(zT_ready, 4 * b + g)
                for t in range(4):
                    last = nc.tensor.transpose(turn_ps[:, t * P:(t + 1) * P],
                                               z[a][:, 4 * (g // 2) + t, (g % 2) * P:(g % 2 + 1) * P], ident[:])
                last.then_inc(z_turned, 1)

            def project_key(unit, b, a, g, t):
                pair, h = g * GP + t % GP, t // GP
                pe.wait_ge(zT_ready, 4 * b + 2 + 2 * h)
                pe.wait_ge(key_read, unit * TILES + t + 1)
                for k in range(KT):
                    last = nc.tensor.matmul(keys_ps[t % 2], wk[:, k, pair * P:(pair + 1) * P],
                                            zT[a][:, k, h * 512:h * 512 + 512], start=k == 0, stop=k == KT - 1)
                last.then_inc(key_mm, 1)

            for g in range(4):
                turn_context(0, 0, g)
            pe.wait_ge(wk_loaded, 16)
            for t in range(TILES):
                project_key(0, 0, 0, 0, t)
            pe.wait_ge(q_act, NPAIR)
            pe.wait_ge(q_dve, NPAIR)
            pe.wait_ge(wvo_loaded, 32)
            qf = q[:].rearrange("p a b h n -> p (a b h n)")

            def weigh(unit, u, t):
                pe.wait_ge(prob_ready, unit * ST + t + 1)
                if t == 0:
                    pe.wait_ge(mix_copied, KT * unit)
                for k in range(KT):
                    last = nc.tensor.matmul(mix_ps[k], z[u // 2][:, t, k * P:(k + 1) * P], prob[t % NE][:],
                                            start=t == 0, stop=t == ST - 1)
                last.then_inc(mix_mm, 1)

            def denominators(i, u):
                pe.wait_ge(sum_done, (i * UNITS + u + 1) * ST + NE)
                if u > 0:
                    pe.wait_ge(mix_ready, i * UNITS + u)
                nc.tensor.matmul(den_ps, ones[:], psum_s[u % 2][:], start=True, stop=True).then_inc(den_mm, 1)

            def project_values(i, n):
                for pair in range(4 * n, 4 * n + 4):
                    for k in range(KT):
                        for hh in range(2):
                            head = 2 * pair + hh
                            last = nc.tensor.matmul(score_ps[n][64 * hh:64 * hh + 64, (pair % 4) * P:(pair % 4 + 1) * P],
                                                    wv[:, k, head * DH:(head + 1) * DH],
                                                    mix[:, k, head].rearrange("p a n -> p (a n)"),
                                                    start=k == 0, stop=k == KT - 1)
                return last

            def turn(i, last):
                for u in range(UNITS):
                    unit = i * UNITS + u
                    for t in range(ST):
                        tile = unit * ST + t
                        if t == 0:
                            pe.wait_ge(key_ready, (unit + 1) * TILES + RING)
                        pe.wait_ge(exp_done, tile + 1)
                        for j in range(GP):
                            pair = (u % 2) * GP + j
                            mm = nc.tensor.matmul(score_ps[t % 2][:, j * P:(j + 1) * P],
                                                  keys[u % 2][:, j, t * P:(t + 1) * P],
                                                  qf[:, bass.ds((2 * i + u // 2) * P + pair * B * P, P)], start=True, stop=True)
                        mm.then_inc(score_mm, 1)
                        if not (last and u == UNITS - 1):
                            project_key(unit + 1, 2 * i + (u + 1) // 2, ((u + 1) // 2) % 2, (u + 1) % 2, t)
                        if t > 0:
                            weigh(unit, u, t - 1)
                        if t == 2 and u > 0:
                            denominators(i, u - 1)
                        if u % 2 == 0 and t >= 5 and not (last and u == 2):
                            turn_context(2 * i + u // 2 + 1, (u // 2 + 1) % 2, t - 5)
                    if u % 2 == 0 and not (last and u == 2):
                        turn_context(2 * i + u // 2 + 1, (u // 2 + 1) % 2, 3)
                    weigh(unit, u, ST - 1)
                denominators(i, UNITS - 1)
                pe.wait_ge(exp_done, (i + 1) * UNITS * ST + RING)
                pe.wait_ge(mix_ready, i * UNITS + 3)
                project_values(i, 0)
                pe.wait_ge(mix_ready, (i + 1) * UNITS)
                project_values(i, 1).then_inc(value_mm, 1)
                pe.wait_ge(outT_ready, 2 * (i + 1))
                for pair in range(NPAIR):
                    mm = nc.tensor.matmul(den_ps[:, 0:D], outT[:, pair, :], wo[:, pair, :],
                                          start=pair == 0, stop=pair == NPAIR - 1)
                mm.then_inc(out_mm, 1)
                pe.wait_ge(x_added, i + 1)

            with pe.Fori(0, TT - 1) as i:
                turn(i, False)
            turn(TT - 1, True)


def self_attention_0(own, nc, A, sb, sem, x, cols, rows, ident, head_mask, band, ps, col, row, finished):
    HD = D // H
    h = sb("sa_h", [P, TT, D], own)
    hT = sb("sa_hT", [P, KT, T], own)
    wqk = sb("sa_wqk", [P, KT, 2 * D], own)
    wgate = sb("sa_wgate", [P, KT, H], own)
    wproj = sb("sa_wproj", [P, KT, D], own)
    qT = sb("sa_qT", [P, KT, T], own)
    kT = sb("sa_kT", [P, KT, T], own)
    keys = sb("sa_keys", [P, TT, D], own)
    gates = sb("sa_gates", [P, TT, H], own)
    gatesT = sb("sa_gatesT", [H, T], own)
    gateX = sb("sa_gateX", [P, KT, T], own)
    spread = sb("sa_spread", [H, D], own)
    own_half = sb("sa_own_half", [P, 2], own)
    qblk = [sb(f"sa_qblk{i}", [P, 2, KT, 8, N], own) for i in range(2)]
    p = [sb(f"sa_p{i}", [P, NPAIR, 2, N], own) for i in range(2)]
    pT = [sb(f"sa_pT{i}", [P, NPAIR, P], own) for i in range(2)]
    outT = [sb(f"sa_outT{i}", [P, KT, P], own) for i in range(2)]
    stats = sb("sa_stats", [P, TT, 6], own)
    mv = sb("sa_mv", [P, TT, 2], own)
    var = sb("sa_var", [P, TT], own)
    rstd = sb("sa_rstd", [P, TT], own)
    half = sb("sa_half", [P, TT], own)
    top = sb("sa_top", [P, 2 * NPAIR], own)
    total = sb("sa_total", [P, 2 * NPAIR], own)

    w_loaded = sem("sa_w_loaded"); consts = sem("sa_consts"); pool_step = sem("sa_pool_step")
    dve_step = sem("sa_dve_step"); var_ready = sem("sa_var"); rstd_ready = sem("sa_rstd")
    h_ready = sem("sa_h_ready"); h_turned = sem("sa_h_turned"); hT_ready = sem("sa_hT_ready")
    qk_mm = sem("sa_qk_mm"); q_ready = sem("sa_q_ready"); k_ready = sem("sa_k_ready"); keys_mm = sem("sa_keys_mm"); keys_ready = sem("sa_keys_ready")
    gate_mm = sem("sa_gate_mm"); gate_arg = sem("sa_gate_arg"); gate_exp = sem("sa_gate_exp")
    gates_ready = sem("sa_gates_ready"); gates_turned = sem("sa_gates_turned"); gatesT_ready = sem("sa_gatesT_ready")
    spread_mm = sem("sa_spread_mm"); gateX_ready = sem("sa_gateX_ready")
    qblk_ready = sem("sa_qblk_ready"); score_mm = sem("sa_score_mm"); score_read = sem("sa_score_read")
    arg_ready = sem("sa_arg_ready"); exp_done = sem("sa_exp_done"); p_ready = sem("sa_p_ready")
    p_turned = sem("sa_p_turned"); pT_ready = sem("sa_pT_ready"); out_mm = sem("sa_out_mm")
    outT_ready = sem("sa_outT_ready"); proj_mm = sem("sa_proj_mm"); x_added = sem("sa_x_added")

    scores = ps[:, 0:4, :].rearrange("p (b c) (a s) -> p b (c a) s", b=2, a=4)
    outs = ps[:, 6:8, 0:KT * P].rearrange("p b (g c) -> p b g c", g=KT)

    with nc.Block() as block:
        @block.sync
        def _(sp):
            sp.dma_start(wqk[:], A["L0_attn_Wqk"].rearrange("(k p) n -> p k n", p=P)).then_inc(w_loaded, 16)
            sp.dma_start(wgate[:], A["L0_attn_Wgate"].rearrange("(k p) n -> p k n", p=P)).then_inc(w_loaded, 16)
            sp.dma_start(wproj[:], A["L0_attn_Wproj"].rearrange("(k p) n -> p k n", p=P)).then_inc(w_loaded, 16)

        @block.gpsimd
        def _(pool):
            for s in finished:
                pool.sem_clear(s)
            step = Chain(pool, pool_step)
            step.link(nc.gpsimd.memset(half[:], -0.5))
            pool.wait_ge(var_ready, 1)
            nc.gpsimd.tensor_tensor(out=rstd[:], in0=var[:], in1=half[:], op=ALU.pow).then_inc(rstd_ready, 1)
            pool.wait_ge(rstd_ready, 1)
            step.link(nc.gpsimd.memset(spread[:], 1.0))
            for sign, base in ((1, 0), (-1, HD - 1)):
                step.link(nc.gpsimd.affine_select(out=spread[:], in_=spread[:], compare_op=ALU.is_ge, fill=0.0,
                                                  base=base, pattern=[[sign, D]], channel_multiplier=-HD * sign))
            pool.sem_inc(consts, 1)
            pool.wait_ge(q_ready, KT)
            for tt in range(TT):
                if tt >= 2:
                    pool.wait_ge(score_mm, tt - 1)
                for b in range(2):
                    for g in range(KT):
                        at = (2 * tt + b) * N
                        step.link(nc.gpsimd.tensor_tensor(
                            out=qblk[tt % 2][:, b, g], in0=head_mask[:].unsqueeze(2).to_broadcast([P, 8, N]),
                            in1=qT[:, g, at:at + N].unsqueeze(1).to_broadcast([P, 8, N]), op=ALU.mult))
                pool.sem_inc(qblk_ready, 1)

        @block.scalar
        def _(act):
            def copy_pT(tt):
                if tt >= 2:
                    act.wait_ge(out_mm, tt - 1)
                for n in range(2):
                    act.wait_ge(p_turned, 2 * tt + n + 1)
                    nc.scalar.copy(pT[tt % 2][:, 4 * n:4 * n + 4, :], ps[:, 4 + n, :].rearrange("p (a t) -> p a t", a=4)).then_inc(pT_ready, 1)

            for k in range(KT):
                act.wait_ge(h_turned, k + 1)
                nc.scalar.copy(hT[:, k, :], ps[:, k, :]).then_inc(hT_ready, 1)
            for g in range(KT):
                act.wait_ge(qk_mm, KT + g + 1)
                nc.scalar.activation(kT[:, g, :], ps[:, 2 + KT + g, :], ACT.Identity,
                                     bias=col("L0_attn_bqk", 2 + g)).then_inc(k_ready, 1)
            act.wait_ge(gate_arg, 1)
            nc.scalar.activation(gates[:], gates[:], ACT.Exp).then_inc(gate_exp, 1)
            act.wait_ge(gates_turned, 1)
            nc.scalar.copy(gatesT[:], ps[0:H, 1, :]).then_inc(gatesT_ready, 1)
            for g in range(KT):
                act.wait_ge(spread_mm, g + 1)
                nc.scalar.copy(gateX[:, g, :], ps[:, 2 + g, :]).then_inc(gateX_ready, 1)
            for tt in range(TT):
                act.wait_ge(arg_ready, tt + 1)
                nc.scalar.activation(p[tt % 2][:], p[tt % 2][:], ACT.Exp).then_inc(exp_done, 1)
                if tt > 0:
                    copy_pT(tt - 1)
            copy_pT(TT - 1)

        @block.vector
        def _(dve):
            step = Chain(dve, dve_step)
            norm_stats(nc, step, x, stats, mv, var, TT, var_ready)
            dve.wait_ge(rstd_ready, 1)
            norm_apply(nc, h, x, mv, rstd, TT).then_inc(h_ready, 1)
            for g in range(KT):
                dve.wait_ge(qk_mm, g + 1)
                nc.vector.tensor_scalar(qT[:, g, :], ps[:, 2 + g, :], col("L0_attn_bqk", g), HD ** -0.5,
                                        ALU.add, ALU.mult).then_inc(q_ready, 1)
            for tt in range(TT):
                dve.wait_ge(keys_mm, 2 * (tt // 2 + 1))
                last = nc.vector.tensor_tensor(out=keys[:, tt, :], in0=ps[:, 6 + tt // 2, (tt % 2) * D:(tt % 2 + 1) * D],
                                               in1=row("L0_attn_bqk", D, D), op=ALU.add)
            last.then_inc(keys_ready, 1)
            step.link(nc.vector.tensor_reduce(out=own_half[:], in_=head_mask[:].rearrange("p (j two) -> p two j", two=2),
                                              axis=AX.X, op=ALU.add))
            dve.wait_ge(gate_mm, 1)
            step.link(nc.vector.tensor_tensor(out=gates[:], in0=ps[:, 0, 0:TT * H].rearrange("p (t h) -> p t h", t=TT),
                                              in1=row("L0_attn_bgate").unsqueeze(1).to_broadcast([P, TT, H]), op=ALU.add))
            softmax_rows(nc, step, gates[:], H, top[:, 0:TT]).then_inc(gate_arg, 1)
            dve.wait_ge(gate_exp, 1)
            normalise_rows(nc, step, gates[:], total[:, 0:TT]).then_inc(gates_ready, 1)

            def scores_to_args(tt):
                dve.wait_ge(score_mm, tt + 1)
                if tt >= 2:
                    dve.wait_ge(p_turned, 2 * (tt - 1))
                pt = p[tt % 2]
                for b in range(2):
                    last = nc.vector.tensor_tensor(out=pt[:, :, b, :], in0=scores[:, b, :, b * N:(b + 1) * N],
                                                   in1=band[:], op=ALU.add)
                last.then_inc(score_read, 1)
                dve.wait_ge(score_read, tt + 1)
                softmax_rows(nc, step, pt[:].rearrange("p a b n -> p (a b) n"), N, top[:]).then_inc(arg_ready, 1)

            def args_to_p(tt):
                dve.wait_ge(exp_done, tt + 1)
                normalise_rows(nc, step, p[tt % 2][:].rearrange("p a b n -> p (a b) n"), total[:]).then_inc(p_ready, 1)

            def finish(tt):
                dve.wait_ge(out_mm, tt + 1)
                if tt == 0:
                    dve.wait_ge(gateX_ready, KT)
                if tt >= 2:
                    dve.wait_ge(proj_mm, tt - 1)
                o = outT[tt % 2]
                for b in range(2):
                    last = nc.vector.tensor_scalar(o[:, :, b * N:(b + 1) * N], outs[:, b, :, 0:N], own_half[:, 0:1], None, ALU.mult)
                step.link(last)
                for b in range(2):
                    part = o[:, :, b * N:(b + 1) * N]
                    last = nc.vector.scalar_tensor_tensor(out=part, in0=outs[:, b, :, N:P], scalar=own_half[:, 1:2], in1=part,
                                                          op0=ALU.mult, op1=ALU.add)
                step.link(last)
                nc.vector.tensor_tensor(out=o[:], in0=o[:], in1=gateX[:, :, tt * P:(tt + 1) * P], op=ALU.mult).then_inc(outT_ready, 1)

            def residual(tt):
                dve.wait_ge(proj_mm, tt + 1)
                step.link(nc.vector.tensor_tensor(out=x[:, tt, :], in0=ps[:, 5, 0:D], in1=x[:, tt, :], op=ALU.add))
                nc.vector.tensor_tensor(out=x[:, tt, :], in0=x[:, tt, :], in1=row("L0_attn_bproj"), op=ALU.add).then_inc(x_added, 1)

            scores_to_args(0)
            for tt in range(TT):
                args_to_p(tt)
                if tt + 1 < TT:
                    scores_to_args(tt + 1)
                finish(tt)
                residual(tt)

        @block.tensor
        def _(pe):
            pe.wait_ge(h_ready, 1)
            for k in range(KT):
                for t in range(TT):
                    last = nc.tensor.transpose(ps[:, k, t * P:(t + 1) * P], h[:, t, k * P:(k + 1) * P], ident[:])
                last.then_inc(h_turned, 1)
            pe.wait_ge(hT_ready, KT)
            pe.wait_ge(w_loaded, 48)
            for n in range(2 * KT):
                for k in range(KT):
                    last = nc.tensor.matmul(ps[:, 2 + n, :], wqk[:, k, n * P:(n + 1) * P], hT[:, k, :],
                                            start=k == 0, stop=k == KT - 1)
                last.then_inc(qk_mm, 1)
            for tt in range(TT):
                for k in range(KT):
                    last = nc.tensor.matmul(ps[:, 6 + tt // 2, (tt % 2) * D:(tt % 2 + 1) * D], hT[:, k, tt * P:(tt + 1) * P],
                                            wqk[:, k, D:2 * D], start=k == 0, stop=k == KT - 1)
                last.then_inc(keys_mm, 1)
            for tt in range(TT):
                for k in range(KT):
                    last = nc.tensor.matmul(ps[:, 0, tt * H:(tt + 1) * H], hT[:, k, tt * P:(tt + 1) * P], wgate[:, k, :],
                                            start=k == 0, stop=k == KT - 1)
            last.then_inc(gate_mm, 1)
            pe.wait_ge(gates_ready, 1)
            for tt in range(TT):
                last = nc.tensor.matmul(ps[0:H, 1, tt * P:(tt + 1) * P], gates[:, tt, :], ident[:], start=True, stop=True)
            last.then_inc(gates_turned, 1)
            pe.wait_ge(gatesT_ready, 1)
            pe.wait_ge(consts, 1)
            pe.wait_ge(q_ready, KT)
            pe.wait_ge(k_ready, KT)
            for g in range(KT):
                nc.tensor.matmul(ps[:, 2 + g, :], spread[:, g * P:(g + 1) * P], gatesT[:], start=True, stop=True).then_inc(spread_mm, 1)
            pe.wait_ge(gateX_ready, KT)
            pe.wait_ge(keys_ready, 1)

            def score(tt):
                pe.wait_ge(qblk_ready, tt + 1)
                if tt > 0:
                    pe.wait_ge(score_read, tt)
                for b in range(2):
                    for pair in range(NPAIR):
                        g, j = pair // 4, pair % 4
                        last = nc.tensor.matmul(scores[:, b, pair, :], qblk[tt % 2][:, b, g, 2 * j:2 * j + 2, :].rearrange("p a n -> p (a n)"),
                                                kT[:, g, tt * P:(tt + 1) * P], start=True, stop=True)
                last.then_inc(score_mm, 1)

            def weigh(tt):
                pe.wait_ge(p_ready, tt + 1)
                for n in range(2):
                    if tt > 0:
                        pe.wait_ge(pT_ready, 2 * (tt - 1) + n + 1)
                        if n == 1:
                            pe.wait_ge(x_added, tt)
                    for j in range(4):
                        last = nc.tensor.transpose(ps[:, 4 + n, j * P:(j + 1) * P],
                                                   p[tt % 2][:, 4 * n + j].rearrange("p b n -> p (b n)"), ident[:])
                    last.then_inc(p_turned, 1)
                pe.wait_ge(pT_ready, 2 * (tt + 1))
                if tt > 0:
                    pe.wait_ge(outT_ready, tt)
                for b in range(2):
                    for pair in range(NPAIR):
                        g, j = pair // 4, pair % 4
                        last = nc.tensor.matmul(outs[32 * j:32 * j + 32, b, g, :], keys[64 * b:64 * b + 64, tt, pair * 32:(pair + 1) * 32],
                                                pT[tt % 2][64 * b:64 * b + 64, pair, :], start=True, stop=True)
                last.then_inc(out_mm, 1)

            def project(tt):
                pe.wait_ge(outT_ready, tt + 1)
                for g in range(KT):
                    last = nc.tensor.matmul(ps[:, 5, 0:D], outT[tt % 2][:, g, :], wproj[:, g, :], start=g == 0, stop=g == KT - 1)
                last.then_inc(proj_mm, 1)

            score(0)
            for tt in range(TT):
                if tt + 1 < TT:
                    score(tt + 1)
                weigh(tt)
                project(tt)


def experts_0(own, nc, A, sb, sem, x, cols, rows, ident, head_mask, band, ps, col, row, finished):
    HT = H0 // P
    h = sb("e0_h", [P, TT, D], own)
    hT = sb("e0_hT", [P, KT, T], own)
    wgate = sb("e0_wgate", [P, KT, E], own)
    w1 = sb("e0_w1", [P, E, KT, H0], own)
    w2 = sb("e0_w2", [P, E, HT, D], own)
    b1 = sb("e0_b1", [P, E * H0], own)
    b2 = sb("e0_b2", [E, D], own)
    gates = sb("e0_gates", [P, TT, E], own)
    chosen = sb("e0_chosen", [P, TT, E], own)
    chosenT = sb("e0_chosenT", [E, T], own)
    rank = sb("e0_rank", [P, E], own)
    work = sb("e0_work", [P, 3, TT, E], own)
    best = sb("e0_best", [P, 3, TT], own)
    hn = [sb(f"e0_hn{i}", [P, H0], own) for i in range(2)]
    act_T = [sb(f"e0_act{i}", [P, HT, P], own) for i in range(2)]
    acc = sb("e0_acc", [P, TT, D], own)
    stats = sb("e0_stats", [P, TT, 6], own)
    mv = sb("e0_mv", [P, TT, 2], own)
    var = sb("e0_var", [P, TT], own)
    rstd = sb("e0_rstd", [P, TT], own)
    half = sb("e0_half", [P, TT], own)
    top = sb("e0_top", [P, TT], own)
    total = sb("e0_total", [P, TT], own)

    act_passed = sem("e0_act_passed"); dve_passed = sem("e0_dve_passed")
    small_loaded = sem("e0_small"); b1_loaded = sem("e0_b1_loaded")
    w1_loaded = sem("e0_w1_loaded"); w2_loaded = sem("e0_w2_loaded")
    pool_step = sem("e0_pool_step"); dve_step = sem("e0_dve_step"); var_ready = sem("e0_var")
    rstd_ready = sem("e0_rstd"); h_ready = sem("e0_h_ready"); h_turned = sem("e0_h_turned"); hT_ready = sem("e0_hT_ready")
    gate_mm = sem("e0_gate_mm"); gate_arg = sem("e0_gate_arg"); gate_exp = sem("e0_gate_exp")
    chosen_ready = sem("e0_chosen_ready"); chosen_turned = sem("e0_chosen_turned"); chosenT_ready = sem("e0_chosenT_ready")
    bias_mm = sem("e0_bias_mm"); acc_started = sem("e0_acc_started")
    up_mm = sem("e0_up_mm"); up_read = sem("e0_up_read"); unit_var = sem("e0_unit_var"); unit_rstd = sem("e0_unit_rstd")
    hn_ready = sem("e0_hn_ready"); hn_turned = sem("e0_hn_turned"); gelu_done = sem("e0_gelu")
    down_mm = sem("e0_down_mm"); acc_added = sem("e0_acc_added")

    RING = 2
    w1f = w1[:].rearrange("p e k n -> p (e k n)")
    w2f = w2[:].rearrange("p e k n -> p (e k n)")

    with nc.Block() as block:
        @block.sync
        def _(sp):
            sp.dma_start(wgate[:], A["L0_ffn_gate_w"].rearrange("(k p) n -> p k n", p=P)).then_inc(small_loaded, 16)
            sp.dma_start(b2[:], A["L0_ffn_b2"]).then_inc(small_loaded, 16)
            sp.dma_start(b1[:], A["L0_ffn_b1"].to_broadcast([P, E * H0])).then_inc(b1_loaded, 16)
            for e in range(E):
                sp.dma_start(w1[:, e], A["L0_ffn_w1"][e].rearrange("(k p) n -> p k n", p=P)).then_inc(w1_loaded, 16)
                sp.dma_start(w2[:, e], A["L0_ffn_w2"][e].rearrange("(k p) n -> p k n", p=P)).then_inc(w2_loaded, 16)
                sp.wait_ge(w1_loaded, 16 * (e + 1))
                sp.wait_ge(w2_loaded, 16 * (e + 1))

        @block.gpsimd
        def _(pool):
            for s in finished:
                pool.sem_clear(s)
            step = Chain(pool, pool_step)
            step.link(nc.gpsimd.memset(half[:], -0.5))
            pool.wait_ge(var_ready, 1)
            nc.gpsimd.tensor_tensor(out=rstd[:], in0=var[:], in1=half[:], op=ALU.pow).then_inc(rstd_ready, 1)
            with pool.Fori(0, E * TT, 2) as n:
                for c in range(2):
                    pool.wait_ge(unit_var, n + c + 1)
                    nc.gpsimd.tensor_tensor(out=rstd[:, c:c + 1], in0=var[:, c:c + 1], in1=half[:, c:c + 1], op=ALU.pow).then_inc(unit_rstd, 1)
            pool.wait_ge(var_ready, 2)
            nc.gpsimd.tensor_tensor(out=rstd[:], in0=var[:], in1=half[:], op=ALU.pow).then_inc(rstd_ready, 1)

        @block.scalar
        def _(act):
            act.sem_inc(gelu_done, RING)
            for k in range(KT):
                act.wait_ge(h_turned, k + 1)
                nc.scalar.copy(hT[:, k, :], ps[:, 6 + k, :]).then_inc(hT_ready, 1)
            act.wait_ge(gate_arg, 1)
            nc.scalar.activation(gates[:], gates[:], ACT.Exp).then_inc(gate_exp, 1)
            act.wait_ge(chosen_turned, 1)
            nc.scalar.copy(chosenT[:], ps[0:E, 7, :]).then_inc(chosenT_ready, 1)
            with act.Fori(0, E) as e:
                for t in range(TT):
                    n = e * TT + t
                    act.wait_ge(hn_turned, n + 1 + RING)
                    wait_alone(act, act_passed, down_mm, n + 1)
                    for k in range(HT):
                        g_at, b_at = COL_AT["L0_ffn_ln1_g"] + e * HT + k, COL_AT["L0_ffn_ln1_b"] + e * HT + k
                        last = nc.scalar.activation(act_T[t % 2][:, k, :], ps[:, 2 + t % 2, k * P:(k + 1) * P], ACT.Gelu,
                                                    bias=cols[:, bass.ds(b_at, 1)], scale=cols[:, bass.ds(g_at, 1)])
                    last.then_inc(gelu_done, 1)

        @block.vector
        def _(dve):
            dve.sem_inc(up_read, RING)
            dve.sem_inc(acc_added, RING)
            step = Chain(dve, dve_step)
            for e in range(E):
                last = nc.vector.memset(rank[:, e:e + 1], float(E - e))
            step.link(last)
            norm_stats(nc, step, x, stats, mv, var, TT, var_ready)
            dve.wait_ge(rstd_ready, 1)
            norm_apply(nc, h, x, mv, rstd, TT).then_inc(h_ready, 1)
            dve.wait_ge(gate_mm, 1)
            step.link(nc.vector.tensor_copy(gates[:], ps[:, 6, 0:TT * E].rearrange("p (t e) -> p t e", t=TT)))
            softmax_rows(nc, step, gates[:], E, top[:]).then_inc(gate_arg, 1)
            dve.wait_ge(gate_exp, 1)
            step.link(normalise_rows(nc, step, gates[:], total[:]))
            top_two(nc, step, gates[:], rank[:], chosen[:], work, best).then_inc(chosen_ready, 1)
            dve.wait_ge(bias_mm, 1)
            for t in range(TT):
                last = nc.vector.tensor_copy(acc[:, t, :], ps[:, 6 + t // 2, (t % 2) * D:(t % 2 + 1) * D])
            step.link(last)
            dve.wait_ge(b1_loaded, 16)

            def norm_unit(e, t):
                n = e * TT + t
                hid, c = hn[t % 2], t % 2
                dve.wait_ge(up_mm, n + 1)
                dve.wait_ge(hn_turned, n + 1)
                nc.vector.tensor_tensor(out=hid[:], in0=ps[:, t % 2, :], in1=b1[:, bass.ds(e * H0, H0)], op=ALU.add).then_inc(up_read, 1)
                dve.wait_ge(up_read, n + 1 + RING)
                step.link_alone(nc.vector.bn_stats(stats[:, c, :], hid[:]), dve_passed)
                step.link(nc.vector.bn_aggr(mv[:, c, :], stats[:, c, :]))
                nc.vector.tensor_scalar(var[:, c:c + 1], mv[:, c, 1:2], EPS, None, ALU.add).then_inc(unit_var, 1)
                dve.wait_ge(unit_rstd, n + 1)
                nc.vector.tensor_scalar(hid[:], hid[:], mv[:, c, 0:1], rstd[:, c:c + 1],
                                        ALU.subtract, ALU.mult).then_inc(hn_ready, 1)

            def add_unit(e, t):
                n = e * TT + t
                dve.wait_ge(down_mm, n + 1 + RING)
                nc.vector.scalar_tensor_tensor(out=acc[:, t, :], in0=ps[:, 4 + t % 2, 0:D],
                                               scalar=chosen[:].rearrange("p t e -> p (t e)")[:, bass.ds(t * E + e, 1)],
                                               in1=acc[:, t, :], op0=ALU.mult, op1=ALU.add).then_inc(acc_added, 1)

            def turn(e, start=False):
                for t in range(TT):
                    norm_unit(e, t)
                    if t >= 2:
                        add_unit(e, t - 2)
                    elif not start:
                        add_unit(e - 1, t + 2)

            turn(0, start=True)
            LINKS = 2 * TT
            first = step.n
            with dve.Fori(1, E) as e:
                step.base, step.n = (e - 1) * LINKS, first
                turn(e)
            assert step.n == first + LINKS
            step.base = (E - 2) * LINKS
            add_unit(E - 1, 2)
            add_unit(E - 1, 3)
            dve.wait_ge(acc_added, E * TT + RING)
            step.link(nc.vector.tensor_tensor(out=acc[:], in0=acc[:], in1=h[:], op=ALU.add))
            norm_stats(nc, step, acc, stats, mv, var, TT, var_ready)
            dve.wait_ge(rstd_ready, 2)
            step.link(norm_apply(nc, acc, acc, mv, rstd, TT))
            step.link(nc.vector.tensor_tensor(out=acc[:], in0=acc[:], in1=row("L0_ffn_ln_g").unsqueeze(1).to_broadcast([P, TT, D]), op=ALU.mult))
            step.link(nc.vector.tensor_tensor(out=x[:], in0=x[:], in1=row("L0_ffn_ln_b").unsqueeze(1).to_broadcast([P, TT, D]), op=ALU.add))
            nc.vector.tensor_tensor(out=x[:], in0=x[:], in1=acc[:], op=ALU.add)

        @block.tensor
        def _(pe):
            pe.sem_inc(hn_turned, RING)
            pe.sem_inc(down_mm, RING)
            pe.wait_ge(h_ready, 1)
            for k in range(KT):
                for t in range(TT):
                    last = nc.tensor.transpose(ps[:, 6 + k, t * P:(t + 1) * P], h[:, t, k * P:(k + 1) * P], ident[:])
                last.then_inc(h_turned, 1)
            pe.wait_ge(hT_ready, KT)
            pe.wait_ge(small_loaded, 32)
            for t in range(TT):
                for k in range(KT):
                    last = nc.tensor.matmul(ps[:, 6, t * E:(t + 1) * E], hT[:, k, t * P:(t + 1) * P], wgate[:, k, :],
                                            start=k == 0, stop=k == KT - 1)
            last.then_inc(gate_mm, 1)

            def up(e, t):
                n = e * TT + t
                pe.wait_ge(up_read, n + 1)
                for k in range(KT):
                    last = nc.tensor.matmul(ps[:, t % 2, :], hT[:, k, t * P:(t + 1) * P],
                                            w1f[:, bass.ds((e * KT + k) * H0, H0)], start=k == 0, stop=k == KT - 1)
                last.then_inc(up_mm, 1)

            def turn_hidden(e, t):
                n = e * TT + t
                pe.wait_ge(hn_ready, n + 1)
                pe.wait_ge(gelu_done, n + 1)
                for k in range(HT):
                    last = nc.tensor.transpose(ps[:, 2 + t % 2, k * P:(k + 1) * P], hn[t % 2][:, k * P:(k + 1) * P], ident[:])
                last.then_inc(hn_turned, 1)

            def down(e, t):
                n = e * TT + t
                pe.wait_ge(gelu_done, n + 1 + RING)
                pe.wait_ge(acc_added, n + 1)
                for k in range(HT):
                    last = nc.tensor.matmul(ps[:, 4 + t % 2, 0:D], act_T[t % 2][:, k, :],
                                            w2f[:, bass.ds((e * HT + k) * D, D)], start=k == 0, stop=k == HT - 1)
                last.then_inc(down_mm, 1)

            pe.wait_ge(w1_loaded, 16)
            up(0, 0)
            up(0, 1)
            pe.wait_ge(chosen_ready, 1)
            for t in range(TT):
                last = nc.tensor.matmul(ps[0:E, 7, t * P:(t + 1) * P], chosen[:, t, :], ident[:], start=True, stop=True)
            last.then_inc(chosen_turned, 1)
            pe.wait_ge(chosenT_ready, 1)
            for t in range(TT):
                last = nc.tensor.matmul(ps[:, 6 + t // 2, (t % 2) * D:(t % 2 + 1) * D], chosenT[:, t * P:(t + 1) * P], b2[:],
                                        start=True, stop=True)
            last.then_inc(bias_mm, 1)
            pe.wait_ge(w2_loaded, 16)
            turn_hidden(0, 0)
            up(0, 2)
            turn_hidden(0, 1)
            down(0, 0)
            up(0, 3)
            turn_hidden(0, 2)
            down(0, 1)
            with pe.Fori(1, E) as e:
                pe.wait_ge(w1_loaded, 16 * (e + 1))
                pe.wait_ge(w2_loaded, 16 * (e + 1))
                for t in range(TT):
                    up(e, t)
                    if t >= 1:
                        turn_hidden(e, t - 1)
                    else:
                        turn_hidden(e - 1, TT - 1)
                    if t >= 2:
                        down(e, t - 2)
                    else:
                        down(e - 1, t + 2)
            turn_hidden(E - 1, TT - 1)
            down(E - 1, TT - 2)
            down(E - 1, TT - 1)


def cross_attention_1(own, nc, A, sb, sem, x, cols, rows, ident, head_mask, band, ps, col, row, finished):
    HD = D // H
    PB = NPAIR
    ITEMS = 12
    h = sb("x1_h", [P, TT, D], own)
    hT = sb("x1_hT", [P, KT, T], own)
    wq, wo = (sb(f"x1_w{n}", [P, KT, D], own) for n in "qo")
    wk_hi, wv_hi = (sb(f"x1_w{n}_hi", [P, KT, D], own, F32R) for n in "kv")
    wk_lo, wv_lo = (sb(f"x1_w{n}_lo", [P, KT, D], own, F32R) for n in "kv")
    qT = h[:].rearrange("p t d -> p (t d)").rearrange("p (k t) -> p k t", k=KT)
    qT_hi = sb("x1_qT_hi", [P, KT, T], own)
    qblk_hi = [sb(f"x1_qblk_hi{i}", [P, KT, 8, N], own, F32R) for i in range(2)]
    qblk_lo = [sb(f"x1_qblk_lo{i}", [P, KT, 8, N], own, F32R) for i in range(2)]
    raw = [sb(f"x1_raw{i}", [P, ST, D], own) for i in range(2)]
    cT_hi = sb("x1_cT_hi", [P, KT, S], own, F32R)
    cT_lo = sb("x1_cT_lo", [P, KT, S], own, F32R)
    kT_hi = [sb(f"x1_kT_hi{i}", [P, KT, S], own, F32R) for i in range(2)]
    kT_lo = [sb(f"x1_kT_lo{i}", [P, KT, S], own, F32R) for i in range(2)]
    v = [sb(f"x1_v{i}", [P, ST, D], own) for i in range(2)]
    p = [sb(f"x1_p{i}", [P, S], own) for i in range(2)]
    p_hi = [sb(f"x1_p_hi{i}", [P, S], own, F16) for i in range(2)]
    p_lo = [sb(f"x1_p_lo{i}", [P, S], own, F16) for i in range(2)]
    small_ident = sb("x1_small_ident", [P, P], own, F16)
    pT = [sb(f"x1_pT{i}", [P, 4, ST, P], own) for i in range(2)]
    wk, wv = (pT[i][:, 0, 0:KT * D // P].rearrange("p (k a) c -> p k (a c)", k=KT) for i in range(2))
    outT = sb("x1_outT", [P, KT, T], own)
    neg_top = sb("x1_neg_top", [P, 2], own)
    total = sb("x1_total", [P, 2], own)
    recip = sb("x1_recip", [P, 2], own)
    part = sb("x1_part", [P, N], own)
    own_half = sb("x1_own_half", [P, 2], own)
    stats = sb("x1_stats", [P, TT, 6], own)
    mv = sb("x1_mv", [P, TT, 2], own)
    var = sb("x1_var", [P, TT], own)
    rstd = sb("x1_rstd", [P, TT], own)
    half = sb("x1_half", [P, TT], own)

    w_loaded = sem("x1_w_loaded"); ctx_loaded = sem("x1_ctx_loaded"); pool_step = sem("x1_pool_step")
    dve_step = sem("x1_dve_step"); var_ready = sem("x1_var"); rstd_ready = sem("x1_rstd")
    h_ready = sem("x1_h_ready"); h_turned = sem("x1_h_turned"); hT_ready = sem("x1_hT_ready")
    q_mm = sem("x1_q_mm"); qT_ready = sem("x1_qT_ready"); qblk_ready = sem("x1_qblk_ready")
    item_mm = sem("x1_item_mm"); item_read = sem("x1_item_read")
    score_mm = sem("x1_score_mm"); max_ready = sem("x1_max_ready"); exp_done = sem("x1_exp_done")
    p_normed = sem("x1_p_normed"); w_rounded = sem("x1_w_rounded"); w_split = sem("x1_w_split"); q_split = sem("x1_q_split")
    item_rest = sem("x1_item_rest"); recip_ready = sem("x1_recip"); p_rounded = sem("x1_p_rounded")
    p_split = sem("x1_p_split"); p_turned = sem("x1_p_turned")
    pT_act = sem("x1_pT_act"); pT_dve = sem("x1_pT_dve"); value_mm = sem("x1_value_mm")
    outT_ready = sem("x1_outT_ready"); proj_mm = sem("x1_proj_mm")

    SCALE = 2.0 ** 14
    score_ps = [ps[:, 2 * a:2 * a + 2, :] for a in range(2)]
    item_ps = ps[:, 7, :]
    ctx_d = A["ctx_1024"].rearrange("b (t p) d -> b p t d", p=P)

    with nc.Block() as block:
        @block.sync
        def _(sp):
            sp.dma_start(raw[0][:], ctx_d[0]).then_inc(ctx_loaded, 16)
            for w, name in ((wq, "q"), (wk, "k"), (wv, "v"), (wo, "o")):
                sp.dma_start(w if name in "kv" else w[:], A[f"L1_xattn_W{name}T"].rearrange("(k p) n -> p k n", p=P)).then_inc(w_loaded, 16)
            sp.wait_ge(ctx_loaded, 16)
            sp.dma_start(raw[1][:], ctx_d[1]).then_inc(ctx_loaded, 16)
            with sp.Fori(0, TT - 1) as i:
                for a in range(2):
                    b = 2 * i + a
                    sp.wait_ge(item_mm, ITEMS * b + 4)
                    sp.wait_ge(ctx_loaded, 16 * (b + 2))
                    sp.dma_start(raw[a][:], ctx_d[bass.ds(b + 2, 1)].rearrange("b p t d -> (b p) t d")).then_inc(ctx_loaded, 16)

        @block.gpsimd
        def _(pool):
            for s in finished:
                pool.sem_clear(s)
            step = Chain(pool, pool_step)
            pool.sem_inc(p_split, 1)
            step.link(nc.gpsimd.memset(half[:], -0.5))
            step.link(nc.gpsimd.tensor_scalar(small_ident[:], ident[:], 1 / SCALE, None, ALU.mult))
            pool.wait_ge(var_ready, 1)
            nc.gpsimd.tensor_tensor(out=rstd[:], in0=var[:], in1=half[:], op=ALU.pow).then_inc(rstd_ready, 1)

            def queries(b, a):
                for g in range(KT):
                    for blk, src in ((qblk_hi, qT_hi), (qblk_lo, qT)):
                        q = src[:, g, :][:, bass.ds(b * N, N)].unsqueeze(1).to_broadcast([P, 8, N])
                        step.link(nc.gpsimd.tensor_tensor(out=blk[a][:, g], in0=head_mask[:].unsqueeze(2).to_broadcast([P, 8, N]),
                                                          in1=q, op=ALU.mult))
                pool.sem_inc(qblk_ready, 1)

            for n, (w, w_hi, w_lo) in enumerate(((wk, wk_hi, wk_lo), (wv, wv_hi, wv_lo))):
                pool.wait_ge(w_rounded, n + 1)
                nc.gpsimd.tensor_tensor(out=w_lo[:], in0=w, in1=w_hi[:].bitcast(F32), op=ALU.subtract).then_inc(w_split, 1)
            pool.wait_ge(q_split, KT)
            queries(0, 0)
            first = step.n

            def probability_rests(n, c):
                pool.wait_ge(p_rounded, n + 1)
                nc.gpsimd.tensor_tensor(out=p_lo[c][:], in0=p[c][:], in1=p_hi[c][:], op=ALU.subtract).then_inc(p_split, 1)

            def turn(i, last):
                step.base, step.n = i * 4 * KT, first
                for a in range(2):
                    for s in range(PB):
                        probability_rests((2 * i + a) * PB + s, s % 2)
                        if s == 2 and not (last and a == 1):
                            pool.wait_ge(score_mm, (2 * i + a + 1) * PB)
                            queries(2 * i + a + 1, (a + 1) % 2)

            with pool.Fori(0, TT - 1) as i:
                turn(i, False)
            turn(TT - 1, True)

        @block.scalar
        def _(act):
            act.sem_inc(pT_act, 1)
            for k in range(KT):
                act.wait_ge(h_turned, k + 1)
                nc.scalar.copy(hT[:, k, :], ps[:, k, :]).then_inc(hT_ready, 1)

            def read_item(b, a, k):
                act.wait_ge(item_mm, ITEMS * b + k + 1)
                if k < 4:
                    ins = nc.scalar.copy(cT_hi[:, k % 2, (k // 2) * 512:(k // 2) * 512 + 512], item_ps)
                elif k < 8:
                    g, half_ = k % 2, (k - 4) // 2
                    ins = nc.scalar.activation(kT_hi[a][:, g, half_ * 512:half_ * 512 + 512], item_ps, ACT.Identity,
                                               bias=col("L1_xattn_bk", g))
                else:
                    ins = nc.scalar.copy(v[a][:, 2 * (k - 8):2 * (k - 8) + 2, :], item_ps.rearrange("p (t d) -> p t d", t=2))
                ins.then_inc(item_read, 1)

            def exponentials(n, c):
                act.wait_ge(max_ready, n + 1)
                nc.scalar.activation(p[c][:], score_ps[c].rearrange("p a s -> p (a s)"), ACT.Exp, bias=neg_top[:, c:c + 1],
                                     accum_out=total[:, c:c + 1]).then_inc(exp_done, 1)

            def normalise_probabilities(n, c):
                act.wait_ge(recip_ready, n + 1)
                nc.scalar.activation(p[c][:], p[c][:], ACT.Copy, scale=recip[:, c:c + 1]).then_inc(p_normed, 1)

            act.wait_ge(w_loaded, 64)
            for w, w_hi in ((wk, wk_hi), (wv, wv_hi)):
                nc.scalar.copy(w_hi[:], w).then_inc(w_rounded, 1)
            for k in range(ITEMS):
                read_item(0, 0, k)
            exponentials(0, 0)
            exponentials(1, 1)
            for c in range(2):
                normalise_probabilities(c, c)

            def turn(i, last):
                for a in range(2):
                    for s in range(PB):
                        n = (2 * i + a) * PB + s
                        more = not (last and a == 1 and s >= PB - 2)
                        items = not (last and a == 1) and s < 6
                        if items:
                            read_item(2 * i + a + 1, (a + 1) % 2, 2 * s)
                        if more:
                            act.wait_ge(p_split, n + 2)
                            exponentials(n + 2, s % 2)
                        act.wait_ge(p_turned, 2 * n + 3)
                        act.wait_ge(value_mm, 4 * i + 2 * a + s // 4 + 1)
                        nc.scalar.copy(pT[s // 4][:, s % 4, 0:4, :], ps[:, 4, :].rearrange("p (t c) -> p t c", t=4)).then_inc(pT_act, 1)
                        if items:
                            read_item(2 * i + a + 1, (a + 1) % 2, 2 * s + 1)
                        if more:
                            normalise_probabilities(n + 2, s % 2)

            with act.Fori(0, TT - 1) as i:
                turn(i, False)
            turn(TT - 1, True)

        @block.vector
        def _(dve):
            step = Chain(dve, dve_step)
            dve.sem_inc(pT_dve, 1)
            dve.sem_inc(outT_ready, 1)
            norm_stats(nc, step, x, stats, mv, var, TT, var_ready)
            step.link(nc.vector.tensor_reduce(out=own_half[:], in_=head_mask[:].rearrange("p (j two) -> p two j", two=2),
                                              axis=AX.X, op=ALU.add))
            dve.wait_ge(rstd_ready, 1)
            norm_apply(nc, h, x, mv, rstd, TT).then_inc(h_ready, 1)
            for g in range(KT):
                dve.wait_ge(q_mm, g + 1)
                nc.vector.tensor_scalar(qT[:, g, :], ps[:, 2 + g, :], col("L1_xattn_bq", g), HD ** -0.5,
                                        ALU.add, ALU.mult).then_inc(qT_ready, 1)
                dve.wait_ge(qT_ready, g + 1)
                step.link(nc.vector.tensor_copy(qT_hi[:, g, :].bitcast(F32R), qT[:, g, :]))
                nc.vector.tensor_tensor(out=qT[:, g, :], in0=qT[:, g, :], in1=qT_hi[:, g, :], op=ALU.subtract).then_inc(q_split, 1)

            def maximum(n, c):
                dve.wait_ge(score_mm, n + 1 + PB)
                nc.vector.tensor_reduce(out=neg_top[:, c:c + 1], in_=score_ps[c], axis=AX.XY, op=ALU.max,
                                        negate=True).then_inc(max_ready, 1)

            def denominator(n, c):
                dve.wait_ge(exp_done, n + 1)
                step.link(nc.vector.reciprocal(recip[:, c:c + 1], total[:, c:c + 1]))
                nc.vector.tensor_scalar(recip[:, c:c + 1], recip[:, c:c + 1], SCALE, None, ALU.mult).then_inc(recip_ready, 1)

            def round_probabilities(n, c):
                dve.wait_ge(p_normed, n + 1)
                nc.vector.tensor_copy(p_hi[c][:], p[c][:]).then_inc(p_rounded, 1)

            def item_rests(b, a, k):
                if k < 8:
                    dve.wait_ge(item_read, ITEMS * b + k + 1)
                    g, at = k % 2, slice((k % 4) // 2 * 512, (k % 4) // 2 * 512 + 512)
                    if k < 4:
                        ins = nc.vector.tensor_tensor(out=cT_lo[:, g, at], in0=item_ps, in1=cT_hi[:, g, at].bitcast(F32), op=ALU.subtract)
                    else:
                        ins = nc.vector.scalar_tensor_tensor(out=kT_lo[a][:, g, at], in0=item_ps, scalar=col("L1_xattn_bk", g),
                                                             in1=kT_hi[a][:, g, at].bitcast(F32), op0=ALU.add, op1=ALU.subtract)
                    ins.then_inc(item_rest, 1)

            def keep_own(i, a, g):
                group = 4 * i + 2 * a + g
                dve.wait_ge(value_mm, group + 3)
                src = ps[:, 6, g * P:(g + 1) * P]
                step.link(nc.vector.tensor_scalar(part[:], src[:, 0:N], own_half[:, 0:1], col("L1_xattn_bv", g), ALU.mult, ALU.add))
                nc.vector.scalar_tensor_tensor(out=outT[:, g, :][:, bass.ds((2 * i + a) * N, N)], in0=src[:, N:P],
                                               scalar=own_half[:, 1:2], in1=part[:], op0=ALU.mult, op1=ALU.add).then_inc(outT_ready, 1)
                dve.wait_ge(outT_ready, group + 2)

            for k in range(8):
                item_rests(0, 0, k)
            maximum(0, 0)
            maximum(1, 1)
            denominator(0, 0)
            denominator(1, 1)
            round_probabilities(0, 0)
            first = step.n

            def turn(i, last):
                step.base, step.n = i * LINKS, first
                for a in range(2):
                    for s in range(PB):
                        n = (2 * i + a) * PB + s
                        items = not (last and a == 1) and s < 6
                        if not (last and a == 1 and s >= PB - 2):
                            maximum(n + 2, s % 2)
                        if not (last and a == 1 and s == PB - 1):
                            round_probabilities(n + 1, (s + 1) % 2)
                        if items:
                            item_rests(2 * i + a + 1, (a + 1) % 2, 2 * s)
                        dve.wait_ge(p_turned, 2 * n + 4)
                        dve.wait_ge(value_mm, 4 * i + 2 * a + s // 4 + 1)
                        nc.vector.tensor_copy(pT[s // 4][:, s % 4, 4:8, :], ps[:, 5, :].rearrange("p (t c) -> p t c", t=4)).then_inc(pT_dve, 1)
                        if items:
                            item_rests(2 * i + a + 1, (a + 1) % 2, 2 * s + 1)
                        if not (last and a == 1 and s >= PB - 2):
                            denominator(n + 2, s % 2)
                        if s % 4 == 3:
                            keep_own(i, a, s // 4)

            LINKS = 2 * PB + 4
            with dve.Fori(0, TT - 1) as i:
                turn(i, False)
            assert step.n == first + LINKS
            turn(TT - 1, True)
            for t in range(TT):
                dve.wait_ge(proj_mm, 2 * (t // 2 + 1))
                step.link(nc.vector.tensor_tensor(out=x[:, t, :], in0=ps[:, t // 2, (t % 2) * D:(t % 2 + 1) * D], in1=x[:, t, :], op=ALU.add))
            nc.vector.tensor_tensor(out=x[:], in0=x[:], in1=row("L1_xattn_bo").unsqueeze(1).to_broadcast([P, TT, D]), op=ALU.add)

        @block.tensor
        def _(pe):
            pe.sem_inc(value_mm, 2)
            pe.sem_inc(p_turned, 2)
            pe.sem_inc(score_mm, PB)
            pe.wait_ge(h_ready, 1)
            for k in range(KT):
                for t in range(TT):
                    last = nc.tensor.transpose(ps[:, k, t * P:(t + 1) * P], h[:, t, k * P:(k + 1) * P], ident[:])
                last.then_inc(h_turned, 1)
            pe.wait_ge(hT_ready, KT)
            pe.wait_ge(w_loaded, 64)
            for g in range(KT):
                for k in range(KT):
                    last = nc.tensor.matmul(ps[:, 2 + g, :], wq[:, k, g * P:(g + 1) * P], hT[:, k, :],
                                            start=k == 0, stop=k == KT - 1)
                last.then_inc(q_mm, 1)

            def item(b, a, k):
                pe.wait_ge(item_read, ITEMS * b + k)
                if 1 <= k <= 8:
                    pe.wait_ge(item_rest, 8 * b + k)
                if k < 4:
                    if k == 0:
                        pe.wait_ge(ctx_loaded, 16 * (b + 1))
                    for t in range(4):
                        last = nc.tensor.transpose(item_ps[:, t * P:(t + 1) * P],
                                                   raw[a][:, 4 * (k // 2) + t, (k % 2) * P:(k % 2 + 1) * P], ident[:])
                elif k < 8:
                    g, half_ = k % 2, (k - 4) // 2
                    for kk in range(KT):
                        at, w_at = (slice(None), kk, slice(half_ * 512, half_ * 512 + 512)), (slice(None), kk, slice(g * P, (g + 1) * P))
                        last = split_matmul(nc, item_ps, (wk_hi[w_at], wk_lo[w_at]), (cT_hi[at], cT_lo[at]), kk == 0, kk == KT - 1)
                else:
                    for t in range(2):
                        st = 2 * (k - 8) + t
                        for kk in range(KT):
                            at, w_at = (slice(None), kk, slice(st * P, (st + 1) * P)), (slice(None), kk)
                            last = split_matmul(nc, item_ps[:, t * D:(t + 1) * D], (cT_hi[at], cT_lo[at]), (wv_hi[w_at], wv_lo[w_at]),
                                                kk == 0, kk == KT - 1)
                last.then_inc(item_mm, 1)

            def score(n, a, s):
                g, j = s // 4, s % 4
                queries = [blk[a][:, g, 2 * j:2 * j + 2, :].rearrange("p a n -> p (a n)") for blk in (qblk_hi, qblk_lo)]
                for c in range(2):
                    at = (slice(None), g, slice(c * 512, (c + 1) * 512))
                    last = split_matmul(nc, score_ps[s % 2][:, c, :], queries, (kT_hi[a][at], kT_lo[a][at]), True, True)
                last.then_inc(score_mm, 1)

            pe.wait_ge(w_split, 2)
            for k in range(ITEMS):
                item(0, 0, k)
            pe.wait_ge(qblk_ready, 1)
            pe.wait_ge(item_read, ITEMS)
            score(0, 0, 0)
            score(1, 0, 1)

            def turn(i, last):
                for a in range(2):
                    b = 2 * i + a
                    for s in range(PB):
                        n = b * PB + s
                        items = not (last and a == 1) and s < 6
                        if not (last and a == 1 and s >= PB - 2):
                            pe.wait_ge(exp_done, n + 1)
                            if s == PB - 2:
                                pe.wait_ge(qblk_ready, b + 2)
                                pe.wait_ge(item_read, ITEMS * (b + 1) + 8)
                            score(n + 2, a if s < PB - 2 else (a + 1) % 2, (s + 2) % PB)
                        if items:
                            item(b + 1, (a + 1) % 2, 2 * s)
                        pe.wait_ge(p_split, n + 2)
                        for hf in range(2):
                            pe.wait_ge(pT_dve if hf else pT_act, n + 1)
                            for t in range(4):
                                for part_ in (p_hi, p_lo):
                                    mm = nc.tensor.matmul(ps[:, 4 + hf, t * P:(t + 1) * P], part_[s % 2][:, (4 * hf + t) * P:(4 * hf + t + 1) * P],
                                                          small_ident[:], start=part_ is p_hi, stop=part_ is p_lo)
                            mm.then_inc(p_turned, 1)
                        if s % 4 == 3:
                            g = s // 4
                            pe.wait_ge(item_read, ITEMS * (b + 1))
                            pe.wait_ge(pT_act, n + 2)
                            pe.wait_ge(pT_dve, n + 2)
                            pe.wait_ge(outT_ready, 4 * i + 2 * a + g + 1)
                            for st in range(ST):
                                for j in range(4):
                                    pair = 4 * g + j
                                    mm = nc.tensor.matmul(ps[32 * j:32 * j + 32, 6, g * P:(g + 1) * P],
                                                          v[a][:, st, pair * 2 * HD:(pair + 1) * 2 * HD], pT[g][:, j, st, :],
                                                          start=st == 0, stop=st == ST - 1)
                            mm.then_inc(value_mm, 1)
                        if items:
                            item(b + 1, (a + 1) % 2, 2 * s + 1)

            with pe.Fori(0, TT - 1) as i:
                turn(i, False)
            turn(TT - 1, True)
            pe.wait_ge(outT_ready, 2 * B + 1)
            for t in range(TT):
                for g in range(KT):
                    mm = nc.tensor.matmul(ps[:, t // 2, (t % 2) * D:(t % 2 + 1) * D], outT[:, g, t * P:(t + 1) * P], wo[:, g, :],
                                          start=g == 0, stop=g == KT - 1)
                mm.then_inc(proj_mm, 1)


def spiral_1(own, nc, A, sb, sem, x, cols, rows, ident, head_mask, band, ps, col, row, finished):
    HT = H1 // P
    TWO_PI = 2 * np.pi
    PI_HI = float(np.float32(TWO_PI))
    PI_LO = float(TWO_PI - np.float64(np.float32(TWO_PI)))
    PI_MAX = float(np.nextafter(np.float32(np.pi), np.float32(0)))
    h0 = sb("sp_h0", [P, TT, D], own)
    h = sb("sp_h", [P, TT, D], own)
    hT = sb("sp_hT", [P, KT, B, N], own)
    y = sb("sp_y", [P, KT, B, N], own)
    w1 = sb("sp_w1", [P, KT, H1], own)
    w2 = sb("sp_w2", [P, HT, D], own)
    act_T = sb("sp_act", [P, HT, T], own)
    turns = sb("sp_turns", [P, KT], own)
    whole = sb("sp_whole", [P, KT], own, I32)
    angle = sb("sp_angle", [P, KT], own)
    quarter = sb("sp_quarter", [P, KT], own)
    gamma = sb("sp_gamma", [P, KT], own)
    c_re = sb("sp_c_re", [P, KT], own)
    c_im = sb("sp_c_im", [P, KT], own)
    re = sb("sp_re", [P, B + 1, KT], own)
    im = sb("sp_im", [P, B + 1, KT], own)
    tmp = sb("sp_tmp", [P, 2, KT], own)
    past = sb("sp_past", [P, KT, B], own)
    stats = sb("sp_stats", [P, TT, 6], own)
    mv = sb("sp_mv", [P, TT, 2], own)
    var = sb("sp_var", [P, TT], own)
    rstd = sb("sp_rstd", [P, TT], own)
    half = sb("sp_half", [P, TT], own)

    w_loaded = sem("sp_w_loaded"); pool_step = sem("sp_pool_step"); dve_step = sem("sp_dve_step")
    act_step = sem("sp_act_step"); angle_ready = sem("sp_angle_ready"); c_parts = sem("sp_c_parts")
    filter_ready = sem("sp_filter_ready"); var_ready = sem("sp_var"); rstd_ready = sem("sp_rstd")
    h_ready = sem("sp_h_ready"); h_turned = sem("sp_h_turned"); hT_ready = sem("sp_hT_ready")
    y_ready = sem("sp_y_ready"); y_turned = sem("sp_y_turned")
    up_mm = sem("sp_up_mm"); silu_done = sem("sp_silu"); down_mm = sem("sp_down_mm")

    with nc.Block() as block:
        @block.sync
        def _(sp):
            sp.dma_start(w1[:], A["L1_attn_w1"].rearrange("(k p) n -> p k n", p=P)).then_inc(w_loaded, 16)
            sp.dma_start(w2[:], A["L1_attn_w2"].rearrange("(k p) n -> p k n", p=P)).then_inc(w_loaded, 16)

        @block.gpsimd
        def _(pool):
            for s in finished:
                pool.sem_clear(s)
            step = Chain(pool, pool_step)
            step.link(nc.gpsimd.memset(half[:], -0.5))
            for n in range(2):
                pool.wait_ge(var_ready, n + 1)
                nc.gpsimd.tensor_tensor(out=rstd[:], in0=var[:], in1=half[:], op=ALU.pow).then_inc(rstd_ready, 1)
            pool.wait_ge(rstd_ready, 2)
            pool.wait_ge(c_parts, 1)
            step.link(nc.gpsimd.memset(re[:, 0, :], 1.0))
            step.link(nc.gpsimd.memset(im[:, 0, :], 0.0))

            def product(out, a, b, op=ALU.mult):
                step.link(nc.gpsimd.tensor_tensor(out=out, in0=a, in1=b, op=op))

            product(c_re[:], c_re[:], gamma[:])
            product(c_im[:], c_im[:], gamma[:])
            for n in range(1, B + 1):
                product(tmp[:, 0], re[:, n - 1], c_re[:])
                product(tmp[:, 1], im[:, n - 1], c_im[:])
                product(re[:, n], tmp[:, 0], tmp[:, 1], ALU.subtract)
                if n < B:
                    product(tmp[:, 0], re[:, n - 1], c_im[:])
                    product(tmp[:, 1], im[:, n - 1], c_re[:])
                    product(im[:, n], tmp[:, 0], tmp[:, 1], ALU.add)
            at = COL_AT["L1_attn_last_conv_init"]
            product(past[:], re[:, 1:B + 1].rearrange("p n k -> p k n"), cols[:, at:at + KT].unsqueeze(2).to_broadcast([P, KT, B]))
            pool.sem_inc(filter_ready, 1)
            pool.wait_ge(var_ready, 3)
            nc.gpsimd.tensor_tensor(out=rstd[:], in0=var[:], in1=half[:], op=ALU.pow).then_inc(rstd_ready, 1)

        @block.scalar
        def _(act):
            step = Chain(act, act_step)
            at = COL_AT["L1_attn_lmlg"]
            step.link(nc.scalar.activation(gamma[:], cols[:, at:at + KT], ACT.Exp))
            step.link(nc.scalar.activation(gamma[:], gamma[:], ACT.Exp, scale=-1.0))
            act.wait_ge(angle_ready, 1)
            step.link(nc.scalar.activation(c_im[:], angle[:], ACT.Sin))
            nc.scalar.activation(c_re[:], quarter[:], ACT.Sin).then_inc(c_parts, 1)

            def affine(n):
                for k in range(KT):
                    act.wait_ge(h_turned, KT * n + k + 1)
                    nc.scalar.activation(hT[:, k].rearrange("p b n -> p (b n)"), ps[:, k, :], ACT.Identity,
                                         bias=col("L1_attn_ln_b", k), scale=col("L1_attn_ln_w", k)).then_inc(hT_ready, 1)

            affine(0)
            affine(1)
            for f in range(HT):
                act.wait_ge(up_mm, f + 1)
                nc.scalar.activation(act_T[:, f, :], ps[:, 2 + f % 2, :], ACT.Silu, bias=col("L1_attn_b1", f)).then_inc(silu_done, 1)

        @block.vector
        def _(dve):
            step = Chain(dve, dve_step)
            at = COL_AT["L1_attn_theta"]
            theta = cols[:, at:at + KT]
            step.link(nc.vector.tensor_scalar(whole[:], theta, 1.0 / TWO_PI, None, ALU.mult))
            step.link(nc.vector.tensor_copy(turns[:], whole[:]))
            step.link(nc.vector.scalar_tensor_tensor(out=angle[:], in0=turns[:], scalar=-PI_HI, in1=theta, op0=ALU.mult, op1=ALU.add))
            step.link(nc.vector.scalar_tensor_tensor(out=angle[:], in0=turns[:], scalar=-PI_LO, in1=angle[:], op0=ALU.mult, op1=ALU.add))
            step.link(nc.vector.tensor_scalar(angle[:], angle[:], PI_MAX, -PI_MAX, ALU.min, ALU.max))
            step.link(nc.vector.scalar_tensor_tensor(out=quarter[:], in0=angle[:], scalar=-1.0, in1=angle[:], op0=ALU.mult, op1=ALU.max))
            nc.vector.tensor_scalar(quarter[:], quarter[:], -1.0, float(np.pi / 2), ALU.mult, ALU.add).then_inc(angle_ready, 1)

            norm_stats(nc, step, x, stats, mv, var, TT, var_ready)
            dve.wait_ge(rstd_ready, 1)
            step.link(norm_apply(nc, h0, x, mv, rstd, TT))
            norm_stats(nc, step, h0, stats, mv, var, TT, var_ready)
            dve.wait_ge(rstd_ready, 2)
            norm_apply(nc, h, h0, mv, rstd, TT).then_inc(h_ready, 1)

            dve.wait_ge(filter_ready, 1)
            dve.wait_ge(hT_ready, KT)
            step.link(nc.vector.tensor_tensor(out=y[:].rearrange("p k b n -> p (k b) n"), in0=hT[:].rearrange("p k b n -> p (k b) n"),
                                              in1=past[:].rearrange("p k b -> p (k b)").unsqueeze(2).to_broadcast([P, KT * B, N]), op=ALU.add))
            for n in range(1, B):
                for k in range(KT):
                    last = nc.vector.scalar_tensor_tensor(out=y[:, k, n:], in0=hT[:, k, 0:B - n], scalar=re[:, n, k:k + 1], in1=y[:, k, n:],
                                                          op0=ALU.mult, op1=ALU.add)
                step.link(last)
            nc.vector.tensor_tensor(out=y[:], in0=y[:], in1=hT[:], op=ALU.mult).then_inc(y_ready, 1)
            for t in range(TT):
                dve.wait_ge(y_turned, 2 * (t // 2 + 1))
                last = nc.vector.tensor_tensor(out=h0[:, t, :], in0=ps[:, 2 + t // 2, (t % 2) * D:(t % 2 + 1) * D], in1=h0[:, t, :], op=ALU.add)
            step.link(last)
            norm_stats(nc, step, h0, stats, mv, var, TT, var_ready)
            dve.wait_ge(rstd_ready, 3)
            norm_apply(nc, h, h0, mv, rstd, TT).then_inc(h_ready, 1)
            dve.wait_ge(h_ready, 2)
            step.link(nc.vector.tensor_tensor(out=h0[:], in0=h0[:], in1=row("L1_attn_b2").unsqueeze(1).to_broadcast([P, TT, D]), op=ALU.add))
            step.link(nc.vector.tensor_tensor(out=x[:], in0=x[:], in1=h0[:], op=ALU.add))
            for t in range(TT):
                dve.wait_ge(down_mm, t + 1)
                nc.vector.tensor_tensor(out=x[:, t, :], in0=ps[:, 4 + t, 0:D], in1=x[:, t, :], op=ALU.add)

        @block.tensor
        def _(pe):
            def turn_h(n):
                pe.wait_ge(h_ready, n + 1)
                for k in range(KT):
                    for t in range(TT):
                        last = nc.tensor.transpose(ps[:, k, t * P:(t + 1) * P], h[:, t, k * P:(k + 1) * P], ident[:])
                    last.then_inc(h_turned, 1)

            turn_h(0)
            pe.wait_ge(y_ready, 1)
            for t in range(TT):
                for k in range(KT):
                    last = nc.tensor.transpose(ps[:, 2 + t // 2, (t % 2) * D + k * P:(t % 2) * D + (k + 1) * P],
                                               y[:, k, 2 * t:2 * t + 2, :].rearrange("p b n -> p (b n)"), ident[:])
                last.then_inc(y_turned, 1)
            turn_h(1)
            pe.wait_ge(hT_ready, 2 * KT)
            pe.wait_ge(w_loaded, 32)
            for f in range(HT):
                if f >= 2:
                    pe.wait_ge(silu_done, f - 1)
                for k in range(KT):
                    last = nc.tensor.matmul(ps[:, 2 + f % 2, :], w1[:, k, f * P:(f + 1) * P], hT[:, k].rearrange("p b n -> p (b n)"),
                                            start=k == 0, stop=k == KT - 1)
                last.then_inc(up_mm, 1)
            for t in range(TT):
                for f in range(HT):
                    if t == 0:
                        pe.wait_ge(silu_done, f + 1)
                    last = nc.tensor.matmul(ps[:, 4 + t, 0:D], act_T[:, f, t * P:(t + 1) * P], w2[:, f, :],
                                            start=f == 0, stop=f == HT - 1)
                last.then_inc(down_mm, 1)


def experts_1(own, nc, A, sb, sem, x, cols, rows, ident, head_mask, band, ps, col, row, finished):
    HT = H1 // P
    h = sb("e1_h", [P, TT, D], own)
    hT = sb("e1_hT", [P, KT, T], own)
    hT_hi = sb("e1_hT_hi", [P, KT, T], own, F32R)
    hT_lo = sb("e1_hT_lo", [P, KT, T], own, F32R)
    wgate = sb("e1_wgate", [P, KT, E], own)
    wshared = sb("e1_wshared", [P, KT, D], own)
    w1 = sb("e1_w1", [P, KT, H1], own)
    w2 = sb("e1_w2", [P, HT, D], own)
    w1_hi = [sb(f"e1_w1_hi{i}", [P, KT, H1], own, F32R) for i in range(2)]
    w2_hi = [sb(f"e1_w2_hi{i}", [P, HT, D], own, F32R) for i in range(2)]
    w1_lo = [sb(f"e1_w1_lo{i}", [P, KT, H1], own, F32R) for i in range(2)]
    w2_lo = [sb(f"e1_w2_lo{i}", [P, HT, D], own, F32R) for i in range(2)]
    b2 = sb("e1_b2", [E, D], own)
    gates = sb("e1_gates", [P, TT, E], own)
    chosen = sb("e1_chosen", [P, TT, E], own)
    chosenT = sb("e1_chosenT", [E, T], own)
    rank = sb("e1_rank", [P, E], own)
    work = sb("e1_work", [P, 3, TT, E], own)
    best = sb("e1_best", [P, 3, TT], own)
    gelu = [sb(f"e1_gelu{i}", [P, T], own) for i in range(2)]
    act_hi = [sb(f"e1_act_hi{i}", [P, HT, T], own, F32R) for i in range(2)]
    act_lo = [sb(f"e1_act_lo{i}", [P, HT, T], own, F32R) for i in range(2)]
    acc = sb("e1_acc", [P, TT, D], own)
    stats = sb("e1_stats", [P, TT, 6], own)
    mv = sb("e1_mv", [P, TT, 2], own)
    var = sb("e1_var", [P, TT], own)
    rstd = sb("e1_rstd", [P, TT], own)
    half = sb("e1_half", [P, TT], own)
    top = sb("e1_top", [P, TT], own)
    total = sb("e1_total", [P, TT], own)

    act_passed = sem("e1_act_passed")
    small_loaded = sem("e1_small"); w1_loaded = sem("e1_w1_loaded")
    w2_loaded = sem("e1_w2_loaded")
    pool_step = sem("e1_pool_step"); dve_step = sem("e1_dve_step"); var_ready = sem("e1_var")
    rstd_ready = sem("e1_rstd"); h_ready = sem("e1_h_ready"); h_turned = sem("e1_h_turned"); hT_ready = sem("e1_hT_ready")
    gate_mm = sem("e1_gate_mm"); gate_arg = sem("e1_gate_arg"); gate_exp = sem("e1_gate_exp")
    chosen_ready = sem("e1_chosen_ready"); chosen_turned = sem("e1_chosen_turned"); chosenT_ready = sem("e1_chosenT_ready")
    shared_mm = sem("e1_shared_mm"); shared_arg = sem("e1_shared_arg"); shared_gelu = sem("e1_shared_gelu")
    bias_mm = sem("e1_bias_mm"); hT_split = sem("e1_hT_split")
    w_rounded = sem("e1_w_rounded"); w1_split = sem("e1_w1_split"); w2_split = sem("e1_w2_split")
    act_rounded = sem("e1_act_rounded"); act_split = sem("e1_act_split")
    up_mm = sem("e1_up_mm"); gelu_done = sem("e1_gelu"); down_mm = sem("e1_down_mm"); acc_added = sem("e1_acc_added")

    RING = 2
    PARTS = 4

    def weight_part(w, j):
        return w.rearrange("p k n -> p (k n)")[:, j * 512:(j + 1) * 512]

    with nc.Block() as block:
        @block.sync
        def _(sp):
            sp.dma_start(wgate[:], A["L1_ffn_gate_W"].rearrange("(k p) n -> p k n", p=P)).then_inc(small_loaded, 16)
            sp.dma_start(b2[:], A["L1_ffn_b2"]).then_inc(small_loaded, 16)
            sp.dma_start(wshared[:], A["L1_ffn_shared_W"].rearrange("(k p) n -> p k n", p=P)).then_inc(small_loaded, 16)
            w1_d = A["L1_ffn_W1"].rearrange("e (k p) n -> (e k) p n", p=P)
            w2_d = A["L1_ffn_W2"].rearrange("e (k p) n -> (e k) p n", p=P)

            sp.dma_start(w1[:], w1_d[0:KT].rearrange("k p n -> p k n")).then_inc(w1_loaded, 16)
            sp.dma_start(w2[:], w2_d[0:HT].rearrange("k p n -> p k n")).then_inc(w2_loaded, 16)
            with sp.Fori(1, E) as e:
                sp.wait_ge(w1_split, e * PARTS)
                sp.dma_start(w1[:], w1_d[bass.ds(e * KT, KT)].rearrange("k p n -> p k n")).then_inc(w1_loaded, 16)
                sp.wait_ge(w2_split, e * PARTS)
                sp.dma_start(w2[:], w2_d[bass.ds(e * HT, HT)].rearrange("k p n -> p k n")).then_inc(w2_loaded, 16)

        @block.gpsimd
        def _(pool):
            for s in finished:
                pool.sem_clear(s)
            step = Chain(pool, pool_step)
            step.link(nc.gpsimd.memset(half[:], -0.5))
            pool.wait_ge(var_ready, 1)
            nc.gpsimd.tensor_tensor(out=rstd[:], in0=var[:], in1=half[:], op=ALU.pow).then_inc(rstd_ready, 1)

            def weight_rests(e, a):
                for m, (lo, hi, w, split) in enumerate(((w1_lo, w1_hi, w1, w1_split), (w2_lo, w2_hi, w2, w2_split))):
                    for j in range(PARTS):
                        pool.wait_ge(w_rounded, (2 * e + m) * PARTS + j + 1)
                        nc.gpsimd.tensor_tensor(out=weight_part(lo[a][:], j), in0=weight_part(w[:], j),
                                                in1=weight_part(hi[a][:].bitcast(F32), j), op=ALU.subtract).then_inc(split, 1)

            weight_rests(0, 0)
            with pool.Fori(0, E // 2 - 1) as i:
                for a in range(2):
                    weight_rests(2 * i + a + 1, 1 - a)
            weight_rests(E - 1, 1)
            pool.wait_ge(var_ready, 2)
            nc.gpsimd.tensor_tensor(out=rstd[:], in0=var[:], in1=half[:], op=ALU.pow).then_inc(rstd_ready, 1)

        @block.scalar
        def _(act):
            act.sem_inc(gelu_done, RING)
            for k in range(KT):
                act.wait_ge(h_turned, k + 1)
                nc.scalar.copy(hT[:, k, :], ps[:, 6 + k, :]).then_inc(hT_ready, 1)
            for w_hi, w, loaded in ((w1_hi, w1, w1_loaded), (w2_hi, w2, w2_loaded)):
                act.wait_ge(loaded, 16)
                for j in range(PARTS):
                    nc.scalar.copy(weight_part(w_hi[0][:], j), weight_part(w[:], j)).then_inc(w_rounded, 1)
            act.wait_ge(gate_arg, 1)
            nc.scalar.activation(gates[:], gates[:], ACT.Exp).then_inc(gate_exp, 1)
            act.wait_ge(chosen_turned, 1)
            nc.scalar.copy(chosenT[:], ps[0:E, 7, :]).then_inc(chosenT_ready, 1)
            act.wait_ge(shared_arg, 1)
            nc.scalar.activation(acc[:], acc[:], ACT.Gelu).then_inc(shared_gelu, 1)

            def turn(i, last):
                for a in range(2):
                    e = 2 * i + a
                    more = not (last and a == 1)
                    for f in range(HT):
                        n = e * HT + f
                        act.wait_ge(up_mm, n + 1)
                        wait_alone(act, act_passed, act_split, n + 1)
                        nc.scalar.activation(gelu[f % 2][:], ps[:, f % 2, :], ACT.Gelu,
                                             bias=cols[:, bass.ds(n + COL_AT["L1_ffn_b1"], 1)]).then_inc(gelu_done, 1)
                        if more and f < PARTS:
                            if f == 0:
                                act.wait_ge(w1_loaded, 16 * (e + 2))
                            nc.scalar.copy(weight_part(w1_hi[1 - a][:], f), weight_part(w1[:], f)).then_inc(w_rounded, 1)
                    if more:
                        act.wait_ge(w2_loaded, 16 * (e + 2))
                        act.wait_ge(down_mm, (e + 2) * TT)
                        for j in range(PARTS):
                            nc.scalar.copy(weight_part(w2_hi[1 - a][:], j), weight_part(w2[:], j)).then_inc(w_rounded, 1)

            with act.Fori(0, E // 2 - 1) as i:
                turn(i, False)
            turn(E // 2 - 1, True)

        @block.vector
        def _(dve):
            dve.sem_inc(acc_added, RING)
            dve.sem_inc(act_split, RING)
            step = Chain(dve, dve_step)
            for e in range(E):
                last = nc.vector.memset(rank[:, e:e + 1], float(E - e))
            step.link(last)
            norm_stats(nc, step, x, stats, mv, var, TT, var_ready)
            dve.wait_ge(rstd_ready, 1)
            norm_apply(nc, h, x, mv, rstd, TT).then_inc(h_ready, 1)
            for k in range(KT):
                dve.wait_ge(hT_ready, k + 1)
                step.link(nc.vector.tensor_copy(hT_hi[:, k, :], hT[:, k, :]))
                nc.vector.tensor_tensor(out=hT_lo[:, k, :], in0=hT[:, k, :], in1=hT_hi[:, k, :].bitcast(F32), op=ALU.subtract).then_inc(hT_split, 1)

            def split_activations(e, a, fs):
                dve.wait_ge(down_mm, (e + 1) * TT)
                for f in fs:
                    n = e * HT + f
                    dve.wait_ge(gelu_done, n + 1 + RING)
                    nc.vector.tensor_copy(act_hi[a][:, f, :], gelu[f % 2][:]).then_inc(act_rounded, 1)
                    dve.wait_ge(act_rounded, n + 1)
                    nc.vector.tensor_tensor(out=act_lo[a][:, f, :], in0=gelu[f % 2][:], in1=act_hi[a][:, f, :].bitcast(F32),
                                            op=ALU.subtract).then_inc(act_split, 1)

            dve.wait_ge(gate_mm, 1)
            step.link(nc.vector.tensor_copy(gates[:], ps[:, 6, 0:TT * E].rearrange("p (t e) -> p t e", t=TT)))
            softmax_rows(nc, step, gates[:], E, top[:]).then_inc(gate_arg, 1)
            dve.wait_ge(shared_mm, 1)
            nc.vector.tensor_tensor(out=acc[:].rearrange("p (a b) d -> p a b d", a=2), in0=ps[:, 2:4, :].rearrange("p a (b d) -> p a b d", b=2),
                                    in1=row("L1_ffn_shared_b").unsqueeze(1).unsqueeze(1).to_broadcast([P, 2, 2, D]), op=ALU.add).then_inc(shared_arg, 1)
            dve.wait_ge(gate_exp, 1)
            step.link(normalise_rows(nc, step, gates[:], total[:]))
            top_two(nc, step, gates[:], rank[:], chosen[:], work, best).then_inc(chosen_ready, 1)
            dve.wait_ge(shared_gelu, 1)
            dve.wait_ge(bias_mm, 1)
            for t in range(TT):
                last = nc.vector.scalar_tensor_tensor(out=acc[:, t, :], in0=acc[:, t, :], scalar=0.5,
                                                      in1=ps[:, 6 + t // 2, (t % 2) * D:(t % 2 + 1) * D], op0=ALU.mult, op1=ALU.add)
            step.link(last)

            def add_experts(e, tiles):
                for t in tiles:
                    n = e * TT + t
                    dve.wait_ge(down_mm, n + 1 + 2 * TT)
                    nc.vector.scalar_tensor_tensor(out=acc[:, t, :], in0=ps[:, 4 + t % 2, 0:D],
                                                   scalar=chosen[:].rearrange("p t e -> p (t e)")[:, bass.ds(t * E + e, 1)],
                                                   in1=acc[:, t, :], op0=ALU.mult, op1=ALU.add).then_inc(acc_added, 1)

            with dve.Fori(0, E // 2) as i:
                for a in range(2):
                    e = 2 * i + a
                    split_activations(e, a, range(HT))
                    add_experts(e, range(TT))
            dve.wait_ge(acc_added, E * TT + RING)
            norm_stats(nc, step, acc, stats, mv, var, TT, var_ready)
            dve.wait_ge(rstd_ready, 2)
            step.link(norm_apply(nc, acc, acc, mv, rstd, TT))
            step.link(nc.vector.tensor_tensor(out=acc[:], in0=acc[:], in1=row("L1_ffn_gamma").unsqueeze(1).to_broadcast([P, TT, D]), op=ALU.mult))
            step.link(nc.vector.tensor_tensor(out=x[:], in0=x[:], in1=row("L1_ffn_beta").unsqueeze(1).to_broadcast([P, TT, D]), op=ALU.add))
            nc.vector.tensor_tensor(out=x[:], in0=x[:], in1=acc[:], op=ALU.add)

        @block.tensor
        def _(pe):
            pe.sem_inc(down_mm, 2 * TT)
            pe.wait_ge(h_ready, 1)
            for k in range(KT):
                for t in range(TT):
                    last = nc.tensor.transpose(ps[:, 6 + k, t * P:(t + 1) * P], h[:, t, k * P:(k + 1) * P], ident[:])
                last.then_inc(h_turned, 1)
            pe.wait_ge(hT_ready, KT)
            pe.wait_ge(small_loaded, 48)
            for t in range(TT):
                for k in range(KT):
                    last = nc.tensor.matmul(ps[:, 6, t * E:(t + 1) * E], hT[:, k, t * P:(t + 1) * P], wgate[:, k, :],
                                            start=k == 0, stop=k == KT - 1)
            last.then_inc(gate_mm, 1)
            for t in range(TT):
                for k in range(KT):
                    last = nc.tensor.matmul(ps[:, 2 + t // 2, (t % 2) * D:(t % 2 + 1) * D], hT[:, k, t * P:(t + 1) * P], wshared[:, k, :],
                                            start=k == 0, stop=k == KT - 1)
            last.then_inc(shared_mm, 1)

            def up(i, a, fs):
                for f in fs:
                    if f == 0:
                        pe.wait_ge(w1_split, (2 * i + a + 1) * PARTS)
                    pe.wait_ge(gelu_done, (2 * i + a) * HT + f + 1)
                    for k in range(KT):
                        at = (slice(None), k, slice(f * P, (f + 1) * P))
                        last = split_matmul(nc, ps[:, f % 2, :], (w1_hi[a][at], w1_lo[a][at]), (hT_hi[:, k, :], hT_lo[:, k, :]),
                                            k == 0, k == KT - 1)
                    last.then_inc(up_mm, 1)

            def down(i, a):
                e = 2 * i + a
                pe.wait_ge(w2_split, (e + 1) * PARTS)
                for t in range(TT):
                    pe.wait_ge(acc_added, e * TT + t + 1)
                    for f in range(HT):
                        if t == 0:
                            pe.wait_ge(act_split, e * HT + f + 1 + RING)
                        at = (slice(None), f, slice(t * P, (t + 1) * P))
                        last = split_matmul(nc, ps[:, 4 + t % 2, 0:D], (act_hi[a][at], act_lo[a][at]),
                                            (w2_hi[a][:, f, :], w2_lo[a][:, f, :]), f == 0, f == HT - 1)
                    last.then_inc(down_mm, 1)

            def gates_turned():
                pe.wait_ge(chosen_ready, 1)
                for t in range(TT):
                    last = nc.tensor.matmul(ps[0:E, 7, t * P:(t + 1) * P], chosen[:, t, :], ident[:], start=True, stop=True)
                last.then_inc(chosen_turned, 1)
                pe.wait_ge(chosenT_ready, 1)
                for t in range(TT):
                    last = nc.tensor.matmul(ps[:, 6 + t // 2, (t % 2) * D:(t % 2 + 1) * D], chosenT[:, t * P:(t + 1) * P], b2[:],
                                            start=True, stop=True)
                last.then_inc(bias_mm, 1)

            pe.wait_ge(hT_split, KT)
            up(0, 0, range(2))
            gates_turned()
            up(0, 0, range(2, HT))
            down(0, 0)
            up(0, 1, range(HT))
            down(0, 1)
            with pe.Fori(1, E // 2) as i:
                for a in range(2):
                    up(i, a, range(HT))
                    down(i, a)


def kernel(**inputs):
    import numpy as _np
    import concourse.bacc as _bacc
    from concourse import mybir as _mybir
    from concourse.bass_utils import run_bass_kernel_spmd as _run

    a = {n: _np.asarray(v) for n, v in inputs.items()}

    def pair_columns(w):
        return w.reshape(D, NPAIR, 2, 2, DH // 4 * 2).transpose(0, 1, 3, 2, 4).reshape(D, H * DH)

    laid = {"x": a["x"], "ctx_1024": a["ctx_1024"],
            "cosT": _np.tile(a["L0_xattn_cos"].T, (4, 1)), "sinT": _np.tile(a["L0_xattn_sin"].T, (4, 1)),
            "wq_pairs": pair_columns(a["L0_xattn_Wq"]), "wk_pairs": pair_columns(a["L0_xattn_Wkv"][:, :H * DH]),
            "wv": a["L0_xattn_Wkv"][:, H * DH:],
            "cols": _np.concatenate([a[n].reshape(-1, P) for n in COLS]).T,
            "rows": _np.concatenate([a[n] for n in ROWS]).reshape(1, NROW),
            "L0_ffn_b1": a["L0_ffn_b1"].reshape(1, E * H0)}
    for name in ("L1_xattn_Wq", "L1_xattn_Wk", "L1_xattn_Wv", "L1_xattn_Wo"):
        laid[name + "T"] = a[name].T
    for name in ("L0_xattn_Wo", "L0_attn_Wqk", "L0_attn_Wgate", "L0_attn_Wproj", "L0_ffn_gate_w", "L0_ffn_w1",
                 "L0_ffn_w2", "L0_ffn_b2", "L1_attn_w1", "L1_attn_w2", "L1_ffn_W1", "L1_ffn_W2", "L1_ffn_b2",
                 "L1_ffn_gate_W", "L1_ffn_shared_W"):
        laid[name] = a[name]

    nc = _bacc.Bacc("TRN2", target_bir_lowering=False, num_devices=1)
    arrays, args = {}, {}
    for name, v in laid.items():
        v = _np.ascontiguousarray(v)
        arrays[f"in_{name}"] = v
        args[name] = nc.dram_tensor(f"in_{name}", v.shape, _mybir.dt.from_np(v.dtype), kind="ExternalInput").ap()
    args["out"] = nc.dram_tensor("out_x", (B, N, D), _mybir.dt.from_np(_np.dtype("float32")), kind="ExternalOutput").ap()
    program(nc, args)
    r = _run(nc, [arrays], core_ids=[0])
    return r.results[0]["out_x"]
```

```python
from contextlib import ExitStack

import numpy as np

import concourse.bass as bass
from concourse import mybir

P = 128
B, N, D, S, H = 8, 64, 256, 1024, 16
T = B * N
TT = T // P
KT = D // P
ST = S // P
EPS = 1e-5
DH = 64
NPAIR = H // 2
E = 8
H0 = 512
H1 = 1024
NEG = -1e30

F32 = mybir.dt.float32
F16 = mybir.dt.float16
F32R = mybir.dt.float32r
I32 = mybir.dt.int32
ALU = mybir.AluOpType
ACT = mybir.ActivationFunctionType
AX = mybir.AxisListType

COLS = {"L0_xattn_ln_lat_g": 2, "L0_xattn_ln_lat_b": 2, "L0_xattn_ln_ctx_g": 2, "L0_xattn_ln_ctx_b": 2,
        "L0_attn_bqk": 4, "L0_ffn_ln1_g": 32, "L0_ffn_ln1_b": 32, "L1_xattn_bq": 2, "L1_xattn_bk": 2,
        "L1_xattn_bv": 2, "L1_attn_lmlg": 2, "L1_attn_theta": 2, "L1_attn_last_conv_init": 2,
        "L1_attn_ln_w": 2, "L1_attn_ln_b": 2, "L1_attn_b1": 8, "L1_ffn_b1": 64}
ROWS = {"L0_xattn_bo": 256, "L0_attn_bqk": 512, "L0_attn_bgate": 16, "L0_attn_bproj": 256,
        "L0_ffn_ln_g": 256, "L0_ffn_ln_b": 256, "L1_xattn_bo": 256, "L1_attn_b2": 256,
        "L1_ffn_shared_b": 256, "L1_ffn_gamma": 256, "L1_ffn_beta": 256}


def offsets(widths):
    at, out = 0, {}
    for name, n in widths.items():
        out[name] = at
        at += n
    return out, at


COL_AT, NCOL = offsets(COLS)
ROW_AT, NROW = offsets(ROWS)


class Chain:

    def __init__(self, eng, sem):
        self.eng, self.sem, self.n, self.base = eng, sem, 0, 0

    def link(self, ins):
        self.n += 1
        ins.then_inc(self.sem, 1)
        self.eng.wait_ge(self.sem, self.base + self.n)

    def link_alone(self, ins, passed):
        self.n += 1
        ins.then_inc(self.sem, 1)
        wait_alone(self.eng, passed, self.sem, self.base + self.n)


def wait_alone(eng, passed, sem, value):
    eng.wait_ge(sem, value)
    eng.sem_inc(passed, 1)


def load_ahead(sp, ahead, loaded):
    for dst, src in ahead["loads"]:
        sp.dma_start(dst, src).then_inc(loaded, 16)
    sp.wait_ge(loaded, 16 * len(ahead["loads"]))


def program(nc, A):
    ctx = ExitStack()
    with ctx:
        def sb(name, shape, stack=ctx, dt=F32):
            return stack.enter_context(nc.sbuf_tensor(name, shape, dt))

        in_stage, finished = [], []

        def sem(name):
            in_stage.append(nc.alloc_semaphore(name))
            return in_stage[-1]

        x = sb("x", [P, TT, D])
        cols = sb("cols", [P, NCOL])
        rows = sb("rows", [P, NROW])
        ident = sb("ident", [P, P])
        head_mask = sb("head_mask", [P, 8])
        band = sb("band", [P, NPAIR, N])
        ps = ctx.enter_context(nc.psum_tensor("ps", [P, 8, 512], F32))

        def col(name, k=0):
            at = COL_AT[name] + k
            return cols[:, at:at + 1]

        def row(name, lo=0, n=None):
            at = ROW_AT[name] + lo
            return rows[:, at:at + (n or ROWS[name])]

        K = dict(nc=nc, A=A, sb=sb, sem=sem, x=x, cols=cols, rows=rows, ident=ident,
                 head_mask=head_mask, band=band, ps=ps, col=col, row=row, finished=finished, ahead=None,
                 spiral=filter_buffers(sb))
        pairs = ((cross_attention_0, self_attention_0), (experts_0, cross_attention_1), (spiral_1, experts_1))
        for n, pair in enumerate(pairs):
            with ExitStack() as both:
                if n == 1:
                    K["ahead"] = cross_attention_1_ahead(sb, both, A)
                elif n == 2:
                    K["ahead"] = experts_1_ahead(sb, both, A)
                for stage in pair:
                    with ExitStack() as own:
                        stage(own, **K)
                    for s in finished:
                        nc.release_semaphore(s)
                    finished[:], in_stage[:] = in_stage, []
        stored = sem("stored")
        with nc.Block() as block:
            @block.sync
            def _(sp):
                sp.dma_start(A["out"].rearrange("(t two) n d -> (two n) t d", two=2), x[:]).then_inc(stored, 16)
                sp.wait_ge(stored, 16)


def norm_stats(nc, step, src, stats, mv, var, tiles, ready):
    for t in range(tiles):
        last = nc.vector.bn_stats(stats[:, t, :], src[:, t, :])
    step.link(last)
    for t in range(tiles):
        last = nc.vector.bn_aggr(mv[:, t, :], stats[:, t, :])
    step.link(last)
    nc.vector.tensor_scalar(var[:, 0:tiles], mv[:, 0:tiles, 1], EPS, None, ALU.add).then_inc(ready, 1)


def split_matmul(nc, out, w, m, start, stop):
    nc.tensor.matmul(out, w[0], m[0], start=start, stop=False)
    nc.tensor.matmul(out, w[0], m[1], start=False, stop=False)
    return nc.tensor.matmul(out, w[1], m[0], start=False, stop=stop)


def norm_apply(nc, dst, src, mv, rstd, tiles):
    for t in range(tiles):
        last = nc.vector.tensor_scalar(dst[:, t, :], src[:, t, :], mv[:, t, 0:1], rstd[:, t:t + 1],
                                       ALU.subtract, ALU.mult)
    return last


def add_norm(nc, dve, step, x, acc, gain, stats, mv, rstd, var, var_ready, rstd_ready):
    norm_stats(nc, step, acc, stats, mv, var, TT, var_ready)
    for t in range(TT):
        last = nc.vector.scalar_tensor_tensor(out=acc[:, t, :], in0=acc[:, t, :], scalar=mv[:, t, 0:1], in1=gain,
                                              op0=ALU.subtract, op1=ALU.mult)
    step.link(last)
    dve.wait_ge(rstd_ready, 2)
    for t in range(TT):
        nc.vector.scalar_tensor_tensor(out=x[:, t, :], in0=acc[:, t, :], scalar=rstd[:, t:t + 1], in1=x[:, t, :],
                                       op0=ALU.mult, op1=ALU.add)


def softmax_rows(nc, step, p, n, top):
    step.link(nc.vector.tensor_reduce(out=top, in_=p, axis=AX.X, op=ALU.max))
    return nc.vector.tensor_tensor(out=p, in0=p, in1=top.unsqueeze(2).to_broadcast(list(p.shape)), op=ALU.subtract)


def normalise_rows(nc, step, p, total):
    step.link(nc.vector.tensor_reduce(out=total, in_=p, axis=AX.X, op=ALU.add))
    step.link(nc.vector.reciprocal(total, total))
    return nc.vector.tensor_tensor(out=p, in0=p, in1=total.unsqueeze(2).to_broadcast(list(p.shape)), op=ALU.mult)


def top_two(nc, step, g, rank, picked, work, best):
    shape = list(g.shape)

    def wide(v):
        return v.unsqueeze(2).to_broadcast(shape)

    ranks = rank.unsqueeze(1).to_broadcast(shape)
    place = work[:, 0]
    taken = work[:, 1]
    rest = work[:, 2]
    top = best[:, 2]
    for n in range(2):
        src = g if n == 0 else rest
        step.link(nc.vector.tensor_reduce(out=best[:, n], in_=src, axis=AX.X, op=ALU.max))
        step.link(nc.vector.tensor_tensor(out=place, in0=src, in1=wide(best[:, n]), op=ALU.is_equal))
        step.link(nc.vector.tensor_tensor(out=place, in0=place, in1=ranks, op=ALU.mult))
        step.link(nc.vector.tensor_reduce(out=top, in_=place, axis=AX.X, op=ALU.max))
        mark = picked if n == 0 else taken
        step.link(nc.vector.tensor_tensor(out=mark, in0=place, in1=wide(top), op=ALU.is_equal))
        if n == 0:
            step.link(nc.vector.scalar_tensor_tensor(out=rest, in0=picked, scalar=-2.0, in1=g, op0=ALU.mult, op1=ALU.add))
    step.link(nc.vector.tensor_tensor(out=picked, in0=picked, in1=taken, op=ALU.add))
    step.link(nc.vector.tensor_tensor(out=picked, in0=picked, in1=g, op=ALU.mult))
    step.link(nc.vector.tensor_tensor(out=top, in0=best[:, 0], in1=best[:, 1], op=ALU.add))
    step.link(nc.vector.reciprocal(top, top))
    return nc.vector.tensor_tensor(out=picked, in0=picked, in1=wide(top), op=ALU.mult)


def cross_attention_0(own, nc, A, sb, sem, x, cols, rows, ident, head_mask, band, ps, col, row, finished, ahead, spiral):
    UNITS = 4
    GP = NPAIR // 2
    M = 8 * N
    wk_hi = sb("wk_hi", [P, KT, H * DH], own, F32R)
    wk_lo = sb("wk_lo", [P, KT, H * DH], own, F32R)
    wv = sb("wv", [P, KT, H * DH], own)
    wo = sb("wo", [P, NPAIR, D], own)
    cosT = sb("cosT", [P, S], own)
    sinT = sb("sinT", [P, S], own)
    z = [sb(f"z{i}", [P, ST, D], own) for i in range(2)]
    zT_hi = sb("zT_hi", [P, KT, S], own, F32R)
    zT_lo = sb("zT_lo", [P, KT, S], own, F32R)
    zT = sb("zT", [P, 512], own)
    q = sb("q", [P, NPAIR, B, 2, N], own)
    keys = [sb(f"keys{i}", [P, GP, S], own) for i in range(2)]
    wq, wk = (keys[1][:].rearrange("p a s -> p (a s)")[:, i * KT * H * DH:(i + 1) * KT * H * DH].rearrange("p (k n) -> p k n", k=KT)
              for i in range(2))
    kcos = [sb(f"kcos{i}", [P, 512], own) for i in range(2)]
    ksin = [sb(f"ksin{i}", [P, 512], own) for i in range(2)]
    NE = 4
    prob = [sb(f"prob{i}", [P, M], own) for i in range(NE)]
    psum_s = [sb(f"prob_sum{i}", [P, M], own) for i in range(2)]
    mix = sb("mix", [P, KT, H, 2, N], own)
    rden = sb("rden", [P, M], own)
    outT = sb("outT", [P, NPAIR, P], own)
    ones = sb("ones", [P, P], own)
    stats = sb("stats", [P, ST, 6], own)
    mv = sb("mv", [P, ST, 2], own)
    var = sb("var", [P, ST], own)
    rstd = sb("rstd", [P, ST], own)
    half = sb("half", [P, ST], own)
    lat = mix[:, 0].rearrange("p h a n -> p (h a n)")[:, 0:TT * D].rearrange("p (t d) -> p t d", t=TT)
    latT = mix[:, 1].rearrange("p h a n -> p (h a n)")[:, 0:KT * T].rearrange("p (k t) -> p k t", k=KT)

    keys_ps = [ps[:, 0, :], ps[:, 1, :]]
    score_ps = [ps[:, 2, :], ps[:, 3, :]]
    mix_ps = [ps[:, 4, :], ps[:, 5, :]]
    turn_ps = ps[:, 6, :]
    den_ps = ps[:, 7, :]

    x_loaded = sem("x_loaded"); cols_loaded = sem("cols_loaded"); rows_loaded = sem("rows_loaded")
    wq_loaded = sem("wq_loaded"); wk_loaded = sem("wk_loaded"); wvo_loaded = sem("wvo_loaded")
    rope_loaded = sem("rope_loaded"); ctx_loaded = sem("ctx_loaded")
    consts_made = sem("consts_made"); pool_step = sem("pool_step0"); dve_step = sem("dve_step0")
    pool_passed = sem("pool_passed0"); dve_passed = sem("dve_passed0")
    act_step = sem("act_step0"); angle_ready = sem("angle_ready")
    x_var = sem("x_var0"); x_rstd = sem("x_rstd0"); lat_ready = sem("lat_ready")
    lat_turned = sem("lat_turned"); latT_ready = sem("latT_ready"); q_done = sem("q_done")
    q_act = sem("q_act"); q_dve = sem("q_dve")
    ctx_var = sem("ctx_var"); ctx_rstd = sem("ctx_rstd"); z_ready = sem("z_ready")
    z_turned = sem("z_turned"); zT_rounded = sem("zT_rounded"); zT_ready = sem("zT_ready")
    q_zeroed = sem("q_zeroed"); wk_rounded = sem("wk_rounded"); wk_ready = sem("wk_ready")
    key_mm = sem("key_mm"); key_read = sem("key_read"); key_ready = sem("key_ready")
    score_mm = sem("score_mm"); exp_done = sem("exp_done"); prob_ready = sem("prob_ready")
    mix_mm = sem("mix_mm"); sum_done = sem("sum_done"); mix_copied = sem("mix_copied")
    den_mm = sem("den_mm"); mix_ready = sem("mix_ready"); value_mm = sem("value_mm")
    outT_ready = sem("outT_ready"); out_mm = sem("out_mm"); x_added = sem("x_added0")

    RING = 2
    TILES = 2 * GP
    ctx_d = A["ctx_1024"].rearrange("b (t p) d -> b p t d", p=P)

    def context_quarter(i, u, t):
        b = 2 * i + u // 2 + 1
        if u % 2 == 0:
            return b, {5: 0, 6: 1}.get(t)
        return b, {0: 2, 1: 3}.get(t)

    with nc.Block() as block:
        @block.sync
        def _(sp):
            sp.dma_start(x[:], A["x"].rearrange("(t two) n d -> (two n) t d", two=2)).then_inc(x_loaded, 16)
            sp.dma_start(cols[:], A["cols"]).then_inc(cols_loaded, 16)
            sp.dma_start(wq, A["wq_pairs"].rearrange("(k p) n -> p k n", p=P)).then_inc(wq_loaded, 16)
            sp.dma_start(z[0][:], ctx_d[0]).then_inc(ctx_loaded, 16)
            sp.dma_start(wk, A["wk_pairs"].rearrange("(k p) n -> p k n", p=P)).then_inc(wk_loaded, 16)
            sp.dma_start(cosT[:], A["cosT"]).then_inc(rope_loaded, 16)
            sp.dma_start(sinT[:], A["sinT"]).then_inc(rope_loaded, 16)
            sp.wait_ge(ctx_loaded, 16)
            sp.dma_start(z[1][:], ctx_d[1]).then_inc(ctx_loaded, 16)
            sp.dma_start(wv[:], A["wv"].rearrange("(k p) n -> p k n", p=P)).then_inc(wvo_loaded, 16)
            sp.dma_start(wo[:], A["L0_xattn_Wo"].rearrange("(k p) n -> p k n", p=P)).then_inc(wvo_loaded, 16)
            sp.dma_start(rows[:], A["rows"].to_broadcast([P, NROW])).then_inc(rows_loaded, 16)
            with sp.Fori(0, TT - 1) as i:
                for a in range(2):
                    sp.wait_ge(mix_mm, (2 * i + a + 1) * 2 * ST + NE)
                    sp.wait_ge(ctx_loaded, 16 * (2 * i + a + 2))
                    sp.dma_start(z[a][:], ctx_d[bass.ds(2 * i + a + 2, 1)].rearrange("b p t d -> (b p) t d")).then_inc(ctx_loaded, 16)

        @block.gpsimd
        def _(pool):
            step = Chain(pool, pool_step)
            step.link(nc.gpsimd.memset(ident[:], 0.0))
            step.link(nc.gpsimd.affine_select(out=ident[:], in_=ident[:], compare_op=ALU.not_equal, fill=1.0,
                                              base=0, pattern=[[-1, P]], channel_multiplier=1))
            step.link(nc.gpsimd.memset(half[:], -0.5))
            step.link(nc.gpsimd.memset(ones[:], 1.0))
            pool.sem_inc(consts_made, 1)
            pool.sem_inc(key_ready, 2)
            pool.sem_inc(sum_done, NE)
            for n in range(2):
                pool.wait_ge(x_var, n + 1)
                nc.gpsimd.tensor_tensor(out=rstd[:, 0:TT], in0=var[:, 0:TT], in1=half[:, 0:TT], op=ALU.pow).then_inc(x_rstd, 1)
                if n == 0:
                    nc.gpsimd.memset(q[:, 0:NPAIR // 4], 0.0).then_inc(q_zeroed, 1)
            nc.gpsimd.memset(q[:, NPAIR // 4:], 0.0).then_inc(q_zeroed, 1)

            def context_rstd(b):
                pool.wait_ge(ctx_var, b + 1)
                step.link(nc.gpsimd.tensor_tensor(out=rstd[:], in0=var[:], in1=half[:], op=ALU.pow))
                pool.sem_inc(ctx_rstd, 1)

            def turn_key(unit, t, parity):
                pool.wait_ge(key_read, unit * TILES + t + 1 + RING)
                nc.gpsimd.tensor_tensor(out=keys[parity][:, t % GP, (t // GP) * 512:(t // GP) * 512 + 512],
                                        in0=kcos[t % 2][:], in1=ksin[t % 2][:], op=ALU.add).then_inc(key_ready, 1)

            pool.wait_ge(x_rstd, 2)
            context_rstd(0)
            pool.wait_ge(wk_rounded, 1)
            nc.gpsimd.tensor_tensor(out=wk_lo[:], in0=wk, in1=wk_hi[:].bitcast(F32), op=ALU.subtract).then_inc(wk_ready, 1)
            for t in range(TILES):
                turn_key(0, t, 0)
            step.link(nc.gpsimd.memset(head_mask[:], 1.0))
            for sign, base in ((1, 0), (-1, 15)):
                step.link(nc.gpsimd.affine_select(out=head_mask[:], in_=head_mask[:], compare_op=ALU.is_ge, fill=0.0,
                                                  base=base, pattern=[[-16 * sign, 8]], channel_multiplier=sign))
            step.link(nc.gpsimd.memset(band[:], 0.0))
            for hh in range(2):
                part = band[64 * hh:64 * hh + 64]
                step.link(nc.gpsimd.affine_select(out=part, in_=part, compare_op=ALU.is_ge, fill=NEG, base=0,
                                                  pattern=[[0, NPAIR], [-1, N]], channel_multiplier=1))
                for pair in range(NPAIR):
                    window = max(4, 256 >> (2 * pair + hh))
                    if window < N:
                        part = band[64 * hh:64 * hh + 64, pair]
                        step.link(nc.gpsimd.affine_select(out=part, in_=part, compare_op=ALU.is_ge, fill=NEG,
                                                          base=window - 1, pattern=[[1, N]], channel_multiplier=-1))

            first = step.n

            def turn(i, last):
                step.base, step.n = i * LINKS if last else i * LINKS, first
                for u in range(UNITS):
                    unit = i * UNITS + u
                    if not (last and u == UNITS - 1):
                        pool.wait_ge(score_mm, unit * ST + 1)
                    for t in range(ST):
                        if t == 0:
                            wait_alone(pool, pool_passed, prob_ready, unit * ST + t + 1)
                        else:
                            pool.wait_ge(prob_ready, unit * ST + t + 1)
                        total, e = psum_s[u % 2], prob[t % NE]
                        if t == 0:
                            nc.gpsimd.tensor_copy(total[:], e[:]).then_inc(sum_done, 1)
                        else:
                            pool.wait_ge(sum_done, unit * ST + t + NE)
                            nc.gpsimd.tensor_tensor(out=total[:], in0=total[:], in1=e[:], op=ALU.add).then_inc(sum_done, 1)
                        if u % 2 == 0 and t == 3 and not (last and u == 2):
                            context_rstd(2 * i + u // 2 + 1)
                        if not (last and u == UNITS - 1):
                            turn_key(unit + 1, t, (u + 1) % 2)

            LINKS = 2
            with pool.Fori(0, TT - 1) as i:
                turn(i, False)
            turn(TT - 1, True)

        @block.scalar
        def _(act):
            act.sem_inc(exp_done, 2)
            act.sem_inc(mix_copied, 1)
            act.wait_ge(cols_loaded, 16)
            filter_parts(nc, act, Chain(act, act_step), spiral, cols, angle_ready)
            for k in range(KT):
                act.wait_ge(lat_turned, k + 1)
                nc.scalar.activation(latT[:, k, :], keys_ps[k], ACT.Identity, bias=col("L0_xattn_ln_lat_b", k),
                                     scale=col("L0_xattn_ln_lat_g", k)).then_inc(latT_ready, 1)
            def normed_context(b, a, g):
                act.wait_ge(z_turned, 4 * b + g + 1)
                k, h = g % 2, g // 2
                for dst in (zT[:], zT_hi[:, k, h * 512:h * 512 + 512]):
                    last = nc.scalar.activation(dst, turn_ps, ACT.Identity, bias=col("L0_xattn_ln_ctx_b", k),
                                                scale=col("L0_xattn_ln_ctx_g", k))
                last.then_inc(zT_rounded, 1)

            act.wait_ge(q_zeroed, 2)
            for pair in range(NPAIR):
                act.wait_ge(q_done, pair + 1)
                src = ps[:, 2 + pair % 4, :]
                for hh in range(2):
                    r = 32 * hh
                    last = nc.scalar.copy(q[r:r + 32, pair, :, hh, :], src[r:r + 32].rearrange("p (b n) -> p b n", b=B))
                last.then_inc(q_act, 1)
                if pair == 0:
                    act.wait_ge(wk_loaded, 16)
                    nc.scalar.copy(wk_hi[:], wk).then_inc(wk_rounded, 1)
                if pair % 2 == 1:
                    if pair > 1:
                        act.wait_ge(zT_ready, pair // 2)
                    normed_context(0, 0, pair // 2)


            def turn(i, last):
                for u in range(UNITS):
                    unit = i * UNITS + u
                    for t in range(ST):
                        tile = unit * ST + t
                        act.wait_ge(score_mm, tile + 2)
                        act.wait_ge(mix_mm, tile + 1)
                        act.wait_ge(sum_done, tile + 1)
                        nc.scalar.activation(prob[t % NE][:], score_ps[t % 2], ACT.Exp, scale=DH ** -0.5).then_inc(exp_done, 1)
                        b, g = context_quarter(i, u, t)
                        if g is not None and not (last and u >= 2):
                            act.wait_ge(zT_ready, 4 * b + g)
                            if g % 2 == 0:
                                act.wait_ge(key_mm, b * 2 * TILES - GP * (1 - g // 2))
                            normed_context(b, 0, g)
                    act.wait_ge(mix_mm, (unit + 1) * ST + NE)
                    if u == 0:
                        act.wait_ge(value_mm, i + 1)
                    for k in range(KT):
                        nc.scalar.copy(mix[:, k, 8 * (u % 2):8 * (u % 2) + 8, u // 2, :],
                                       mix_ps[k].rearrange("p (h n) -> p h n", h=8)).then_inc(mix_copied, 1)
                act.wait_ge(value_mm, i + 2)
                for n in range(2):
                    nc.scalar.copy(outT[:, 4 * n:4 * n + 4, :], score_ps[n].rearrange("p (a t) -> p a t", a=4)).then_inc(outT_ready, 1)

            with act.Fori(0, TT - 1) as i:
                turn(i, False)
            turn(TT - 1, True)

        @block.vector
        def _(dve):
            step = Chain(dve, dve_step)
            dve.sem_inc(key_read, RING)

            def norm_latents(n, src):
                for t in range(TT):
                    last = nc.vector.bn_stats(stats[:, t, :], src[:, t, :])
                step.link(last)
                for t in range(TT):
                    last = nc.vector.bn_aggr(mv[:, t, :], stats[:, t, :])
                step.link(last)
                nc.vector.tensor_scalar(var[:, 0:TT], mv[:, 0:TT, 1], EPS, None, ALU.add).then_inc(x_var, 1)
                dve.wait_ge(x_rstd, n + 1)
                for t in range(TT):
                    last = nc.vector.tensor_scalar(lat[:, t, :], src[:, t, :], mv[:, t, 0:1], rstd[:, t:t + 1],
                                                   ALU.subtract, ALU.mult)
                return last

            dve.wait_ge(x_loaded, 16)
            step.link(norm_latents(0, x))
            norm_latents(1, lat).then_inc(lat_ready, 1)
            dve.wait_ge(cols_loaded, 16)
            filter_angle(nc, step, spiral, cols, angle_ready)

            def context_stats(b, a, lo, hi):
                if lo == 0:
                    dve.wait_ge(ctx_loaded, 16 * (b + 1))
                for t in range(lo, hi):
                    last = nc.vector.bn_stats(stats[:, t, :], z[a][:, t, :])
                if hi == ST:
                    step.link_alone(last, dve_passed)
                    for t in range(ST):
                        last = nc.vector.bn_aggr(mv[:, t, :], stats[:, t, :])
                    step.link(last)
                    nc.vector.tensor_scalar(var[:], mv[:, :, 1], EPS, None, ALU.add).then_inc(ctx_var, 1)

            def context_norm(b, a, lo, hi):
                dve.wait_ge(ctx_rstd, b + 1)
                for t in range(lo, hi):
                    last = nc.vector.tensor_scalar(z[a][:, t, :], z[a][:, t, :], mv[:, t, 0:1], rstd[:, t:t + 1],
                                                   ALU.subtract, ALU.mult)
                last.then_inc(z_ready, 1)

            dve.wait_ge(lat_ready, 1)
            context_stats(0, 0, 0, ST)
            context_norm(0, 0, 0, ST // 2)
            context_norm(0, 0, ST // 2, ST)
            def context_rests(b, g):
                dve.wait_ge(zT_rounded, 4 * b + g + 1)
                at = (slice(None), g % 2, slice((g // 2) * 512, (g // 2) * 512 + 512))
                nc.vector.tensor_tensor(out=zT_lo[at], in0=zT[:], in1=zT_hi[at].bitcast(F32), op=ALU.subtract).then_inc(zT_ready, 1)

            dve.wait_ge(q_zeroed, 2)
            for pair in range(NPAIR):
                dve.wait_ge(q_done, pair + 1)
                src = ps[:, 2 + pair % 4, :]
                for hh in range(2):
                    r = 64 + 32 * hh
                    last = nc.vector.tensor_copy(q[r:r + 32, pair, :, hh, :], src[r:r + 32].rearrange("p (b n) -> p b n", b=B))
                last.then_inc(q_dve, 1)
                if pair % 2 == 1:
                    context_rests(0, pair // 2)
            dve.wait_ge(rope_loaded, 32)
            dve.wait_ge(cols_loaded, 16)

            def key_products(unit, t):
                tile = unit * TILES + t
                dve.wait_ge(key_mm, tile + 1)
                dve.wait_ge(key_ready, tile + 1)
                src, at = keys_ps[t % 2], slice((t // GP) * 512, (t // GP) * 512 + 512)
                nc.vector.tensor_tensor(out=kcos[t % 2][:], in0=src, in1=cosT[:, at], op=ALU.mult)
                nc.vector.scalar_tensor_tensor(out=ksin[t % 2][0:64], in0=src[64:128], scalar=-1.0, in1=sinT[0:64, at],
                                               op0=ALU.mult, op1=ALU.mult)
                nc.vector.tensor_tensor(out=ksin[t % 2][64:128], in0=src[0:64], in1=sinT[64:128, at],
                                        op=ALU.mult).then_inc(key_read, 1)

            for t in range(TILES):
                key_products(0, t)
            first = step.n

            def turn(i, last):
                step.base, step.n = i * LINKS, first
                for u in range(UNITS):
                    unit = i * UNITS + u
                    for t in range(ST):
                        dve.wait_ge(exp_done, unit * ST + t + 1 + RING)
                        nc.vector.tensor_scalar(prob[t % NE][:], prob[t % NE][:], float(np.exp(np.float32(11))),
                                                float(np.exp(np.float32(-11))), ALU.min, ALU.max).then_inc(prob_ready, 1)
                        b, g = context_quarter(i, u, t - 1)
                        if g is not None and not (last and u >= 2):
                            context_rests(b, g)
                        if not (last and u == UNITS - 1):
                            key_products(unit + 1, t)
                        if u % 2 == 0 and not (last and u == 2):
                            b, a = 2 * i + u // 2 + 1, (u // 2 + 1) % 2
                            if t == 2:
                                context_stats(b, a, 0, ST // 2)
                            if t == 3:
                                context_stats(b, a, ST // 2, ST)
                            if t == 4:
                                context_norm(b, a, 0, ST // 2)
                            if t == 5:
                                context_norm(b, a, ST // 2, ST)
                        if t == 3 and u > 0:
                            finish_mix(i, u - 1)
                finish_mix(i, UNITS - 1)
                dve.wait_ge(out_mm, i + 1)
                xt = x[:].rearrange("p t d -> p (t d)")[:, bass.ds(i * D, D)]
                dve.wait_ge(rows_loaded, 16)
                step.link(nc.vector.tensor_tensor(out=xt, in0=den_ps[:, 0:D], in1=xt, op=ALU.add))
                nc.vector.tensor_tensor(out=xt, in0=xt, in1=row("L0_xattn_bo"), op=ALU.add).then_inc(x_added, 1)

            def finish_mix(i, u):
                dve.wait_ge(den_mm, i * UNITS + u + 1)
                step.link(nc.vector.reciprocal(rden[:], den_ps))
                dve.wait_ge(mix_copied, KT * (i * UNITS + u + 1) + 1)
                for k in range(KT):
                    part = mix[:, k, 8 * (u % 2):8 * (u % 2) + 8, u // 2, :]
                    step.link(nc.vector.scalar_tensor_tensor(out=part, in0=part, scalar=col("L0_xattn_ln_ctx_g", k),
                                                             in1=rden[:].rearrange("p (h n) -> p h n", h=8),
                                                             op0=ALU.mult, op1=ALU.mult))
                    last = nc.vector.tensor_scalar(part, part, col("L0_xattn_ln_ctx_b", k), None, ALU.add)
                last.then_inc(mix_ready, 1)

            LINKS = UNITS * 3 + 2 * 2 + 1
            with dve.Fori(0, TT - 1) as i:
                turn(i, False)
            assert step.n == first + LINKS
            turn(TT - 1, True)

        @block.tensor
        def _(pe):
            pe.sem_inc(mix_mm, NE)
            pe.sem_inc(score_mm, 1)
            pe.sem_inc(value_mm, 1)
            pe.wait_ge(consts_made, 1)
            pe.wait_ge(lat_ready, 1)
            for k in range(KT):
                for t in range(TT):
                    last = nc.tensor.transpose(keys_ps[k][:, t * P:(t + 1) * P], lat[:, t, k * P:(k + 1) * P], ident[:])
                last.then_inc(lat_turned, 1)
            pe.wait_ge(latT_ready, KT)
            pe.wait_ge(wq_loaded, 16)
            def turn_context(b, a, g):
                pe.wait_ge(z_ready, 2 * b + 1 + g // 2)
                pe.wait_ge(zT_rounded, 4 * b + g)
                for t in range(4):
                    last = nc.tensor.transpose(turn_ps[:, t * P:(t + 1) * P],
                                               z[a][:, 4 * (g // 2) + t, (g % 2) * P:(g % 2 + 1) * P], ident[:])
                last.then_inc(z_turned, 1)

            for pair in range(NPAIR):
                if pair >= 4:
                    pe.wait_ge(q_act, pair - 3)
                    pe.wait_ge(q_dve, pair - 3)
                for k in range(KT):
                    last = nc.tensor.matmul(ps[:, 2 + pair % 4, :], wq[:, k, pair * P:(pair + 1) * P], latT[:, k, :],
                                            start=k == 0, stop=k == KT - 1)
                last.then_inc(q_done, 1)
                if pair % 2 == 1:
                    turn_context(0, 0, pair // 2)

            def project_key(unit, b, a, g, t):
                pair, h = g * GP + t % GP, t // GP
                pe.wait_ge(zT_ready, 4 * b + 2 + 2 * h)
                pe.wait_ge(key_read, unit * TILES + t + 1)
                for k in range(KT):
                    at, w_at = (slice(None), k, slice(h * 512, h * 512 + 512)), (slice(None), k, slice(pair * P, (pair + 1) * P))
                    last = split_matmul(nc, keys_ps[t % 2], (wk_hi[w_at], wk_lo[w_at]), (zT_hi[at], zT_lo[at]), k == 0, k == KT - 1)
                last.then_inc(key_mm, 1)

            pe.wait_ge(wk_ready, 1)
            for t in range(TILES):
                project_key(0, 0, 0, 0, t)
            pe.wait_ge(q_act, NPAIR)
            pe.wait_ge(q_dve, NPAIR)
            qf = q[:].rearrange("p a b h n -> p (a b h n)")

            def weigh(unit, u, t):
                pe.wait_ge(prob_ready, unit * ST + t + 1)
                if t == 0:
                    pe.wait_ge(mix_copied, KT * unit + 1)
                for k in range(KT):
                    last = nc.tensor.matmul(mix_ps[k], z[u // 2][:, t, k * P:(k + 1) * P], prob[t % NE][:],
                                            start=t == 0, stop=t == ST - 1)
                last.then_inc(mix_mm, 1)

            def denominators(i, u):
                pe.wait_ge(sum_done, (i * UNITS + u + 1) * ST + NE)
                if u > 0:
                    pe.wait_ge(mix_ready, i * UNITS + u)
                nc.tensor.matmul(den_ps, ones[:], psum_s[u % 2][:], start=True, stop=True).then_inc(den_mm, 1)

            def project_values(i, n):
                for pair in range(4 * n, 4 * n + 4):
                    for k in range(KT):
                        for hh in range(2):
                            head = 2 * pair + hh
                            last = nc.tensor.matmul(score_ps[n][64 * hh:64 * hh + 64, (pair % 4) * P:(pair % 4 + 1) * P],
                                                    wv[:, k, head * DH:(head + 1) * DH],
                                                    mix[:, k, head].rearrange("p a n -> p (a n)"),
                                                    start=k == 0, stop=k == KT - 1)
                return last

            def turn(i, last):
                for u in range(UNITS):
                    unit = i * UNITS + u
                    for t in range(ST):
                        tile = unit * ST + t
                        if t == 0:
                            pe.wait_ge(key_ready, (unit + 1) * TILES + RING)
                        pe.wait_ge(exp_done, tile + 1)
                        for j in range(GP):
                            pair = (u % 2) * GP + j
                            mm = nc.tensor.matmul(score_ps[t % 2][:, j * P:(j + 1) * P],
                                                  keys[u % 2][:, j, t * P:(t + 1) * P],
                                                  qf[:, bass.ds((2 * i + u // 2) * P + pair * B * P, P)], start=True, stop=True)
                        mm.then_inc(score_mm, 1)
                        if not (last and u == UNITS - 1):
                            project_key(unit + 1, 2 * i + (u + 1) // 2, ((u + 1) // 2) % 2, (u + 1) % 2, t)
                        if t > 0:
                            weigh(unit, u, t - 1)
                        if t == 2 and u > 0:
                            denominators(i, u - 1)
                        b, g = context_quarter(i, u, t)
                        if g is not None and not (last and u >= 2):
                            turn_context(b, (u // 2 + 1) % 2, g)
                    weigh(unit, u, ST - 1)
                denominators(i, UNITS - 1)
                pe.wait_ge(exp_done, (i + 1) * UNITS * ST + RING)
                pe.wait_ge(wvo_loaded, 32)
                pe.wait_ge(mix_ready, i * UNITS + 3)
                project_values(i, 0)
                pe.wait_ge(mix_ready, (i + 1) * UNITS)
                project_values(i, 1).then_inc(value_mm, 1)
                pe.wait_ge(outT_ready, 2 * (i + 1))
                for pair in range(NPAIR):
                    mm = nc.tensor.matmul(den_ps[:, 0:D], outT[:, pair, :], wo[:, pair, :],
                                          start=pair == 0, stop=pair == NPAIR - 1)
                mm.then_inc(out_mm, 1)
                pe.wait_ge(x_added, i + 1)

            with pe.Fori(0, TT - 1) as i:
                turn(i, False)
            turn(TT - 1, True)


def self_attention_0(own, nc, A, sb, sem, x, cols, rows, ident, head_mask, band, ps, col, row, finished, ahead, spiral):
    HD = D // H
    h = sb("sa_h", [P, TT, D], own)
    hT = sb("sa_hT", [P, KT, T], own)
    wqk = sb("sa_wqk", [P, KT, 2 * D], own)
    wgate = sb("sa_wgate", [P, KT, H], own)
    wproj = sb("sa_wproj", [P, KT, D], own)
    qT = sb("sa_qT", [P, KT, T], own)
    kT = sb("sa_kT", [P, KT, T], own)
    keys = sb("sa_keys", [P, TT, D], own)
    gates = sb("sa_gates", [P, TT, H], own)
    gatesT = sb("sa_gatesT", [H, T], own)
    gateX = sb("sa_gateX", [P, KT, T], own)
    spread = sb("sa_spread", [H, D], own)
    own_half = sb("sa_own_half", [P, 2], own)
    qblk = [sb(f"sa_qblk{i}", [P, 2, KT, 8, N], own) for i in range(2)]
    p = [sb(f"sa_p{i}", [P, NPAIR, 2, N], own) for i in range(2)]
    pT = [sb(f"sa_pT{i}", [P, NPAIR, P], own) for i in range(2)]
    outT = [sb(f"sa_outT{i}", [P, KT, P], own) for i in range(2)]
    stats = sb("sa_stats", [P, TT, 6], own)
    mv = sb("sa_mv", [P, TT, 2], own)
    var = sb("sa_var", [P, TT], own)
    rstd = sb("sa_rstd", [P, TT], own)
    half = sb("sa_half", [P, TT], own)
    top = sb("sa_top", [P, 2 * NPAIR], own)
    total = sb("sa_total", [P, 2 * NPAIR], own)

    w_loaded = sem("sa_w_loaded"); consts = sem("sa_consts"); pool_step = sem("sa_pool_step")
    dve_step = sem("sa_dve_step"); var_ready = sem("sa_var"); rstd_ready = sem("sa_rstd")
    h_ready = sem("sa_h_ready"); h_turned = sem("sa_h_turned"); hT_ready = sem("sa_hT_ready")
    qk_mm = sem("sa_qk_mm"); q_ready = sem("sa_q_ready"); k_ready = sem("sa_k_ready"); keys_mm = sem("sa_keys_mm"); keys_ready = sem("sa_keys_ready")
    gate_mm = sem("sa_gate_mm"); gate_arg = sem("sa_gate_arg"); gate_exp = sem("sa_gate_exp")
    gates_ready = sem("sa_gates_ready"); gates_turned = sem("sa_gates_turned"); gatesT_ready = sem("sa_gatesT_ready")
    spread_mm = sem("sa_spread_mm"); gateX_ready = sem("sa_gateX_ready")
    qblk_ready = sem("sa_qblk_ready"); score_mm = sem("sa_score_mm"); score_read = sem("sa_score_read")
    arg_ready = sem("sa_arg_ready"); exp_done = sem("sa_exp_done"); p_ready = sem("sa_p_ready")
    p_turned = sem("sa_p_turned"); pT_ready = sem("sa_pT_ready"); out_mm = sem("sa_out_mm")
    outT_ready = sem("sa_outT_ready"); proj_mm = sem("sa_proj_mm"); x_added = sem("sa_x_added")

    scores = ps[:, 0:4, :].rearrange("p (b c) (a s) -> p b (c a) s", b=2, a=4)
    outs = ps[:, 6:8, 0:KT * P].rearrange("p b (g c) -> p b g c", g=KT)

    with nc.Block() as block:
        @block.sync
        def _(sp):
            sp.dma_start(wqk[:], A["L0_attn_Wqk"].rearrange("(k p) n -> p k n", p=P)).then_inc(w_loaded, 16)
            sp.dma_start(wgate[:], A["L0_attn_Wgate"].rearrange("(k p) n -> p k n", p=P)).then_inc(w_loaded, 16)
            sp.dma_start(wproj[:], A["L0_attn_Wproj"].rearrange("(k p) n -> p k n", p=P)).then_inc(w_loaded, 16)

        @block.gpsimd
        def _(pool):
            for s in finished:
                pool.sem_clear(s)
            step = Chain(pool, pool_step)
            step.link(nc.gpsimd.memset(half[:], -0.5))
            pool.wait_ge(var_ready, 1)
            nc.gpsimd.tensor_tensor(out=rstd[:], in0=var[:], in1=half[:], op=ALU.pow).then_inc(rstd_ready, 1)
            pool.wait_ge(rstd_ready, 1)
            step.link(nc.gpsimd.memset(spread[:], 1.0))
            for sign, base in ((1, 0), (-1, HD - 1)):
                step.link(nc.gpsimd.affine_select(out=spread[:], in_=spread[:], compare_op=ALU.is_ge, fill=0.0,
                                                  base=base, pattern=[[sign, D]], channel_multiplier=-HD * sign))
            pool.sem_inc(consts, 1)
            pool.wait_ge(q_ready, KT)
            for tt in range(TT):
                if tt >= 2:
                    pool.wait_ge(score_mm, tt - 1)
                for b in range(2):
                    for g in range(KT):
                        at = (2 * tt + b) * N
                        step.link(nc.gpsimd.tensor_tensor(
                            out=qblk[tt % 2][:, b, g], in0=head_mask[:].unsqueeze(2).to_broadcast([P, 8, N]),
                            in1=qT[:, g, at:at + N].unsqueeze(1).to_broadcast([P, 8, N]), op=ALU.mult))
                pool.sem_inc(qblk_ready, 1)
            filter_powers(nc, step, spiral, cols)

        @block.scalar
        def _(act):
            def copy_pT(tt):
                if tt >= 2:
                    act.wait_ge(out_mm, tt - 1)
                for n in range(2):
                    act.wait_ge(p_turned, 2 * tt + n + 1)
                    nc.scalar.copy(pT[tt % 2][:, 4 * n:4 * n + 4, :], ps[:, 4 + n, :].rearrange("p (a t) -> p a t", a=4)).then_inc(pT_ready, 1)

            for k in range(KT):
                act.wait_ge(h_turned, k + 1)
                nc.scalar.copy(hT[:, k, :], ps[:, k, :]).then_inc(hT_ready, 1)
            for g in range(KT):
                act.wait_ge(qk_mm, KT + g + 1)
                nc.scalar.activation(kT[:, g, :], ps[:, 2 + KT + g, :], ACT.Identity,
                                     bias=col("L0_attn_bqk", 2 + g)).then_inc(k_ready, 1)
            act.wait_ge(gate_arg, 1)
            nc.scalar.activation(gates[:], gates[:], ACT.Exp).then_inc(gate_exp, 1)
            act.wait_ge(gates_turned, 1)
            nc.scalar.copy(gatesT[:], ps[0:H, 4, :]).then_inc(gatesT_ready, 1)
            for g in range(KT):
                act.wait_ge(spread_mm, g + 1)
                nc.scalar.copy(gateX[:, g, :], ps[:, 6 + g, :]).then_inc(gateX_ready, 1)
            for tt in range(TT):
                if tt > 0:
                    copy_pT(tt - 1)
                act.wait_ge(arg_ready, tt + 1)
                nc.scalar.activation(p[tt % 2][:], p[tt % 2][:], ACT.Exp).then_inc(exp_done, 1)
            copy_pT(TT - 1)

        @block.vector
        def _(dve):
            step = Chain(dve, dve_step)
            norm_stats(nc, step, x, stats, mv, var, TT, var_ready)
            dve.wait_ge(rstd_ready, 1)
            norm_apply(nc, h, x, mv, rstd, TT).then_inc(h_ready, 1)
            for g in range(KT):
                dve.wait_ge(qk_mm, g + 1)
                nc.vector.tensor_scalar(qT[:, g, :], ps[:, 2 + g, :], col("L0_attn_bqk", g), HD ** -0.5,
                                        ALU.add, ALU.mult).then_inc(q_ready, 1)
            for tt in range(TT):
                dve.wait_ge(keys_mm, 2 * (tt // 2 + 1))
                last = nc.vector.tensor_tensor(out=keys[:, tt, :], in0=ps[:, 6 + tt // 2, (tt % 2) * D:(tt % 2 + 1) * D],
                                               in1=row("L0_attn_bqk", D, D), op=ALU.add)
            last.then_inc(keys_ready, 1)
            step.link(nc.vector.tensor_reduce(out=own_half[:], in_=head_mask[:].rearrange("p (j two) -> p two j", two=2),
                                              axis=AX.X, op=ALU.add))
            dve.wait_ge(gate_mm, 1)
            step.link(nc.vector.tensor_tensor(out=gates[:], in0=ps[:, 0, 0:TT * H].rearrange("p (t h) -> p t h", t=TT),
                                              in1=row("L0_attn_bgate").unsqueeze(1).to_broadcast([P, TT, H]), op=ALU.add))
            softmax_rows(nc, step, gates[:], H, top[:, 0:TT]).then_inc(gate_arg, 1)
            dve.wait_ge(gate_exp, 1)
            normalise_rows(nc, step, gates[:], total[:, 0:TT]).then_inc(gates_ready, 1)

            def scores_to_args(tt):
                dve.wait_ge(score_mm, tt + 1)
                if tt >= 2:
                    dve.wait_ge(p_turned, 2 * (tt - 1))
                pt = p[tt % 2]
                for b in range(2):
                    last = nc.vector.tensor_tensor(out=pt[:, :, b, :], in0=scores[:, b, :, b * N:(b + 1) * N],
                                                   in1=band[:], op=ALU.add)
                last.then_inc(score_read, 1)
                dve.wait_ge(score_read, tt + 1)
                softmax_rows(nc, step, pt[:].rearrange("p a b n -> p (a b) n"), N, top[:]).then_inc(arg_ready, 1)

            def args_to_p(tt):
                dve.wait_ge(exp_done, tt + 1)
                normalise_rows(nc, step, p[tt % 2][:].rearrange("p a b n -> p (a b) n"), total[:]).then_inc(p_ready, 1)

            def finish(tt):
                dve.wait_ge(out_mm, tt + 1)
                if tt == 0:
                    dve.wait_ge(gateX_ready, KT)
                if tt >= 2:
                    dve.wait_ge(proj_mm, tt - 1)
                o = outT[tt % 2]
                for b in range(2):
                    last = nc.vector.tensor_scalar(o[:, :, b * N:(b + 1) * N], outs[:, b, :, 0:N], own_half[:, 0:1], None, ALU.mult)
                step.link(last)
                for b in range(2):
                    part = o[:, :, b * N:(b + 1) * N]
                    last = nc.vector.scalar_tensor_tensor(out=part, in0=outs[:, b, :, N:P], scalar=own_half[:, 1:2], in1=part,
                                                          op0=ALU.mult, op1=ALU.add)
                step.link(last)
                nc.vector.tensor_tensor(out=o[:], in0=o[:], in1=gateX[:, :, tt * P:(tt + 1) * P], op=ALU.mult).then_inc(outT_ready, 1)

            def residual(tt):
                dve.wait_ge(proj_mm, tt + 1)
                step.link(nc.vector.tensor_tensor(out=x[:, tt, :], in0=ps[:, 5, 0:D], in1=x[:, tt, :], op=ALU.add))
                nc.vector.tensor_tensor(out=x[:, tt, :], in0=x[:, tt, :], in1=row("L0_attn_bproj"), op=ALU.add).then_inc(x_added, 1)

            scores_to_args(0)
            for tt in range(TT):
                args_to_p(tt)
                if tt + 1 < TT:
                    scores_to_args(tt + 1)
                finish(tt)
                residual(tt)

        @block.tensor
        def _(pe):
            pe.wait_ge(h_ready, 1)
            for k in range(KT):
                for t in range(TT):
                    last = nc.tensor.transpose(ps[:, k, t * P:(t + 1) * P], h[:, t, k * P:(k + 1) * P], ident[:])
                last.then_inc(h_turned, 1)
            pe.wait_ge(hT_ready, KT)
            pe.wait_ge(w_loaded, 48)
            for n in range(2 * KT):
                for k in range(KT):
                    last = nc.tensor.matmul(ps[:, 2 + n, :], wqk[:, k, n * P:(n + 1) * P], hT[:, k, :],
                                            start=k == 0, stop=k == KT - 1)
                last.then_inc(qk_mm, 1)
            for tt in range(TT):
                for k in range(KT):
                    last = nc.tensor.matmul(ps[:, 6 + tt // 2, (tt % 2) * D:(tt % 2 + 1) * D], hT[:, k, tt * P:(tt + 1) * P],
                                            wqk[:, k, D:2 * D], start=k == 0, stop=k == KT - 1)
                last.then_inc(keys_mm, 1)
            for tt in range(TT):
                for k in range(KT):
                    last = nc.tensor.matmul(ps[:, 0, tt * H:(tt + 1) * H], hT[:, k, tt * P:(tt + 1) * P], wgate[:, k, :],
                                            start=k == 0, stop=k == KT - 1)
            last.then_inc(gate_mm, 1)
            pe.wait_ge(q_ready, KT)
            pe.wait_ge(k_ready, KT)
            pe.wait_ge(gate_arg, 1)

            def spread_gates():
                pe.wait_ge(gates_ready, 1)
                for tt in range(TT):
                    last = nc.tensor.matmul(ps[0:H, 4, tt * P:(tt + 1) * P], gates[:, tt, :], ident[:], start=True, stop=True)
                last.then_inc(gates_turned, 1)
                pe.wait_ge(gatesT_ready, 1)
                pe.wait_ge(consts, 1)
                pe.wait_ge(keys_ready, 1)
                for g in range(KT):
                    nc.tensor.matmul(ps[:, 6 + g, :], spread[:, g * P:(g + 1) * P], gatesT[:], start=True, stop=True).then_inc(spread_mm, 1)
                pe.wait_ge(gateX_ready, KT)

            def score(tt):
                pe.wait_ge(qblk_ready, tt + 1)
                if tt > 0:
                    pe.wait_ge(score_read, tt)
                for b in range(2):
                    for pair in range(NPAIR):
                        g, j = pair // 4, pair % 4
                        last = nc.tensor.matmul(scores[:, b, pair, :], qblk[tt % 2][:, b, g, 2 * j:2 * j + 2, :].rearrange("p a n -> p (a n)"),
                                                kT[:, g, tt * P:(tt + 1) * P], start=True, stop=True)
                last.then_inc(score_mm, 1)

            def weigh(tt):
                pe.wait_ge(p_ready, tt + 1)
                for n in range(2):
                    if tt > 0:
                        pe.wait_ge(pT_ready, 2 * (tt - 1) + n + 1)
                        if n == 1:
                            pe.wait_ge(x_added, tt)
                    for j in range(4):
                        last = nc.tensor.transpose(ps[:, 4 + n, j * P:(j + 1) * P],
                                                   p[tt % 2][:, 4 * n + j].rearrange("p b n -> p (b n)"), ident[:])
                    last.then_inc(p_turned, 1)
                pe.wait_ge(pT_ready, 2 * (tt + 1))
                if tt > 0:
                    pe.wait_ge(outT_ready, tt)
                for b in range(2):
                    for pair in range(NPAIR):
                        g, j = pair // 4, pair % 4
                        last = nc.tensor.matmul(outs[32 * j:32 * j + 32, b, g, :], keys[64 * b:64 * b + 64, tt, pair * 32:(pair + 1) * 32],
                                                pT[tt % 2][64 * b:64 * b + 64, pair, :], start=True, stop=True)
                last.then_inc(out_mm, 1)

            def project(tt):
                pe.wait_ge(outT_ready, tt + 1)
                for g in range(KT):
                    last = nc.tensor.matmul(ps[:, 5, 0:D], outT[tt % 2][:, g, :], wproj[:, g, :], start=g == 0, stop=g == KT - 1)
                last.then_inc(proj_mm, 1)

            score(0)
            spread_gates()
            for tt in range(TT):
                if tt + 1 < TT:
                    score(tt + 1)
                weigh(tt)
                project(tt)


def experts_0(own, nc, A, sb, sem, x, cols, rows, ident, head_mask, band, ps, col, row, finished, ahead, spiral):
    HT = H0 // P
    h = sb("e0_h", [P, TT, D], own)
    hT = sb("e0_hT", [P, KT, T], own)
    wgate = sb("e0_wgate", [P, KT, E], own)
    hT_hi = sb("e0_hT_hi", [P, KT, T], own, F32R)
    hT_lo = sb("e0_hT_lo", [P, KT, T], own, F32R)
    w1 = sb("e0_w1", [P, KT, H0], own)
    w2 = sb("e0_w2", [P, HT, D], own)
    w1_hi, w1_lo = ([sb(f"e0_w1_{part}{i}", [P, KT, H0], own, F32R) for i in range(2)] for part in ("hi", "lo"))
    w2_hi, w2_lo = ([sb(f"e0_w2_{part}{i}", [P, HT, D], own, F32R) for i in range(2)] for part in ("hi", "lo"))
    b1 = sb("e0_b1", [P, E * H0], own)
    b2 = sb("e0_b2", [E, D], own)
    gates = sb("e0_gates", [P, TT, E], own)
    chosen = sb("e0_chosen", [P, TT, E], own)
    chosenT = sb("e0_chosenT", [E, T], own)
    rank = sb("e0_rank", [P, E], own)
    work = sb("e0_work", [P, 3, TT, E], own)
    best = sb("e0_best", [P, 3, TT], own)
    hn = [sb(f"e0_hn{i}", [P, H0], own) for i in range(2)]
    gelu = [sb(f"e0_gelu{i}", [P, HT, P], own) for i in range(2)]
    act_hi = [sb(f"e0_act_hi{i}", [P, HT, P], own, F32R) for i in range(2)]
    act_lo = [sb(f"e0_act_lo{i}", [P, HT, P], own, F32R) for i in range(2)]
    acc = sb("e0_acc", [P, TT, D], own)
    stats = sb("e0_stats", [P, TT, 6], own)
    mv = sb("e0_mv", [P, TT, 2], own)
    var = sb("e0_var", [P, TT], own)
    rstd = sb("e0_rstd", [P, TT], own)
    half = sb("e0_half", [P, TT], own)
    top = sb("e0_top", [P, TT], own)
    total = sb("e0_total", [P, TT], own)

    hT_split = sem("e0_hT_split"); w_rounded = sem("e0_w_rounded"); w_split = sem("e0_w_split")
    act_rounded = sem("e0_act_rounded"); act_split = sem("e0_act_split")
    act_passed = sem("e0_act_passed"); dve_passed = sem("e0_dve_passed")
    ahead_loaded = sem("e0_ahead")
    small_loaded = sem("e0_small"); b1_loaded = sem("e0_b1_loaded")
    w1_loaded = sem("e0_w1_loaded"); w2_loaded = sem("e0_w2_loaded")
    pool_step = sem("e0_pool_step"); dve_step = sem("e0_dve_step"); var_ready = sem("e0_var")
    rstd_ready = sem("e0_rstd"); h_ready = sem("e0_h_ready"); h_turned = sem("e0_h_turned"); hT_ready = sem("e0_hT_ready")
    gate_mm = sem("e0_gate_mm"); gate_arg = sem("e0_gate_arg"); gate_exp = sem("e0_gate_exp")
    chosen_ready = sem("e0_chosen_ready"); chosen_turned = sem("e0_chosen_turned"); chosenT_ready = sem("e0_chosenT_ready")
    bias_mm = sem("e0_bias_mm"); acc_started = sem("e0_acc_started")
    up_mm = sem("e0_up_mm"); up_read = sem("e0_up_read"); unit_var = sem("e0_unit_var"); unit_rstd = sem("e0_unit_rstd")
    hn_ready = sem("e0_hn_ready"); hn_turned = sem("e0_hn_turned"); gelu_done = sem("e0_gelu")
    down_mm = sem("e0_down_mm"); acc_added = sem("e0_acc_added")

    RING = 2
    PARTS = 4

    def weight_part(m1, m2, j):
        m = (m1, m2)[j // 2].rearrange("p k n -> p (k n)")
        return m[:, (j % 2) * 512:(j % 2) * 512 + 512]

    def experts(eng, turn):
        with eng.Fori(0, E // 2 - 1) as i:
            turn(i, 2 * i + 1, 1)
            turn(i, 2 * i + 2, 0)
        turn(E // 2 - 1, E - 1, 1)

    with nc.Block() as block:
        @block.sync
        def _(sp):
            sp.dma_start(wgate[:], A["L0_ffn_gate_w"].rearrange("(k p) n -> p k n", p=P)).then_inc(small_loaded, 16)
            sp.dma_start(b2[:], A["L0_ffn_b2"]).then_inc(small_loaded, 16)
            sp.dma_start(b1[:], A["L0_ffn_b1"].to_broadcast([P, E * H0])).then_inc(b1_loaded, 16)
            w1_d = A["L0_ffn_w1"].rearrange("e (k p) n -> (e k) p n", p=P)
            w2_d = A["L0_ffn_w2"].rearrange("e (k p) n -> (e k) p n", p=P)
            sp.dma_start(w1[:], w1_d[0:KT].rearrange("k p n -> p k n")).then_inc(w1_loaded, 16)
            sp.dma_start(w2[:], w2_d[0:HT].rearrange("k p n -> p k n")).then_inc(w2_loaded, 16)
            with sp.Fori(1, E) as e:
                sp.wait_ge(w_split, e * PARTS - 2)
                sp.dma_start(w1[:], w1_d[bass.ds(e * KT, KT)].rearrange("k p n -> p k n")).then_inc(w1_loaded, 16)
                sp.wait_ge(w_split, e * PARTS)
                sp.dma_start(w2[:], w2_d[bass.ds(e * HT, HT)].rearrange("k p n -> p k n")).then_inc(w2_loaded, 16)
            load_ahead(sp, ahead, ahead_loaded)

        @block.gpsimd
        def _(pool):
            for s in finished:
                pool.sem_clear(s)
            step = Chain(pool, pool_step)
            step.link(nc.gpsimd.memset(half[:], -0.5))
            pool.wait_ge(var_ready, 1)
            nc.gpsimd.tensor_tensor(out=rstd[:], in0=var[:], in1=half[:], op=ALU.pow).then_inc(rstd_ready, 1)

            def unit_scale(n, c):
                pool.wait_ge(unit_var, n + 1)
                nc.gpsimd.tensor_tensor(out=rstd[:, c:c + 1], in0=var[:, c:c + 1], in1=half[:, c:c + 1], op=ALU.pow).then_inc(unit_rstd, 1)

            def activation_rests(n, c):
                pool.wait_ge(act_rounded, n + 1)
                nc.gpsimd.tensor_tensor(out=act_lo[c][:], in0=gelu[c][:], in1=act_hi[c][:].bitcast(F32), op=ALU.subtract).then_inc(act_split, 1)

            unit_scale(0, 0)
            with pool.Fori(0, E * TT - 2, 2) as n:
                for c in range(2):
                    unit_scale(n + c + 1, 1 - c)
                    activation_rests(n + c, c)
            unit_scale(E * TT - 1, 1)
            for c in range(2):
                activation_rests(E * TT - 2 + c, c)
            pool.wait_ge(var_ready, 2)
            nc.gpsimd.tensor_tensor(out=rstd[:], in0=var[:], in1=half[:], op=ALU.pow).then_inc(rstd_ready, 1)

        @block.scalar
        def _(act):
            act.sem_inc(gelu_done, RING)
            for k in range(KT):
                act.wait_ge(h_turned, k + 1)
                nc.scalar.copy(hT[:, k, :], ps[:, 6 + k, :]).then_inc(hT_ready, 1)
            for j in range(PARTS):
                if j % 2 == 0:
                    act.wait_ge((w1_loaded, w2_loaded)[j // 2], 16)
                nc.scalar.copy(weight_part(w1_hi[0][:], w2_hi[0][:], j), weight_part(w1[:], w2[:], j)).then_inc(w_rounded, 1)
            act.wait_ge(gate_arg, 1)
            nc.scalar.activation(gates[:], gates[:], ACT.Exp).then_inc(gate_exp, 1)
            act.wait_ge(chosen_turned, 1)
            nc.scalar.copy(chosenT[:], ps[0:E, 7, :]).then_inc(chosenT_ready, 1)

            def turn(i, e, a):
                for t in range(TT):
                    n = e * TT + t
                    if not (isinstance(e, int) and e == E - 1):
                        if t % 2 == 0:
                            act.wait_ge((w1_loaded, w2_loaded)[t // 2], 16 * (e + 2))
                            if not isinstance(e, int):
                                act.wait_ge(*((up_mm, e * TT) if t == 0 else (down_mm, e * TT + RING)))
                        nc.scalar.copy(weight_part(w1_hi[1 - a][:], w2_hi[1 - a][:], t), weight_part(w1[:], w2[:], t)).then_inc(w_rounded, 1)
                    act.wait_ge(hn_turned, n + 1 + RING)
                    wait_alone(act, act_passed, act_split, n + 1)
                    for k in range(HT):
                        g_at, b_at = COL_AT["L0_ffn_ln1_g"] + e * HT + k, COL_AT["L0_ffn_ln1_b"] + e * HT + k
                        last = nc.scalar.activation(gelu[t % 2][:, k, :], ps[:, 2 + t % 2, k * P:(k + 1) * P], ACT.Gelu,
                                                    bias=cols[:, bass.ds(b_at, 1)], scale=cols[:, bass.ds(g_at, 1)])
                    last.then_inc(gelu_done, 1)
                    act.wait_ge(gelu_done, n + 1 + RING)
                    act.wait_ge(down_mm, n + 1)
                    nc.scalar.copy(act_hi[t % 2][:], gelu[t % 2][:]).then_inc(act_rounded, 1)

            turn(None, 0, 0)
            experts(act, turn)

        @block.vector
        def _(dve):
            dve.sem_inc(up_read, RING)
            dve.sem_inc(acc_added, RING)
            dve.sem_inc(act_split, RING)
            step = Chain(dve, dve_step)
            for e in range(E):
                last = nc.vector.memset(rank[:, e:e + 1], float(E - e))
            step.link(last)
            norm_stats(nc, step, x, stats, mv, var, TT, var_ready)
            dve.wait_ge(rstd_ready, 1)
            norm_apply(nc, h, x, mv, rstd, TT).then_inc(h_ready, 1)
            for k in range(KT):
                dve.wait_ge(hT_ready, k + 1)
                step.link(nc.vector.tensor_copy(hT_hi[:, k, :], hT[:, k, :]))
                nc.vector.tensor_tensor(out=hT_lo[:, k, :], in0=hT[:, k, :], in1=hT_hi[:, k, :].bitcast(F32), op=ALU.subtract).then_inc(hT_split, 1)

            def weight_rests(e, a, j):
                dve.wait_ge(w_rounded, e * PARTS + j + 1)
                nc.vector.tensor_tensor(out=weight_part(w1_lo[a][:], w2_lo[a][:], j), in0=weight_part(w1[:], w2[:], j),
                                        in1=weight_part(w1_hi[a][:].bitcast(F32), w2_hi[a][:].bitcast(F32), j),
                                        op=ALU.subtract).then_inc(w_split, 1)

            for j in range(PARTS):
                weight_rests(0, 0, j)
            dve.wait_ge(gate_mm, 1)
            step.link(nc.vector.tensor_copy(gates[:], ps[:, 6, 0:TT * E].rearrange("p (t e) -> p t e", t=TT)))
            softmax_rows(nc, step, gates[:], E, top[:]).then_inc(gate_arg, 1)
            dve.wait_ge(gate_exp, 1)
            step.link(normalise_rows(nc, step, gates[:], total[:]))
            top_two(nc, step, gates[:], rank[:], chosen[:], work, best).then_inc(chosen_ready, 1)
            dve.wait_ge(bias_mm, 1)
            for t in range(TT):
                last = nc.vector.tensor_tensor(out=acc[:, t, :], in0=ps[:, 6 + t // 2, (t % 2) * D:(t % 2 + 1) * D], in1=h[:, t, :], op=ALU.add)
            step.link(last)
            step.link(nc.vector.tensor_tensor(out=x[:], in0=x[:], in1=row("L0_ffn_ln_b").unsqueeze(1).to_broadcast([P, TT, D]), op=ALU.add))
            dve.wait_ge(b1_loaded, 16)

            def unit_stats(e, t):
                n = e * TT + t
                hid, c = hn[t % 2], t % 2
                dve.wait_ge(up_mm, n + 1)
                dve.wait_ge(hn_turned, n + 1)
                nc.vector.tensor_tensor(out=hid[:], in0=ps[:, t % 2, :], in1=b1[:, bass.ds(e * H0, H0)], op=ALU.add).then_inc(up_read, 1)
                dve.wait_ge(up_read, n + 1 + RING)
                step.link_alone(nc.vector.bn_stats(stats[:, c, :], hid[:]), dve_passed)
                step.link(nc.vector.bn_aggr(mv[:, c, :], stats[:, c, :]))
                nc.vector.tensor_scalar(var[:, c:c + 1], mv[:, c, 1:2], EPS, None, ALU.add).then_inc(unit_var, 1)

            def norm_unit(e, t):
                n = e * TT + t
                hid, c = hn[t % 2], t % 2
                dve.wait_ge(unit_rstd, n + 1)
                nc.vector.tensor_scalar(hid[:], hid[:], mv[:, c, 0:1], rstd[:, c:c + 1],
                                        ALU.subtract, ALU.mult).then_inc(hn_ready, 1)

            def add_unit(e, t):
                n = e * TT + t
                dve.wait_ge(down_mm, n + 1 + RING)
                nc.vector.scalar_tensor_tensor(out=acc[:, t, :], in0=ps[:, 4 + t % 2, 0:D],
                                               scalar=chosen[:].rearrange("p t e -> p (t e)")[:, bass.ds(t * E + e, 1)],
                                               in1=acc[:, t, :], op0=ALU.mult, op1=ALU.add).then_inc(acc_added, 1)

            def turn(i, e, a):
                if i is not None:
                    step.base, step.n = i * 2 * LINKS, first + (1 - a) * LINKS
                for t in range(TT):
                    unit_stats(e, t)
                    if t >= 1 and not (isinstance(e, int) and e == E - 1):
                        weight_rests(e + 1, 1 - a, t - 1)
                    elif t == 0 and i is not None:
                        weight_rests(e, a, PARTS - 1)
                    if t >= 2:
                        add_unit(e, t - 2)
                    elif i is not None:
                        add_unit(e - 1, t + 2)
                    norm_unit(e, t)

            LINKS = 2 * TT
            turn(None, 0, 0)
            first = step.n
            experts(dve, turn)
            assert step.n == first + LINKS
            add_unit(E - 1, 2)
            add_unit(E - 1, 3)
            dve.wait_ge(acc_added, E * TT + RING)
            add_norm(nc, dve, step, x, acc, row("L0_ffn_ln_g"), stats, mv, rstd, var, var_ready, rstd_ready)

        @block.tensor
        def _(pe):
            pe.sem_inc(hn_turned, RING)
            pe.sem_inc(down_mm, RING)
            pe.wait_ge(h_ready, 1)
            for k in range(KT):
                for t in range(TT):
                    last = nc.tensor.transpose(ps[:, 6 + k, t * P:(t + 1) * P], h[:, t, k * P:(k + 1) * P], ident[:])
                last.then_inc(h_turned, 1)
            pe.wait_ge(hT_ready, KT)
            pe.wait_ge(small_loaded, 32)
            for t in range(TT):
                for k in range(KT):
                    last = nc.tensor.matmul(ps[:, 6, t * E:(t + 1) * E], hT[:, k, t * P:(t + 1) * P], wgate[:, k, :],
                                            start=k == 0, stop=k == KT - 1)
            last.then_inc(gate_mm, 1)

            def up(e, a, t):
                n = e * TT + t
                pe.wait_ge(up_read, n + 1)
                for k in range(KT):
                    at = (slice(None), k, slice(t * P, (t + 1) * P))
                    last = split_matmul(nc, ps[:, t % 2, :], (hT_hi[at], hT_lo[at]), (w1_hi[a][:, k, :], w1_lo[a][:, k, :]),
                                        k == 0, k == KT - 1)
                last.then_inc(up_mm, 1)

            def turn_hidden(e, t):
                n = e * TT + t
                pe.wait_ge(hn_ready, n + 1)
                pe.wait_ge(gelu_done, n + 1)
                for k in range(HT):
                    last = nc.tensor.transpose(ps[:, 2 + t % 2, k * P:(k + 1) * P], hn[t % 2][:, k * P:(k + 1) * P], ident[:])
                last.then_inc(hn_turned, 1)

            def down(e, a, t):
                n = e * TT + t
                pe.wait_ge(act_split, n + 1 + RING)
                pe.wait_ge(acc_added, n + 1)
                for k in range(HT):
                    last = split_matmul(nc, ps[:, 4 + t % 2, 0:D], (act_hi[t % 2][:, k, :], act_lo[t % 2][:, k, :]),
                                        (w2_hi[a][:, k, :], w2_lo[a][:, k, :]), k == 0, k == HT - 1)
                last.then_inc(down_mm, 1)

            pe.wait_ge(hT_split, KT)
            pe.wait_ge(w_split, 2)
            up(0, 0, 0)
            up(0, 0, 1)
            pe.wait_ge(chosen_ready, 1)
            for t in range(TT):
                last = nc.tensor.matmul(ps[0:E, 7, t * P:(t + 1) * P], chosen[:, t, :], ident[:], start=True, stop=True)
            last.then_inc(chosen_turned, 1)
            pe.wait_ge(chosenT_ready, 1)
            for t in range(TT):
                last = nc.tensor.matmul(ps[:, 6 + t // 2, (t % 2) * D:(t % 2 + 1) * D], chosenT[:, t * P:(t + 1) * P], b2[:],
                                        start=True, stop=True)
            last.then_inc(bias_mm, 1)
            pe.wait_ge(w_split, PARTS)
            turn_hidden(0, 0)
            up(0, 0, 2)
            turn_hidden(0, 1)
            down(0, 0, 0)
            up(0, 0, 3)
            turn_hidden(0, 2)
            down(0, 0, 1)

            def turn(i, e, a):
                for t in range(TT):
                    if t % 2 == 0:
                        pe.wait_ge(w_split, e * PARTS + 2 + t)
                    up(e, a, t)
                    if t >= 1:
                        turn_hidden(e, t - 1)
                        down(*((e, a, t - 2) if t >= 2 else (e - 1, 1 - a, t + 2)))
                    else:
                        turn_hidden(e - 1, TT - 1)
                        down(e - 1, 1 - a, t + 2)

            experts(pe, turn)
            turn_hidden(E - 1, TT - 1)
            down(E - 1, 1, TT - 2)
            down(E - 1, 1, TT - 1)


def cross_attention_1_ahead(sb, stack, A):
    raw = [sb(f"x1_raw{i}", [P, ST, D], stack) for i in range(2)]
    w = {n: sb(f"x1_w{n}", [P, KT, D], stack) for n in "qkvo"}
    loads = [(w[n][:], A[f"L1_xattn_W{n}T"].rearrange("(k p) n -> p k n", p=P)) for n in "qkvo"]
    loads += [(raw[b][:], A["ctx_1024"][b].rearrange("(t p) d -> p t d", p=P)) for b in range(2)]
    return {"raw": raw, "w": w, "loads": loads}


def cross_attention_1(own, nc, A, sb, sem, x, cols, rows, ident, head_mask, band, ps, col, row, finished, ahead, spiral):
    HD = D // H
    PB = NPAIR
    ITEMS = 12
    h = sb("x1_h", [P, TT, D], own)
    hT = sb("x1_hT", [P, KT, T], own)
    raw = ahead["raw"]
    wq, wk, wv, wo = (ahead["w"][n] for n in "qkvo")
    wk_hi, wv_hi = (sb(f"x1_w{n}_hi", [P, KT, D], own, F32R) for n in "kv")
    wk_lo, wv_lo = (sb(f"x1_w{n}_lo", [P, KT, D], own, F32R) for n in "kv")
    qT = h[:].rearrange("p t d -> p (t d)").rearrange("p (k t) -> p k t", k=KT)
    qT_hi = sb("x1_qT_hi", [P, KT, T], own)
    qblk_hi = [sb(f"x1_qblk_hi{i}", [P, KT, 8, N], own, F32R) for i in range(2)]
    qblk_lo = [sb(f"x1_qblk_lo{i}", [P, KT, 8, N], own, F32R) for i in range(2)]
    cT_hi = sb("x1_cT_hi", [P, KT, S], own, F32R)
    cT_lo = sb("x1_cT_lo", [P, KT, S], own, F32R)
    kT_hi = [sb(f"x1_kT_hi{i}", [P, KT, S], own, F32R) for i in range(2)]
    kT_lo = [sb(f"x1_kT_lo{i}", [P, KT, S], own, F32R) for i in range(2)]
    v = [sb(f"x1_v{i}", [P, ST, D], own) for i in range(2)]
    p = [sb(f"x1_p{i}", [P, S], own) for i in range(2)]
    p_hi = [sb(f"x1_p_hi{i}", [P, S], own, F16) for i in range(2)]
    p_lo = [sb(f"x1_p_lo{i}", [P, S], own, F16) for i in range(2)]
    small_ident = sb("x1_small_ident", [P, P], own, F16)
    pT = [sb(f"x1_pT{i}", [P, 4, ST, P], own) for i in range(2)]
    outT = sb("x1_outT", [P, KT, T], own)
    neg_top = sb("x1_neg_top", [P, 2], own)
    total = sb("x1_total", [P, 2], own)
    recip = sb("x1_recip", [P, 2], own)
    part = sb("x1_part", [P, N], own)
    own_half = sb("x1_own_half", [P, 2], own)
    stats = sb("x1_stats", [P, TT, 6], own)
    mv = sb("x1_mv", [P, TT, 2], own)
    var = sb("x1_var", [P, TT], own)
    rstd = sb("x1_rstd", [P, TT], own)
    half = sb("x1_half", [P, TT], own)

    ctx_loaded = sem("x1_ctx_loaded"); pool_step = sem("x1_pool_step")
    dve_step = sem("x1_dve_step"); var_ready = sem("x1_var"); rstd_ready = sem("x1_rstd")
    h_ready = sem("x1_h_ready"); h_turned = sem("x1_h_turned"); hT_ready = sem("x1_hT_ready")
    q_mm = sem("x1_q_mm"); qT_ready = sem("x1_qT_ready"); qblk_ready = sem("x1_qblk_ready")
    item_mm = sem("x1_item_mm"); item_read = sem("x1_item_read")
    score_mm = sem("x1_score_mm"); max_ready = sem("x1_max_ready"); exp_done = sem("x1_exp_done")
    p_normed = sem("x1_p_normed"); w_rounded = sem("x1_w_rounded"); w_split = sem("x1_w_split"); q_split = sem("x1_q_split")
    item_rest = sem("x1_item_rest"); recip_ready = sem("x1_recip"); p_rounded = sem("x1_p_rounded")
    p_split = sem("x1_p_split"); p_turned = sem("x1_p_turned")
    pT_act = sem("x1_pT_act"); pT_dve = sem("x1_pT_dve"); value_mm = sem("x1_value_mm")
    outT_ready = sem("x1_outT_ready"); proj_mm = sem("x1_proj_mm")

    SCALE = 2.0 ** 14
    score_ps = [ps[:, 2 * a:2 * a + 2, :] for a in range(2)]

    def item_bank(k, first):
        return ps[:, k % 4, :] if first else ps[:, 7, :]

    ctx_d = A["ctx_1024"].rearrange("b (t p) d -> b p t d", p=P)

    with nc.Block() as block:
        @block.sync
        def _(sp):
            sp.sem_inc(ctx_loaded, 32)
            with sp.Fori(0, TT - 1) as i:
                for a in range(2):
                    b = 2 * i + a
                    sp.wait_ge(item_mm, ITEMS * b + 4)
                    sp.wait_ge(ctx_loaded, 16 * (b + 2))
                    sp.dma_start(raw[a][:], ctx_d[bass.ds(b + 2, 1)].rearrange("b p t d -> (b p) t d")).then_inc(ctx_loaded, 16)

        @block.gpsimd
        def _(pool):
            for s in finished:
                pool.sem_clear(s)
            step = Chain(pool, pool_step)
            pool.sem_inc(p_split, 1)
            step.link(nc.gpsimd.memset(half[:], -0.5))
            step.link(nc.gpsimd.tensor_scalar(small_ident[:], ident[:], 1 / SCALE, None, ALU.mult))
            pool.wait_ge(var_ready, 1)
            nc.gpsimd.tensor_tensor(out=rstd[:], in0=var[:], in1=half[:], op=ALU.pow).then_inc(rstd_ready, 1)

            def queries(b, a, n):
                g, (blk, src) = n // 2, ((qblk_hi, qT_hi), (qblk_lo, qT))[n % 2]
                q = src[:, g, :][:, bass.ds(b * N, N)].unsqueeze(1).to_broadcast([P, 8, N])
                step.link(nc.gpsimd.tensor_tensor(out=blk[a][:, g], in0=head_mask[:].unsqueeze(2).to_broadcast([P, 8, N]),
                                                  in1=q, op=ALU.mult))
                if n == 3:
                    pool.sem_inc(qblk_ready, 1)

            for n, (w, w_hi, w_lo) in enumerate(((wk, wk_hi, wk_lo), (wv, wv_hi, wv_lo))):
                pool.wait_ge(w_rounded, n + 1)
                nc.gpsimd.tensor_tensor(out=w_lo[:], in0=w[:], in1=w_hi[:].bitcast(F32), op=ALU.subtract).then_inc(w_split, 1)
            pool.wait_ge(q_split, KT)
            for n in range(4):
                queries(0, 0, n)
            first = step.n

            def probability_rests(n, c):
                pool.wait_ge(p_rounded, n + 1)
                nc.gpsimd.tensor_tensor(out=p_lo[c][:], in0=p[c][:], in1=p_hi[c][:], op=ALU.subtract).then_inc(p_split, 1)

            def turn(i, last):
                step.base, step.n = i * 4 * KT, first
                for a in range(2):
                    for s in range(PB):
                        probability_rests((2 * i + a) * PB + s, s % 2)
                        if 1 <= s <= 4 and not (last and a == 1):
                            if s == 1:
                                pool.wait_ge(score_mm, (2 * i + a + 1) * PB)
                            queries(2 * i + a + 1, (a + 1) % 2, s - 1)

            with pool.Fori(0, TT - 1) as i:
                turn(i, False)
            turn(TT - 1, True)

        @block.scalar
        def _(act):
            act.sem_inc(pT_act, 1)
            for k in range(KT):
                act.wait_ge(h_turned, k + 1)
                nc.scalar.copy(hT[:, k, :], ps[:, k, :]).then_inc(hT_ready, 1)

            def read_item(b, a, k, first=False):
                item_ps = item_bank(k, first)
                act.wait_ge(item_mm, ITEMS * b + k + 1)
                if k < 4:
                    ins = nc.scalar.copy(cT_hi[:, k % 2, (k // 2) * 512:(k // 2) * 512 + 512], item_ps)
                elif k < 8:
                    g, half_ = k % 2, (k - 4) // 2
                    ins = nc.scalar.activation(kT_hi[a][:, g, half_ * 512:half_ * 512 + 512], item_ps, ACT.Identity,
                                               bias=col("L1_xattn_bk", g))
                else:
                    ins = nc.scalar.copy(v[a][:, 2 * (k - 8):2 * (k - 8) + 2, :], item_ps.rearrange("p (t d) -> p t d", t=2))
                ins.then_inc(item_read, 1)

            def exponentials(n, c):
                act.wait_ge(max_ready, n + 1)
                nc.scalar.activation(p[c][:], score_ps[c].rearrange("p a s -> p (a s)"), ACT.Exp, bias=neg_top[:, c:c + 1],
                                     accum_out=total[:, c:c + 1]).then_inc(exp_done, 1)

            def normalise_probabilities(n, c):
                act.wait_ge(recip_ready, n + 1)
                nc.scalar.activation(p[c][:], p[c][:], ACT.Copy, scale=recip[:, c:c + 1]).then_inc(p_normed, 1)

            for w, w_hi in ((wk, wk_hi), (wv, wv_hi)):
                nc.scalar.copy(w_hi[:], w[:]).then_inc(w_rounded, 1)
            for k in range(ITEMS):
                read_item(0, 0, k, first=True)
            exponentials(0, 0)
            exponentials(1, 1)
            for c in range(2):
                normalise_probabilities(c, c)

            def turn(i, last):
                for a in range(2):
                    for s in range(PB):
                        n = (2 * i + a) * PB + s
                        more = not (last and a == 1 and s >= PB - 2)
                        items = not (last and a == 1) and s < 6
                        if items:
                            read_item(2 * i + a + 1, (a + 1) % 2, 2 * s)
                        if more:
                            act.wait_ge(p_split, n + 2)
                            exponentials(n + 2, s % 2)
                        act.wait_ge(p_turned, 2 * n + 3)
                        act.wait_ge(value_mm, 4 * i + 2 * a + s // 4 + 1)
                        nc.scalar.copy(pT[s // 4][:, s % 4, 0:4, :], ps[:, 4, :].rearrange("p (t c) -> p t c", t=4)).then_inc(pT_act, 1)
                        if items:
                            read_item(2 * i + a + 1, (a + 1) % 2, 2 * s + 1)
                        if more:
                            normalise_probabilities(n + 2, s % 2)

            with act.Fori(0, TT - 1) as i:
                turn(i, False)
            turn(TT - 1, True)

        @block.vector
        def _(dve):
            step = Chain(dve, dve_step)
            dve.sem_inc(pT_dve, 1)
            dve.sem_inc(outT_ready, 1)
            norm_stats(nc, step, x, stats, mv, var, TT, var_ready)
            step.link(nc.vector.tensor_reduce(out=own_half[:], in_=head_mask[:].rearrange("p (j two) -> p two j", two=2),
                                              axis=AX.X, op=ALU.add))
            dve.wait_ge(rstd_ready, 1)
            norm_apply(nc, h, x, mv, rstd, TT).then_inc(h_ready, 1)
            for g in range(KT):
                dve.wait_ge(q_mm, g + 1)
                nc.vector.tensor_scalar(qT[:, g, :], ps[:, 2 + g, :], col("L1_xattn_bq", g), HD ** -0.5,
                                        ALU.add, ALU.mult).then_inc(qT_ready, 1)
                dve.wait_ge(qT_ready, g + 1)
                step.link(nc.vector.tensor_copy(qT_hi[:, g, :].bitcast(F32R), qT[:, g, :]))
                nc.vector.tensor_tensor(out=qT[:, g, :], in0=qT[:, g, :], in1=qT_hi[:, g, :], op=ALU.subtract).then_inc(q_split, 1)

            def maximum(n, c):
                dve.wait_ge(score_mm, n + 1 + PB)
                nc.vector.tensor_reduce(out=neg_top[:, c:c + 1], in_=score_ps[c], axis=AX.XY, op=ALU.max,
                                        negate=True).then_inc(max_ready, 1)

            def denominator(n, c):
                dve.wait_ge(exp_done, n + 1)
                step.link(nc.vector.reciprocal(recip[:, c:c + 1], total[:, c:c + 1]))
                nc.vector.tensor_scalar(recip[:, c:c + 1], recip[:, c:c + 1], SCALE, None, ALU.mult).then_inc(recip_ready, 1)

            def round_probabilities(n, c):
                dve.wait_ge(p_normed, n + 1)
                nc.vector.tensor_copy(p_hi[c][:], p[c][:]).then_inc(p_rounded, 1)

            def item_rests(b, a, k, first=False):
                item_ps = item_bank(k, first)
                if k < 8:
                    dve.wait_ge(item_read, ITEMS * b + k + 1)
                    g, at = k % 2, slice((k % 4) // 2 * 512, (k % 4) // 2 * 512 + 512)
                    if k < 4:
                        ins = nc.vector.tensor_tensor(out=cT_lo[:, g, at], in0=item_ps, in1=cT_hi[:, g, at].bitcast(F32), op=ALU.subtract)
                    else:
                        ins = nc.vector.scalar_tensor_tensor(out=kT_lo[a][:, g, at], in0=item_ps, scalar=col("L1_xattn_bk", g),
                                                             in1=kT_hi[a][:, g, at].bitcast(F32), op0=ALU.add, op1=ALU.subtract)
                    ins.then_inc(item_rest, 1)

            def keep_own(i, a, g):
                group = 4 * i + 2 * a + g
                dve.wait_ge(value_mm, group + 3)
                src = ps[:, 6, g * P:(g + 1) * P]
                step.link(nc.vector.tensor_scalar(part[:], src[:, 0:N], own_half[:, 0:1], col("L1_xattn_bv", g), ALU.mult, ALU.add))
                nc.vector.scalar_tensor_tensor(out=outT[:, g, :][:, bass.ds((2 * i + a) * N, N)], in0=src[:, N:P],
                                               scalar=own_half[:, 1:2], in1=part[:], op0=ALU.mult, op1=ALU.add).then_inc(outT_ready, 1)
                dve.wait_ge(outT_ready, group + 2)

            for k in range(8):
                item_rests(0, 0, k, first=True)
            maximum(0, 0)
            maximum(1, 1)
            denominator(0, 0)
            denominator(1, 1)
            round_probabilities(0, 0)
            first = step.n

            def turn(i, last):
                step.base, step.n = i * LINKS, first
                for a in range(2):
                    for s in range(PB):
                        n = (2 * i + a) * PB + s
                        items = not (last and a == 1) and s < 6
                        if not (last and a == 1 and s >= PB - 2):
                            maximum(n + 2, s % 2)
                        if not (last and a == 1 and s == PB - 1):
                            round_probabilities(n + 1, (s + 1) % 2)
                        if items:
                            item_rests(2 * i + a + 1, (a + 1) % 2, 2 * s)
                        dve.wait_ge(p_turned, 2 * n + 4)
                        dve.wait_ge(value_mm, 4 * i + 2 * a + s // 4 + 1)
                        nc.vector.tensor_copy(pT[s // 4][:, s % 4, 4:8, :], ps[:, 5, :].rearrange("p (t c) -> p t c", t=4)).then_inc(pT_dve, 1)
                        if items:
                            item_rests(2 * i + a + 1, (a + 1) % 2, 2 * s + 1)
                        if not (last and a == 1 and s >= PB - 2):
                            denominator(n + 2, s % 2)
                        if s % 4 == 3:
                            keep_own(i, a, s // 4)

            LINKS = 2 * PB + 4
            with dve.Fori(0, TT - 1) as i:
                turn(i, False)
            assert step.n == first + LINKS
            turn(TT - 1, True)
            for t in range(TT):
                dve.wait_ge(proj_mm, 2 * (t // 2 + 1))
                step.link(nc.vector.tensor_tensor(out=x[:, t, :], in0=ps[:, t // 2, (t % 2) * D:(t % 2 + 1) * D], in1=x[:, t, :], op=ALU.add))
            nc.vector.tensor_tensor(out=x[:], in0=x[:], in1=row("L1_xattn_bo").unsqueeze(1).to_broadcast([P, TT, D]), op=ALU.add)

        @block.tensor
        def _(pe):
            pe.sem_inc(value_mm, 2)
            pe.sem_inc(p_turned, 2)
            pe.sem_inc(score_mm, PB)
            pe.wait_ge(h_ready, 1)
            for k in range(KT):
                for t in range(TT):
                    last = nc.tensor.transpose(ps[:, k, t * P:(t + 1) * P], h[:, t, k * P:(k + 1) * P], ident[:])
                last.then_inc(h_turned, 1)
            pe.wait_ge(hT_ready, KT)
            for g in range(KT):
                for k in range(KT):
                    last = nc.tensor.matmul(ps[:, 2 + g, :], wq[:, k, g * P:(g + 1) * P], hT[:, k, :],
                                            start=k == 0, stop=k == KT - 1)
                last.then_inc(q_mm, 1)

            def item(b, a, k, first=False):
                item_ps = item_bank(k, first)
                if first:
                    need = max(k - 3, 0 if k < 4 else 2 if k < 6 else 4)
                    if need > 0:
                        pe.wait_ge(item_read, need)
                        pe.wait_ge(item_rest, min(need, 8))
                else:
                    pe.wait_ge(item_read, ITEMS * b + k)
                    if 1 <= k <= 8:
                        pe.wait_ge(item_rest, 8 * b + k)
                if k < 4:
                    if k == 0 and not first:
                        pe.wait_ge(ctx_loaded, 16 * (b + 1))
                    for t in range(4):
                        last = nc.tensor.transpose(item_ps[:, t * P:(t + 1) * P],
                                                   raw[a][:, 4 * (k // 2) + t, (k % 2) * P:(k % 2 + 1) * P], ident[:])
                elif k < 8:
                    g, half_ = k % 2, (k - 4) // 2
                    for kk in range(KT):
                        at, w_at = (slice(None), kk, slice(half_ * 512, half_ * 512 + 512)), (slice(None), kk, slice(g * P, (g + 1) * P))
                        last = split_matmul(nc, item_ps, (wk_hi[w_at], wk_lo[w_at]), (cT_hi[at], cT_lo[at]), kk == 0, kk == KT - 1)
                else:
                    for t in range(2):
                        st = 2 * (k - 8) + t
                        for kk in range(KT):
                            at, w_at = (slice(None), kk, slice(st * P, (st + 1) * P)), (slice(None), kk)
                            last = split_matmul(nc, item_ps[:, t * D:(t + 1) * D], (cT_hi[at], cT_lo[at]), (wv_hi[w_at], wv_lo[w_at]),
                                                kk == 0, kk == KT - 1)
                last.then_inc(item_mm, 1)

            def score(n, a, s):
                g, j = s // 4, s % 4
                queries = [blk[a][:, g, 2 * j:2 * j + 2, :].rearrange("p a n -> p (a n)") for blk in (qblk_hi, qblk_lo)]
                for c in range(2):
                    at = (slice(None), g, slice(c * 512, (c + 1) * 512))
                    last = split_matmul(nc, score_ps[s % 2][:, c, :], queries, (kT_hi[a][at], kT_lo[a][at]), True, True)
                last.then_inc(score_mm, 1)

            pe.wait_ge(qT_ready, KT)
            for k in range(ITEMS):
                if k == 4:
                    pe.wait_ge(w_split, 2)
                item(0, 0, k, first=True)
            pe.wait_ge(qblk_ready, 1)
            pe.wait_ge(item_read, ITEMS)
            pe.wait_ge(item_rest, 8)
            score(0, 0, 0)
            score(1, 0, 1)

            def turn(i, last):
                for a in range(2):
                    b = 2 * i + a
                    for s in range(PB):
                        n = b * PB + s
                        items = not (last and a == 1) and s < 6
                        if not (last and a == 1 and s >= PB - 2):
                            pe.wait_ge(exp_done, n + 1)
                            if s == PB - 2:
                                pe.wait_ge(qblk_ready, b + 2)
                                pe.wait_ge(item_read, ITEMS * (b + 1) + 8)
                            score(n + 2, a if s < PB - 2 else (a + 1) % 2, (s + 2) % PB)
                        if items:
                            item(b + 1, (a + 1) % 2, 2 * s)
                        pe.wait_ge(p_split, n + 2)
                        for hf in range(2):
                            pe.wait_ge(pT_dve if hf else pT_act, n + 1)
                            for t in range(4):
                                for part_ in (p_hi, p_lo):
                                    mm = nc.tensor.matmul(ps[:, 4 + hf, t * P:(t + 1) * P], part_[s % 2][:, (4 * hf + t) * P:(4 * hf + t + 1) * P],
                                                          small_ident[:], start=part_ is p_hi, stop=part_ is p_lo)
                            mm.then_inc(p_turned, 1)
                        if s % 4 == 3:
                            g = s // 4
                            pe.wait_ge(item_read, ITEMS * (b + 1))
                            pe.wait_ge(pT_act, n + 2)
                            pe.wait_ge(pT_dve, n + 2)
                            pe.wait_ge(outT_ready, 4 * i + 2 * a + g + 1)
                            for st in range(ST):
                                for j in range(4):
                                    pair = 4 * g + j
                                    mm = nc.tensor.matmul(ps[32 * j:32 * j + 32, 6, g * P:(g + 1) * P],
                                                          v[a][:, st, pair * 2 * HD:(pair + 1) * 2 * HD], pT[g][:, j, st, :],
                                                          start=st == 0, stop=st == ST - 1)
                            mm.then_inc(value_mm, 1)
                        if items:
                            item(b + 1, (a + 1) % 2, 2 * s + 1)

            with pe.Fori(0, TT - 1) as i:
                turn(i, False)
            turn(TT - 1, True)
            pe.wait_ge(outT_ready, 2 * B + 1)
            for t in range(TT):
                for g in range(KT):
                    mm = nc.tensor.matmul(ps[:, t // 2, (t % 2) * D:(t % 2 + 1) * D], outT[:, g, t * P:(t + 1) * P], wo[:, g, :],
                                          start=g == 0, stop=g == KT - 1)
                mm.then_inc(proj_mm, 1)


def filter_buffers(sb):
    return dict(turns=sb("sp_turns", [P, KT]), whole=sb("sp_whole", [P, KT], dt=I32), angle=sb("sp_angle", [P, KT]),
                quarter=sb("sp_quarter", [P, KT]), gamma=sb("sp_gamma", [P, KT]), c_re=sb("sp_c_re", [P, KT]),
                c_im=sb("sp_c_im", [P, KT]), tmp=sb("sp_tmp", [P, 2, KT]),
                re=sb("sp_re", [P, B + 1, KT]),
                im=sb("sp_im", [P, B + 1, KT]),
                past=sb("sp_past", [P, KT, B]))


def filter_angle(nc, step, f, cols, angle_ready):
    two_pi = 2 * np.pi
    pi_hi = float(np.float32(two_pi))
    pi_lo = float(two_pi - np.float64(np.float32(two_pi)))
    pi_max = float(np.nextafter(np.float32(np.pi), np.float32(0)))
    at = COL_AT["L1_attn_theta"]
    theta = cols[:, at:at + KT]
    turns, angle, quarter = f["turns"], f["angle"], f["quarter"]
    step.link(nc.vector.tensor_scalar(f["whole"][:], theta, 1.0 / two_pi, None, ALU.mult))
    step.link(nc.vector.tensor_copy(turns[:], f["whole"][:]))
    step.link(nc.vector.scalar_tensor_tensor(out=angle[:], in0=turns[:], scalar=-pi_hi, in1=theta, op0=ALU.mult, op1=ALU.add))
    step.link(nc.vector.scalar_tensor_tensor(out=angle[:], in0=turns[:], scalar=-pi_lo, in1=angle[:], op0=ALU.mult, op1=ALU.add))
    step.link(nc.vector.tensor_scalar(angle[:], angle[:], pi_max, -pi_max, ALU.min, ALU.max))
    step.link(nc.vector.scalar_tensor_tensor(out=quarter[:], in0=angle[:], scalar=-1.0, in1=angle[:], op0=ALU.mult, op1=ALU.max))
    nc.vector.tensor_scalar(quarter[:], quarter[:], -1.0, float(np.pi / 2), ALU.mult, ALU.add).then_inc(angle_ready, 1)


def filter_parts(nc, act, step, f, cols, angle_ready):
    at = COL_AT["L1_attn_lmlg"]
    step.link(nc.scalar.activation(f["gamma"][:], cols[:, at:at + KT], ACT.Exp))
    step.link(nc.scalar.activation(f["gamma"][:], f["gamma"][:], ACT.Exp, scale=-1.0))
    act.wait_ge(angle_ready, 1)
    step.link(nc.scalar.activation(f["c_im"][:], f["angle"][:], ACT.Sin))
    nc.scalar.activation(f["c_re"][:], f["quarter"][:], ACT.Sin)


def filter_powers(nc, step, f, cols):
    re, im, tmp, c_re, c_im = f["re"], f["im"], f["tmp"], f["c_re"], f["c_im"]
    step.link(nc.gpsimd.memset(re[:, 0, :], 1.0))
    step.link(nc.gpsimd.memset(im[:, 0, :], 0.0))

    def product(out, a, b, op=ALU.mult):
        step.link(nc.gpsimd.tensor_tensor(out=out, in0=a, in1=b, op=op))

    product(c_re[:], c_re[:], f["gamma"][:])
    product(c_im[:], c_im[:], f["gamma"][:])
    for n in range(1, B + 1):
        product(tmp[:, 0], re[:, n - 1], c_re[:])
        product(tmp[:, 1], im[:, n - 1], c_im[:])
        product(re[:, n], tmp[:, 0], tmp[:, 1], ALU.subtract)
        if n < B:
            product(tmp[:, 0], re[:, n - 1], c_im[:])
            product(tmp[:, 1], im[:, n - 1], c_re[:])
            product(im[:, n], tmp[:, 0], tmp[:, 1], ALU.add)
    at = COL_AT["L1_attn_last_conv_init"]
    product(f["past"][:], re[:, 1:B + 1].rearrange("p n k -> p k n"), cols[:, at:at + KT].unsqueeze(2).to_broadcast([P, KT, B]))


def spiral_1(own, nc, A, sb, sem, x, cols, rows, ident, head_mask, band, ps, col, row, finished, ahead, spiral):
    HT = H1 // P
    h0 = sb("sp_h0", [P, TT, D], own)
    h = sb("sp_h", [P, TT, D], own)
    hT = sb("sp_hT", [P, KT, B, N], own)
    y = sb("sp_y", [P, KT, B, N], own)
    w1 = sb("sp_w1", [P, KT, H1], own)
    w2 = sb("sp_w2", [P, HT, D], own)
    act_T = sb("sp_act", [P, HT, T], own)
    re, past = spiral["re"], spiral["past"]
    stats = sb("sp_stats", [P, TT, 6], own)
    mv = sb("sp_mv", [P, TT, 2], own)
    var = sb("sp_var", [P, TT], own)
    rstd = sb("sp_rstd", [P, TT], own)
    half = sb("sp_half", [P, TT], own)

    ahead_loaded = sem("sp_ahead"); w_loaded = sem("sp_w_loaded"); pool_step = sem("sp_pool_step"); dve_step = sem("sp_dve_step")
    var_ready = sem("sp_var"); rstd_ready = sem("sp_rstd")
    h_ready = sem("sp_h_ready"); h_turned = sem("sp_h_turned"); hT_ready = sem("sp_hT_ready")
    y_ready = sem("sp_y_ready"); y_turned = sem("sp_y_turned")
    up_mm = sem("sp_up_mm"); silu_done = sem("sp_silu"); down_mm = sem("sp_down_mm")

    with nc.Block() as block:
        @block.sync
        def _(sp):
            sp.dma_start(w1[:], A["L1_attn_w1"].rearrange("(k p) n -> p k n", p=P)).then_inc(w_loaded, 16)
            sp.dma_start(w2[:], A["L1_attn_w2"].rearrange("(k p) n -> p k n", p=P)).then_inc(w_loaded, 16)
            load_ahead(sp, ahead, ahead_loaded)

        @block.gpsimd
        def _(pool):
            for s in finished:
                pool.sem_clear(s)
            step = Chain(pool, pool_step)
            step.link(nc.gpsimd.memset(half[:], -0.5))
            for n in range(2):
                pool.wait_ge(var_ready, n + 1)
                nc.gpsimd.tensor_tensor(out=rstd[:], in0=var[:], in1=half[:], op=ALU.pow).then_inc(rstd_ready, 1)
            pool.wait_ge(var_ready, 3)
            nc.gpsimd.tensor_tensor(out=rstd[:], in0=var[:], in1=half[:], op=ALU.pow).then_inc(rstd_ready, 1)

        @block.scalar
        def _(act):
            def affine(n):
                for k in range(KT):
                    act.wait_ge(h_turned, KT * n + k + 1)
                    nc.scalar.activation(hT[:, k].rearrange("p b n -> p (b n)"), ps[:, k, :], ACT.Identity,
                                         bias=col("L1_attn_ln_b", k), scale=col("L1_attn_ln_w", k)).then_inc(hT_ready, 1)

            affine(0)
            affine(1)
            for f in range(HT):
                act.wait_ge(up_mm, f + 1)
                nc.scalar.activation(act_T[:, f, :], ps[:, 2 + f % 2, :], ACT.Silu, bias=col("L1_attn_b1", f)).then_inc(silu_done, 1)

        @block.vector
        def _(dve):
            step = Chain(dve, dve_step)
            norm_stats(nc, step, x, stats, mv, var, TT, var_ready)
            dve.wait_ge(rstd_ready, 1)
            step.link(norm_apply(nc, h0, x, mv, rstd, TT))
            norm_stats(nc, step, h0, stats, mv, var, TT, var_ready)
            dve.wait_ge(rstd_ready, 2)
            norm_apply(nc, h, h0, mv, rstd, TT).then_inc(h_ready, 1)

            for k in range(KT):
                dve.wait_ge(hT_ready, k + 1)
                last = nc.vector.tensor_tensor(out=y[:, k], in0=hT[:, k], in1=past[:, k].unsqueeze(2).to_broadcast([P, B, N]), op=ALU.add)
            step.link(last)
            for n in range(1, B):
                for k in range(KT):
                    last = nc.vector.scalar_tensor_tensor(out=y[:, k, n:], in0=hT[:, k, 0:B - n], scalar=re[:, n, k:k + 1], in1=y[:, k, n:],
                                                          op0=ALU.mult, op1=ALU.add)
                step.link(last)
            for k in range(KT):
                nc.vector.tensor_tensor(out=y[:, k], in0=y[:, k], in1=hT[:, k], op=ALU.mult).then_inc(y_ready, 1)
            for t in range(TT):
                dve.wait_ge(y_turned, 2 * (t // 2 + 1))
                last = nc.vector.tensor_tensor(out=h0[:, t, :], in0=ps[:, 2 + t // 2, (t % 2) * D:(t % 2 + 1) * D], in1=h0[:, t, :], op=ALU.add)
            step.link(last)
            norm_stats(nc, step, h0, stats, mv, var, TT, var_ready)
            dve.wait_ge(rstd_ready, 3)
            norm_apply(nc, h, h0, mv, rstd, TT).then_inc(h_ready, 1)
            dve.wait_ge(h_ready, 2)
            step.link(nc.vector.tensor_tensor(out=h0[:], in0=h0[:], in1=row("L1_attn_b2").unsqueeze(1).to_broadcast([P, TT, D]), op=ALU.add))
            step.link(nc.vector.tensor_tensor(out=x[:], in0=x[:], in1=h0[:], op=ALU.add))
            for t in range(TT):
                dve.wait_ge(down_mm, t + 1)
                nc.vector.tensor_tensor(out=x[:, t, :], in0=ps[:, 4 + t, 0:D], in1=x[:, t, :], op=ALU.add)

        @block.tensor
        def _(pe):
            def turn_h(n):
                pe.wait_ge(h_ready, n + 1)
                for k in range(KT):
                    for t in range(TT):
                        last = nc.tensor.transpose(ps[:, k, t * P:(t + 1) * P], h[:, t, k * P:(k + 1) * P], ident[:])
                    last.then_inc(h_turned, 1)

            turn_h(0)
            for k in range(KT):
                pe.wait_ge(y_ready, k + 1)
                for t in range(TT):
                    mm = nc.tensor.transpose(ps[:, 2 + t // 2, (t % 2) * D + k * P:(t % 2) * D + (k + 1) * P],
                                             y[:, k, 2 * t:2 * t + 2, :].rearrange("p b n -> p (b n)"), ident[:])
                    if k == KT - 1:
                        mm.then_inc(y_turned, 1)
            turn_h(1)
            pe.wait_ge(hT_ready, 2 * KT)
            pe.wait_ge(w_loaded, 32)
            for f in range(HT):
                if f >= 2:
                    pe.wait_ge(silu_done, f - 1)
                for k in range(KT):
                    last = nc.tensor.matmul(ps[:, 2 + f % 2, :], w1[:, k, f * P:(f + 1) * P], hT[:, k].rearrange("p b n -> p (b n)"),
                                            start=k == 0, stop=k == KT - 1)
                last.then_inc(up_mm, 1)
            for t in range(TT):
                for f in range(HT):
                    if t == 0:
                        pe.wait_ge(silu_done, f + 1)
                    last = nc.tensor.matmul(ps[:, 4 + t, 0:D], act_T[:, f, t * P:(t + 1) * P], w2[:, f, :],
                                            start=f == 0, stop=f == HT - 1)
                last.then_inc(down_mm, 1)


def experts_1_ahead(sb, stack, A):
    wgate = sb("e1_wgate", [P, KT, E], stack)
    wshared = sb("e1_wshared", [P, KT, D], stack)
    b2 = sb("e1_b2", [E, D], stack)
    w1 = sb("e1_w1", [P, KT, H1], stack)
    w2 = sb("e1_w2", [P, H1 // P, D], stack)
    loads = [(w[:], src.rearrange("(k p) n -> p k n", p=P))
             for w, src in ((wgate, A["L1_ffn_gate_W"]), (wshared, A["L1_ffn_shared_W"]), (w1, A["L1_ffn_W1"][0]), (w2, A["L1_ffn_W2"][0]))]
    return {"wgate": wgate, "wshared": wshared, "b2": b2, "w1": w1, "w2": w2, "loads": loads + [(b2[:], A["L1_ffn_b2"])]}


def experts_1(own, nc, A, sb, sem, x, cols, rows, ident, head_mask, band, ps, col, row, finished, ahead, spiral):
    HT = H1 // P
    h = sb("e1_h", [P, TT, D], own)
    hT = sb("e1_hT", [P, KT, T], own)
    hT_hi = sb("e1_hT_hi", [P, KT, T], own, F32R)
    hT_lo = sb("e1_hT_lo", [P, KT, T], own, F32R)
    wgate, wshared, b2 = ahead["wgate"], ahead["wshared"], ahead["b2"]
    w1, w2 = ahead["w1"], ahead["w2"]
    w1_hi = [sb(f"e1_w1_hi{i}", [P, KT, H1], own, F32R) for i in range(2)]
    w2_hi = [sb(f"e1_w2_hi{i}", [P, HT, D], own, F32R) for i in range(2)]
    w1_lo = [sb(f"e1_w1_lo{i}", [P, KT, H1], own, F32R) for i in range(2)]
    w2_lo = [sb(f"e1_w2_lo{i}", [P, HT, D], own, F32R) for i in range(2)]
    gates = sb("e1_gates", [P, TT, E], own)
    chosen = sb("e1_chosen", [P, TT, E], own)
    chosenT = sb("e1_chosenT", [E, T], own)
    rank = sb("e1_rank", [P, E], own)
    work = sb("e1_work", [P, 3, TT, E], own)
    best = sb("e1_best", [P, 3, TT], own)
    gelu = [sb(f"e1_gelu{i}", [P, T], own) for i in range(2)]
    act_hi = [sb(f"e1_act_hi{i}", [P, HT, T], own, F32R) for i in range(2)]
    act_lo = [sb(f"e1_act_lo{i}", [P, HT, T], own, F32R) for i in range(2)]
    acc = sb("e1_acc", [P, TT, D], own)
    stats = sb("e1_stats", [P, TT, 6], own)
    mv = sb("e1_mv", [P, TT, 2], own)
    var = sb("e1_var", [P, TT], own)
    rstd = sb("e1_rstd", [P, TT], own)
    half = sb("e1_half", [P, TT], own)
    top = sb("e1_top", [P, TT], own)
    total = sb("e1_total", [P, TT], own)

    act_passed = sem("e1_act_passed")
    w1_loaded = sem("e1_w1_loaded")
    w2_loaded = sem("e1_w2_loaded")
    pool_step = sem("e1_pool_step"); dve_step = sem("e1_dve_step"); var_ready = sem("e1_var")
    rstd_ready = sem("e1_rstd"); h_ready = sem("e1_h_ready"); h_turned = sem("e1_h_turned"); hT_ready = sem("e1_hT_ready")
    gate_mm = sem("e1_gate_mm"); gate_arg = sem("e1_gate_arg"); gate_exp = sem("e1_gate_exp")
    chosen_ready = sem("e1_chosen_ready"); chosen_turned = sem("e1_chosen_turned"); chosenT_ready = sem("e1_chosenT_ready")
    shared_mm = sem("e1_shared_mm"); shared_arg = sem("e1_shared_arg"); shared_gelu = sem("e1_shared_gelu")
    bias_mm = sem("e1_bias_mm"); hT_split = sem("e1_hT_split")
    w_rounded = sem("e1_w_rounded"); w1_split = sem("e1_w1_split"); w2_split = sem("e1_w2_split")
    act_rounded = sem("e1_act_rounded"); act_split = sem("e1_act_split")
    up_mm = sem("e1_up_mm"); gelu_done = sem("e1_gelu"); down_mm = sem("e1_down_mm"); acc_added = sem("e1_acc_added")

    RING = 2
    PARTS = 4

    def weight_part(w, j):
        return w.rearrange("p k n -> p (k n)")[:, j * 512:(j + 1) * 512]

    with nc.Block() as block:
        @block.sync
        def _(sp):
            sp.sem_inc(w1_loaded, 16)
            sp.sem_inc(w2_loaded, 16)
            w1_d = A["L1_ffn_W1"].rearrange("e (k p) n -> (e k) p n", p=P)
            w2_d = A["L1_ffn_W2"].rearrange("e (k p) n -> (e k) p n", p=P)

            with sp.Fori(1, E) as e:
                sp.wait_ge(w1_split, e * PARTS)
                sp.dma_start(w1[:], w1_d[bass.ds(e * KT, KT)].rearrange("k p n -> p k n")).then_inc(w1_loaded, 16)
                sp.wait_ge(w2_split, e * PARTS)
                sp.dma_start(w2[:], w2_d[bass.ds(e * HT, HT)].rearrange("k p n -> p k n")).then_inc(w2_loaded, 16)

        @block.gpsimd
        def _(pool):
            for s in finished:
                pool.sem_clear(s)
            step = Chain(pool, pool_step)
            step.link(nc.gpsimd.memset(half[:], -0.5))
            pool.wait_ge(var_ready, 1)
            nc.gpsimd.tensor_tensor(out=rstd[:], in0=var[:], in1=half[:], op=ALU.pow).then_inc(rstd_ready, 1)

            def weight_rests(e, a):
                for m, (lo, hi, w, split) in enumerate(((w1_lo, w1_hi, w1, w1_split), (w2_lo, w2_hi, w2, w2_split))):
                    for j in range(PARTS):
                        pool.wait_ge(w_rounded, (2 * e + m) * PARTS + j + 1)
                        nc.gpsimd.tensor_tensor(out=weight_part(lo[a][:], j), in0=weight_part(w[:], j),
                                                in1=weight_part(hi[a][:].bitcast(F32), j), op=ALU.subtract).then_inc(split, 1)

            weight_rests(0, 0)
            with pool.Fori(0, E // 2 - 1) as i:
                for a in range(2):
                    weight_rests(2 * i + a + 1, 1 - a)
            weight_rests(E - 1, 1)
            pool.wait_ge(var_ready, 2)
            nc.gpsimd.tensor_tensor(out=rstd[:], in0=var[:], in1=half[:], op=ALU.pow).then_inc(rstd_ready, 1)

        @block.scalar
        def _(act):
            act.sem_inc(gelu_done, RING)
            for k in range(KT):
                act.wait_ge(h_turned, k + 1)
                nc.scalar.copy(hT[:, k, :], ps[:, 6 + k, :]).then_inc(hT_ready, 1)
            for w_hi, w, loaded in ((w1_hi, w1, w1_loaded), (w2_hi, w2, w2_loaded)):
                act.wait_ge(loaded, 16)
                for j in range(PARTS):
                    nc.scalar.copy(weight_part(w_hi[0][:], j), weight_part(w[:], j)).then_inc(w_rounded, 1)
            act.wait_ge(gate_arg, 1)
            nc.scalar.activation(gates[:], gates[:], ACT.Exp).then_inc(gate_exp, 1)
            act.wait_ge(chosen_turned, 1)
            nc.scalar.copy(chosenT[:], ps[0:E, 7, :]).then_inc(chosenT_ready, 1)
            act.wait_ge(shared_arg, 1)
            nc.scalar.activation(acc[:], acc[:], ACT.Gelu).then_inc(shared_gelu, 1)

            def turn(i, last):
                for a in range(2):
                    e = 2 * i + a
                    more = not (last and a == 1)
                    for f in range(HT):
                        n = e * HT + f
                        act.wait_ge(up_mm, n + 1)
                        wait_alone(act, act_passed, act_split, n + 1)
                        nc.scalar.activation(gelu[f % 2][:], ps[:, f % 2, :], ACT.Gelu,
                                             bias=cols[:, bass.ds(n + COL_AT["L1_ffn_b1"], 1)]).then_inc(gelu_done, 1)
                        if more and f < PARTS:
                            if f == 0:
                                act.wait_ge(w1_loaded, 16 * (e + 2))
                            nc.scalar.copy(weight_part(w1_hi[1 - a][:], f), weight_part(w1[:], f)).then_inc(w_rounded, 1)
                    if more:
                        act.wait_ge(w2_loaded, 16 * (e + 2))
                        act.wait_ge(down_mm, (e + 2) * TT)
                        for j in range(PARTS):
                            nc.scalar.copy(weight_part(w2_hi[1 - a][:], j), weight_part(w2[:], j)).then_inc(w_rounded, 1)

            with act.Fori(0, E // 2 - 1) as i:
                turn(i, False)
            turn(E // 2 - 1, True)

        @block.vector
        def _(dve):
            dve.sem_inc(acc_added, RING)
            dve.sem_inc(act_split, RING)
            step = Chain(dve, dve_step)
            for e in range(E):
                last = nc.vector.memset(rank[:, e:e + 1], float(E - e))
            step.link(last)
            norm_stats(nc, step, x, stats, mv, var, TT, var_ready)
            dve.wait_ge(rstd_ready, 1)
            norm_apply(nc, h, x, mv, rstd, TT).then_inc(h_ready, 1)
            for k in range(KT):
                dve.wait_ge(hT_ready, k + 1)
                step.link(nc.vector.tensor_copy(hT_hi[:, k, :], hT[:, k, :]))
                nc.vector.tensor_tensor(out=hT_lo[:, k, :], in0=hT[:, k, :], in1=hT_hi[:, k, :].bitcast(F32), op=ALU.subtract).then_inc(hT_split, 1)

            def split_activations(e, a, fs):
                dve.wait_ge(down_mm, (e + 1) * TT)
                for f in fs:
                    n = e * HT + f
                    dve.wait_ge(gelu_done, n + 1 + RING)
                    nc.vector.tensor_copy(act_hi[a][:, f, :], gelu[f % 2][:]).then_inc(act_rounded, 1)
                    dve.wait_ge(act_rounded, n + 1)
                    nc.vector.tensor_tensor(out=act_lo[a][:, f, :], in0=gelu[f % 2][:], in1=act_hi[a][:, f, :].bitcast(F32),
                                            op=ALU.subtract).then_inc(act_split, 1)

            dve.wait_ge(gate_mm, 1)
            step.link(nc.vector.tensor_copy(gates[:], ps[:, 6, 0:TT * E].rearrange("p (t e) -> p t e", t=TT)))
            softmax_rows(nc, step, gates[:], E, top[:]).then_inc(gate_arg, 1)
            dve.wait_ge(shared_mm, 1)
            nc.vector.tensor_tensor(out=acc[:].rearrange("p (a b) d -> p a b d", a=2), in0=ps[:, 2:4, :].rearrange("p a (b d) -> p a b d", b=2),
                                    in1=row("L1_ffn_shared_b").unsqueeze(1).unsqueeze(1).to_broadcast([P, 2, 2, D]), op=ALU.add).then_inc(shared_arg, 1)
            dve.wait_ge(gate_exp, 1)
            step.link(normalise_rows(nc, step, gates[:], total[:]))
            top_two(nc, step, gates[:], rank[:], chosen[:], work, best).then_inc(chosen_ready, 1)
            dve.wait_ge(shared_gelu, 1)
            dve.wait_ge(bias_mm, 1)
            for t in range(TT):
                last = nc.vector.scalar_tensor_tensor(out=acc[:, t, :], in0=acc[:, t, :], scalar=0.5,
                                                      in1=ps[:, 6 + t // 2, (t % 2) * D:(t % 2 + 1) * D], op0=ALU.mult, op1=ALU.add)
            step.link(last)

            step.link(nc.vector.tensor_tensor(out=x[:], in0=x[:], in1=row("L1_ffn_beta").unsqueeze(1).to_broadcast([P, TT, D]), op=ALU.add))

            def add_experts(e, tiles):
                for t in tiles:
                    n = e * TT + t
                    dve.wait_ge(down_mm, n + 1 + 2 * TT)
                    nc.vector.scalar_tensor_tensor(out=acc[:, t, :], in0=ps[:, 4 + t % 2, 0:D],
                                                   scalar=chosen[:].rearrange("p t e -> p (t e)")[:, bass.ds(t * E + e, 1)],
                                                   in1=acc[:, t, :], op0=ALU.mult, op1=ALU.add).then_inc(acc_added, 1)

            with dve.Fori(0, E // 2) as i:
                for a in range(2):
                    e = 2 * i + a
                    split_activations(e, a, range(HT))
                    add_experts(e, range(TT))
            dve.wait_ge(acc_added, E * TT + RING)
            add_norm(nc, dve, step, x, acc, row("L1_ffn_gamma"), stats, mv, rstd, var, var_ready, rstd_ready)

        @block.tensor
        def _(pe):
            pe.sem_inc(down_mm, 2 * TT)
            pe.wait_ge(h_ready, 1)
            for k in range(KT):
                for t in range(TT):
                    last = nc.tensor.transpose(ps[:, 6 + k, t * P:(t + 1) * P], h[:, t, k * P:(k + 1) * P], ident[:])
                last.then_inc(h_turned, 1)
            pe.wait_ge(hT_ready, KT)
            for t in range(TT):
                for k in range(KT):
                    last = nc.tensor.matmul(ps[:, 6, t * E:(t + 1) * E], hT[:, k, t * P:(t + 1) * P], wgate[:, k, :],
                                            start=k == 0, stop=k == KT - 1)
            last.then_inc(gate_mm, 1)
            for t in range(TT):
                for k in range(KT):
                    last = nc.tensor.matmul(ps[:, 2 + t // 2, (t % 2) * D:(t % 2 + 1) * D], hT[:, k, t * P:(t + 1) * P], wshared[:, k, :],
                                            start=k == 0, stop=k == KT - 1)
            last.then_inc(shared_mm, 1)

            def up(i, a, fs):
                for f in fs:
                    if f == 0:
                        pe.wait_ge(w1_split, (2 * i + a + 1) * PARTS)
                    pe.wait_ge(gelu_done, (2 * i + a) * HT + f + 1)
                    for k in range(KT):
                        at = (slice(None), k, slice(f * P, (f + 1) * P))
                        last = split_matmul(nc, ps[:, f % 2, :], (w1_hi[a][at], w1_lo[a][at]), (hT_hi[:, k, :], hT_lo[:, k, :]),
                                            k == 0, k == KT - 1)
                    last.then_inc(up_mm, 1)

            def down(i, a):
                e = 2 * i + a
                pe.wait_ge(w2_split, (e + 1) * PARTS)
                for t in range(TT):
                    pe.wait_ge(acc_added, e * TT + t + 1)
                    for f in range(HT):
                        if t == 0:
                            pe.wait_ge(act_split, e * HT + f + 1 + RING)
                        at = (slice(None), f, slice(t * P, (t + 1) * P))
                        last = split_matmul(nc, ps[:, 4 + t % 2, 0:D], (act_hi[a][at], act_lo[a][at]),
                                            (w2_hi[a][:, f, :], w2_lo[a][:, f, :]), f == 0, f == HT - 1)
                    last.then_inc(down_mm, 1)

            def gates_turned():
                pe.wait_ge(chosen_ready, 1)
                for t in range(TT):
                    last = nc.tensor.matmul(ps[0:E, 7, t * P:(t + 1) * P], chosen[:, t, :], ident[:], start=True, stop=True)
                last.then_inc(chosen_turned, 1)
                pe.wait_ge(chosenT_ready, 1)
                for t in range(TT):
                    last = nc.tensor.matmul(ps[:, 6 + t // 2, (t % 2) * D:(t % 2 + 1) * D], chosenT[:, t * P:(t + 1) * P], b2[:],
                                            start=True, stop=True)
                last.then_inc(bias_mm, 1)

            pe.wait_ge(hT_split, KT)
            up(0, 0, range(2))
            gates_turned()
            up(0, 0, range(2, HT))
            down(0, 0)
            up(0, 1, range(HT))
            down(0, 1)
            with pe.Fori(1, E // 2) as i:
                for a in range(2):
                    up(i, a, range(HT))
                    down(i, a)


def kernel(**inputs):
    import numpy as _np
    import concourse.bacc as _bacc
    from concourse import mybir as _mybir
    from concourse.bass_utils import run_bass_kernel_spmd as _run

    a = {n: _np.asarray(v) for n, v in inputs.items()}

    def pair_columns(w):
        return w.reshape(D, NPAIR, 2, 2, DH // 4 * 2).transpose(0, 1, 3, 2, 4).reshape(D, H * DH)

    laid = {"x": a["x"], "ctx_1024": a["ctx_1024"],
            "cosT": _np.tile(a["L0_xattn_cos"].T, (4, 1)), "sinT": _np.tile(a["L0_xattn_sin"].T, (4, 1)),
            "wq_pairs": pair_columns(a["L0_xattn_Wq"]), "wk_pairs": pair_columns(a["L0_xattn_Wkv"][:, :H * DH]),
            "wv": a["L0_xattn_Wkv"][:, H * DH:],
            "cols": _np.concatenate([a[n].reshape(-1, P) for n in COLS]).T,
            "rows": _np.concatenate([a[n] for n in ROWS]).reshape(1, NROW),
            "L0_ffn_b1": a["L0_ffn_b1"].reshape(1, E * H0)}
    for name in ("L1_xattn_Wq", "L1_xattn_Wk", "L1_xattn_Wv", "L1_xattn_Wo"):
        laid[name + "T"] = a[name].T
    for name in ("L0_xattn_Wo", "L0_attn_Wqk", "L0_attn_Wgate", "L0_attn_Wproj", "L0_ffn_gate_w", "L0_ffn_w1",
                 "L0_ffn_w2", "L0_ffn_b2", "L1_attn_w1", "L1_attn_w2", "L1_ffn_W1", "L1_ffn_W2", "L1_ffn_b2",
                 "L1_ffn_gate_W", "L1_ffn_shared_W"):
        laid[name] = a[name]

    nc = _bacc.Bacc("TRN2", target_bir_lowering=False, num_devices=1)
    arrays, args = {}, {}
    for name, v in laid.items():
        v = _np.ascontiguousarray(v)
        arrays[f"in_{name}"] = v
        args[name] = nc.dram_tensor(f"in_{name}", v.shape, _mybir.dt.from_np(v.dtype), kind="ExternalInput").ap()
    args["out"] = nc.dram_tensor("out_x", (B, N, D), _mybir.dt.from_np(_np.dtype("float32")), kind="ExternalOutput").ap()
    program(nc, args)
    r = _run(nc, [arrays], core_ids=[0])
    return r.results[0]["out_x"]
```
